# Optimizing a Trainium2 kernel written in Bass

```python
import numpy as np
import jax
import jax.numpy as jnp

def _softmax(x, axis=-1):
    return jax.nn.softmax(x, axis=axis)

def _gelu(x):
    return jax.nn.gelu(x, approximate=True)

def _silu(x):
    return jax.nn.silu(x)

def _sigmoid(x):
    return jax.nn.sigmoid(x)

def _layernorm(x, axis=-1, eps=1e-05):
    m = jnp.mean(x, axis=axis, keepdims=True)
    v = jnp.var(x, axis=axis, keepdims=True)
    return (x - m) / jnp.sqrt(v + eps)

def _scatter_add(tgt, idx, src, axis=0):
    return tgt.at[idx].add(src)

def _segment_sum(src, seg, n):
    return jax.ops.segment_sum(src, seg, n)
kernel_name = 'mk_xattn_ffn_d4_seqx_r4_d4779f'

def setup_inputs(seed: int=0):
    np.random.seed(seed)
    _w = jnp.asarray

    def _rec_inputs():
        import jax
        import jax.numpy as jnp
        _rk = jax.random.key(seed)
        x = 7.22e-05 + 1 * jax.random.normal(jax.random.fold_in(_rk, 1), (32, 256, 256), jnp.float32)
        _lenS = 256 - jax.random.randint(jax.random.fold_in(_rk, 7), (32,), 0, max(1, 256 // 4) + 1, jnp.int32)
        _lenS2 = 120 - jax.random.randint(jax.random.fold_in(_rk, 8), (32,), 0, max(1, 120 // 4) + 1, jnp.int32)
        _ctx_768P = jax.random.normal(jax.random.fold_in(_rk, 11), (32, 16, 192), jnp.float32)
        _ctx_768c = jax.random.dirichlet(jax.random.fold_in(_rk, 511), 0.3 * jnp.ones((16,), jnp.float32), (32, 120))
        _ctx_768t = jnp.einsum('bsk,bkd->bsd', _ctx_768c, _ctx_768P)
        _ctx_768t = _ctx_768t * jax.lax.rsqrt(jnp.mean(jnp.square(_ctx_768t)) + 1e-12) * 0.953939
        ctx_768 = -0.000191848 + 0.999787 * (_ctx_768t + 0.3 * jax.random.normal(jax.random.fold_in(_rk, 611), (32, 120, 192), jnp.float32))
        _validS = jnp.arange(256)[None, :] < _lenS[:, None]
        _validS2 = jnp.arange(120)[None, :] < _lenS2[:, None]
        _causal = jnp.tril(jnp.ones((256, 256), dtype=bool))
        mask_BxS_bf1 = jnp.ones((32, 256), dtype=bool)
        mask_BxS2_bf1 = jnp.ones((32, 120), dtype=bool)
        return (x, ctx_768, mask_BxS_bf1, mask_BxS2_bf1)
    x, ctx_768, mask_BxS_bf1, mask_BxS2_bf1 = _rec_inputs()

    def _L0_xattn_setup():
        import jax, jax.numpy as jnp
        import numpy as np
        NUM_HEADS = 16
        CLAMP = 10000.0
        key = jax.random.key(seed)
        ks = jax.random.split(key, 8)
        B, Nq, Nkv, Cq, Ckv = (4, 512, 512, 256, 192)
        s_q = 1.0 / np.sqrt(Cq)
        s_kv = 1.0 / np.sqrt(Ckv)
        return {'query': jax.random.normal(ks[0], (B, Nq, Cq), jnp.float32), 'key_value': jax.random.normal(ks[1], (B, Nkv, Ckv), jnp.float32), 'Wq': jax.random.normal(ks[2], (Cq, Cq), jnp.float32) * s_q, 'bq': jnp.zeros((Cq,), jnp.float32), 'Wk': jax.random.normal(ks[3], (Ckv, Cq), jnp.float32) * s_kv, 'bk': jnp.zeros((Cq,), jnp.float32), 'Wv': jax.random.normal(ks[4], (Ckv, Cq), jnp.float32) * s_kv, 'bv': jnp.zeros((Cq,), jnp.float32), 'Wo': jax.random.normal(ks[5], (Cq, Cq), jnp.float32) * s_q, 'bo': jnp.zeros((Cq,), jnp.float32)}
    _L0_xattn_all = _L0_xattn_setup()
    _L0_xattn_in = {k: v for k, v in _L0_xattn_all.items() if k in ('Wq', 'bq', 'Wk', 'bk', 'Wv', 'bv', 'Wo', 'bo')}
    del _L0_xattn_all

    def _L0_ffn_setup():
        import jax, jax.numpy as jnp
        import numpy as np
        B, S, D_MODEL, D_HIDDEN = (4, 512, 256, 1024)

        def act_quant(x):
            scale = 127.0 / jnp.clip(jnp.max(jnp.abs(x), axis=-1, keepdims=True), 1e-05)
            return jnp.clip(jnp.round(x * scale), -128, 127) / scale

        def weight_quant(w):
            scale = 1.0 / jnp.clip(jnp.mean(jnp.abs(w)), 1e-05)
            return jnp.clip(jnp.round(w * scale), -1, 1) / scale

        def bit_linear(x, w):
            xq = x + jax.lax.stop_gradient(act_quant(x) - x)
            wq = w + jax.lax.stop_gradient(weight_quant(w) - w)
            return jnp.einsum('bsd,hd->bsh', xq, wq)

        def depthwise_conv1d(x_bcl, w, b):
            y = jax.lax.conv_general_dilated(x_bcl, w, window_strides=(1,), padding=[(1, 1)], dimension_numbers=('NCH', 'OIH', 'NCH'), feature_group_count=x_bcl.shape[1])
            return y + b[None, :, None]
        key = jax.random.key(seed)
        ks = jax.random.split(key, 5)
        lim1 = 1.0 / np.sqrt(D_MODEL)
        lim2 = 1.0 / np.sqrt(D_HIDDEN)
        limc = 1.0 / np.sqrt(3.0)
        return {'x': jax.random.normal(ks[0], (B, S, D_MODEL), dtype=jnp.float32), 'w1': jax.random.uniform(ks[1], (D_HIDDEN, D_MODEL), jnp.float32, -lim1, lim1), 'conv_w': jax.random.uniform(ks[2], (D_HIDDEN, 1, 3), jnp.float32, -limc, limc), 'conv_b': jax.random.uniform(ks[3], (D_HIDDEN,), jnp.float32, -limc, limc), 'w2': jax.random.uniform(ks[4], (D_MODEL, D_HIDDEN), jnp.float32, -lim2, lim2)}
    _L0_ffn_all = _L0_ffn_setup()
    _L0_ffn_in = {k: v for k, v in _L0_ffn_all.items() if k in ('w1', 'conv_w', 'conv_b', 'w2')}
    del _L0_ffn_all

    def _L1_xattn_setup():
        import jax, jax.numpy as jnp
        import numpy as np
        EPS = 1e-05
        key = jax.random.key(seed)
        ks = jax.random.split(key, 6)
        B, Nq, Nk, Dq, Dk = (16, 512, 512, 256, 192)
        s = lambda d: 1.0 / np.sqrt(d)
        return {'q': jax.random.normal(ks[0], (B, Nq, Dq), dtype=jnp.float32), 'k': jax.random.normal(ks[1], (B, Nk, Dk), dtype=jnp.float32), 'Wq': jax.random.normal(ks[2], (Dq, Dq), dtype=jnp.float32) * s(Dq), 'Wk': jax.random.normal(ks[3], (Dq, Dk), dtype=jnp.float32) * s(Dk), 'Wv': jax.random.normal(ks[4], (Dq, Dk), dtype=jnp.float32) * s(Dk), 'Wo': jax.random.normal(ks[5], (Dq, Dq), dtype=jnp.float32) * s(Dq)}
    _L1_xattn_all = _L1_xattn_setup()
    _L1_xattn_in = {k: v for k, v in _L1_xattn_all.items() if k in ('Wq', 'Wk', 'Wv', 'Wo')}
    del _L1_xattn_all

    def _L1_ffn_setup():
        import jax, jax.numpy as jnp
        import numpy as np
        B, T, C, E, K, CAP, H = (8, 512, 256, 8, 2, 1024, 1024)
        key = jax.random.key(seed)
        ks = jax.random.split(key, 6)
        s = 0.02
        return {'x': jax.random.normal(ks[0], (B, T, C), jnp.float32), 'rw1': s * jax.random.normal(ks[1], (C, H), jnp.float32), 'rb1': jnp.zeros((H,), jnp.float32), 'rw2': s * jax.random.normal(ks[2], (H, E), jnp.float32), 'rb2': jnp.zeros((E,), jnp.float32), 'ew1': s * jax.random.normal(ks[3], (E, C, H), jnp.float32), 'eb1': jnp.zeros((E, H), jnp.float32), 'ew2': s * jax.random.normal(ks[4], (E, H, C), jnp.float32), 'eb2': jnp.zeros((E, C), jnp.float32)}
    _L1_ffn_all = _L1_ffn_setup()
    _L1_ffn_in = {k: v for k, v in _L1_ffn_all.items() if k in ('rw1', 'rb1', 'rw2', 'rb2', 'ew1', 'eb1', 'ew2', 'eb2')}
    del _L1_ffn_all

    def _L2_xattn_setup():
        import jax, jax.numpy as jnp
        import numpy as np
        N_HEADS = 16
        D_EMBED = 256
        D_CROSS = 192
        D_HEAD = D_EMBED // N_HEADS
        key = jax.random.key(seed)
        ks = jax.random.split(key, 10)
        B, SQ, SKV = (8, 1024, 77)
        s_e = 1.0 / np.sqrt(D_EMBED)
        s_c = 1.0 / np.sqrt(D_CROSS)
        return {'x': jax.random.normal(ks[0], (B, SQ, D_EMBED), jnp.float32), 'y': jax.random.normal(ks[1], (B, SKV, D_CROSS), jnp.float32), 'wq': jax.random.normal(ks[2], (D_EMBED, D_EMBED), jnp.float32) * s_e, 'bq': jnp.zeros((D_EMBED,), jnp.float32), 'wk': jax.random.normal(ks[3], (D_CROSS, D_EMBED), jnp.float32) * s_c, 'bk': jnp.zeros((D_EMBED,), jnp.float32), 'wv': jax.random.normal(ks[4], (D_CROSS, D_EMBED), jnp.float32) * s_c, 'bv': jnp.zeros((D_EMBED,), jnp.float32), 'wo': jax.random.normal(ks[5], (D_EMBED, D_EMBED), jnp.float32) * s_e, 'bo': jnp.zeros((D_EMBED,), jnp.float32)}
    _L2_xattn_all = _L2_xattn_setup()
    _L2_xattn_in = {k: v for k, v in _L2_xattn_all.items() if k in ('wq', 'bq', 'wk', 'bk', 'wv', 'bv', 'wo', 'bo')}
    del _L2_xattn_all

    def _L2_ffn_setup():
        import jax, jax.numpy as jnp
        import numpy as np
        D_MODEL = 256
        E = 4
        MIN_E = 1
        TH_LO = 0.5
        TH_HI = 2.0
        key = jax.random.key(seed)
        ks = jax.random.split(key, 12)
        B, N, D, H = (4, 512, D_MODEL, 2 * D_MODEL)
        s = 0.02
        return {'x': jax.random.normal(ks[0], (B, N, D), dtype=jnp.float32), 'gate_w': jax.random.normal(ks[1], (D, E), dtype=jnp.float32) * s, 'gate_b': jnp.zeros((E,), dtype=jnp.float32), 'dp_w1': jax.random.normal(ks[2], (D, D // 2), dtype=jnp.float32) * s, 'dp_b1': jnp.zeros((D // 2,), dtype=jnp.float32), 'dp_w2': jax.random.normal(ks[3], (D // 2, 1), dtype=jnp.float32) * s, 'dp_b2': jnp.zeros((1,), dtype=jnp.float32), 'ew1': jax.random.normal(ks[4], (E, D, H), dtype=jnp.float32) * s, 'eb1': jnp.zeros((E, H), dtype=jnp.float32), 'ew2': jax.random.normal(ks[5], (E, H, D), dtype=jnp.float32) * s, 'eb2': jnp.zeros((E, D), dtype=jnp.float32)}
    _L2_ffn_all = _L2_ffn_setup()
    _L2_ffn_in = {k: v for k, v in _L2_ffn_all.items() if k in ('gate_w', 'gate_b', 'dp_w1', 'dp_b1', 'dp_w2', 'dp_b2', 'ew1', 'eb1', 'ew2', 'eb2')}
    del _L2_ffn_all

    def _L3_xattn_setup():
        import jax, jax.numpy as jnp
        import numpy as np
        B, T, DT, G, DV = (16, 128, 256, 144, 192)
        H, DH = (4, 32)
        INNER = H * DH
        HID = 4 * DT
        N_STATE = 64
        K_TOP = 32

        def layernorm(x, g, b, eps=1e-05):
            m = x.mean(-1, keepdims=True)
            v = x.var(-1, keepdims=True)
            return (x - m) * jax.lax.rsqrt(v + eps) * g + b

        def s4d(x, log_dt, A_re, A_im, C_re, C_im, D_skip):
            Bb, L, D = x.shape
            dt = jnp.exp(log_dt)
            A = A_re + 1j * A_im
            C = C_re + 1j * C_im
            dtA = dt[:, None] * A
            dC = C * (jnp.exp(dtA) - 1.0) / A
            powers = jnp.exp(dtA[:, :, None] * jnp.arange(L))
            K = 2.0 * jnp.einsum('dn,dnl->dl', dC, powers).real
            n = 2 * L
            Kf = jnp.fft.rfft(K, n=n, axis=-1)
            xf = jnp.fft.rfft(x, n=n, axis=1)
            y = jnp.fft.irfft(xf * Kf.T[None], n=n, axis=1)[:, :L]
            return y + x * D_skip
        key = jax.random.key(seed)
        ks = jax.random.split(key, 16)
        s = 0.02
        inp = {'x_text': jax.random.normal(ks[0], (B, T, DT), jnp.float32), 'x_vision': jax.random.normal(ks[1], (B, G, DV), jnp.float32), 'text_mask': jnp.ones((B, T), bool), 'vision_mask': jnp.ones((B, G), bool), 'Wq': jax.random.normal(ks[2], (DT, INNER), jnp.float32) * s, 'Wk': jax.random.normal(ks[3], (DV, INNER), jnp.float32) * s, 'Wv': jax.random.normal(ks[4], (DV, DT), jnp.float32) * s, 'W_film_in': jax.random.normal(ks[5], (DT, 2 * DT), jnp.float32) * s, 'b_film_in': jnp.zeros((2 * DT,), jnp.float32), 'W_film_out': jax.random.normal(ks[6], (DT, 2 * DT), jnp.float32) * s, 'b_film_out': jnp.zeros((2 * DT,), jnp.float32), 'g_norm_in': jnp.ones((DT,), jnp.float32), 'b_norm_in': jnp.zeros((DT,), jnp.float32), 'g_norm_out': jnp.ones((DT,), jnp.float32), 'b_norm_out': jnp.zeros((DT,), jnp.float32), 'g_ffn': jnp.ones((DT,), jnp.float32), 'b_ffn': jnp.zeros((DT,), jnp.float32), 'W1': jax.random.normal(ks[7], (DT, HID), jnp.float32) * s, 'b1': jnp.zeros((HID,), jnp.float32), 'W2': jax.random.normal(ks[8], (HID, DT), jnp.float32) * s, 'b2': jnp.zeros((DT,), jnp.float32), 'log_dt': jnp.log(0.001) + jax.random.uniform(ks[9], (DT,), jnp.float32) * (jnp.log(0.1) - jnp.log(0.001)), 'A_re': -0.5 * jnp.ones((DT, N_STATE), jnp.float32), 'A_im': jnp.tile(jnp.pi * jnp.arange(N_STATE, dtype=jnp.float32), (DT, 1)), 'C_re': jax.random.normal(ks[10], (DT, N_STATE), jnp.float32) * 0.5 ** 0.5, 'C_im': jax.random.normal(ks[11], (DT, N_STATE), jnp.float32) * 0.5 ** 0.5, 'D_skip': jax.random.normal(ks[12], (DT,), jnp.float32), 'mod_gate': jnp.array(0.5, jnp.float32)}
        return inp
    _L3_xattn_all = _L3_xattn_setup()
    _L3_xattn_in = {k: v for k, v in _L3_xattn_all.items() if k in ('Wq', 'Wk', 'Wv', 'W_film_in', 'b_film_in', 'W_film_out', 'b_film_out', 'g_norm_in', 'b_norm_in', 'g_norm_out', 'b_norm_out', 'g_ffn', 'b_ffn', 'W1', 'b1', 'W2', 'b2', 'log_dt', 'A_re', 'A_im', 'C_re', 'C_im', 'D_skip', 'mod_gate')}
    del _L3_xattn_all

    def _L3_ffn_setup():
        import jax, jax.numpy as jnp
        import numpy as np
        D_MODEL, D_FF, RANK = (256, 1024, 64)
        B, S = (4, 1024)
        key = jax.random.key(seed)
        ks = jax.random.split(key, 7)
        return {'x': jax.random.normal(ks[0], (B, S, D_MODEL), dtype=jnp.float32), 'U1': jax.random.normal(ks[1], (D_MODEL, RANK), dtype=jnp.float32) * 0.02, 'V1': jax.random.normal(ks[2], (RANK, D_FF), dtype=jnp.float32) * 0.02, 'b1': jnp.zeros((D_FF,), dtype=jnp.float32), 'U2': jax.random.normal(ks[3], (D_FF, RANK), dtype=jnp.float32) * 0.02, 'V2': jax.random.normal(ks[4], (RANK, D_MODEL), dtype=jnp.float32) * 0.02, 'b2': jnp.zeros((D_MODEL,), dtype=jnp.float32)}
    _L3_ffn_all = _L3_ffn_setup()
    _L3_ffn_in = {k: v for k, v in _L3_ffn_all.items() if k in ('U1', 'V1', 'b1', 'U2', 'V2', 'b2')}
    del _L3_ffn_all
    return {'x': x, 'ctx_768': ctx_768, 'mask_BxS_bf1': mask_BxS_bf1, 'mask_BxS2_bf1': mask_BxS2_bf1, 'L0_xattn_Wq': _L0_xattn_in['Wq'], 'L0_xattn_bq': _L0_xattn_in['bq'], 'L0_xattn_Wk': _L0_xattn_in['Wk'], 'L0_xattn_bk': _L0_xattn_in['bk'], 'L0_xattn_Wv': _L0_xattn_in['Wv'], 'L0_xattn_bv': _L0_xattn_in['bv'], 'L0_xattn_Wo': _L0_xattn_in['Wo'], 'L0_xattn_bo': _L0_xattn_in['bo'], 'L0_ffn_w1': _L0_ffn_in['w1'], 'L0_ffn_conv_w': _L0_ffn_in['conv_w'], 'L0_ffn_conv_b': _L0_ffn_in['conv_b'], 'L0_ffn_w2': _L0_ffn_in['w2'], 'L1_xattn_Wq': _L1_xattn_in['Wq'], 'L1_xattn_Wk': _L1_xattn_in['Wk'], 'L1_xattn_Wv': _L1_xattn_in['Wv'], 'L1_xattn_Wo': _L1_xattn_in['Wo'], 'L1_ffn_rw1': _L1_ffn_in['rw1'], 'L1_ffn_rb1': _L1_ffn_in['rb1'], 'L1_ffn_rw2': _L1_ffn_in['rw2'], 'L1_ffn_rb2': _L1_ffn_in['rb2'], 'L1_ffn_ew1': _L1_ffn_in['ew1'], 'L1_ffn_eb1': _L1_ffn_in['eb1'], 'L1_ffn_ew2': _L1_ffn_in['ew2'], 'L1_ffn_eb2': _L1_ffn_in['eb2'], 'L2_xattn_wq': _L2_xattn_in['wq'], 'L2_xattn_bq': _L2_xattn_in['bq'], 'L2_xattn_wk': _L2_xattn_in['wk'], 'L2_xattn_bk': _L2_xattn_in['bk'], 'L2_xattn_wv': _L2_xattn_in['wv'], 'L2_xattn_bv': _L2_xattn_in['bv'], 'L2_xattn_wo': _L2_xattn_in['wo'], 'L2_xattn_bo': _L2_xattn_in['bo'], 'L2_ffn_gate_w': _L2_ffn_in['gate_w'], 'L2_ffn_gate_b': _L2_ffn_in['gate_b'], 'L2_ffn_dp_w1': _L2_ffn_in['dp_w1'], 'L2_ffn_dp_b1': _L2_ffn_in['dp_b1'], 'L2_ffn_dp_w2': _L2_ffn_in['dp_w2'], 'L2_ffn_dp_b2': _L2_ffn_in['dp_b2'], 'L2_ffn_ew1': _L2_ffn_in['ew1'], 'L2_ffn_eb1': _L2_ffn_in['eb1'], 'L2_ffn_ew2': _L2_ffn_in['ew2'], 'L2_ffn_eb2': _L2_ffn_in['eb2'], 'L3_xattn_Wq': _L3_xattn_in['Wq'], 'L3_xattn_Wk': _L3_xattn_in['Wk'], 'L3_xattn_Wv': _L3_xattn_in['Wv'], 'L3_xattn_W_film_in': _L3_xattn_in['W_film_in'], 'L3_xattn_b_film_in': _L3_xattn_in['b_film_in'], 'L3_xattn_W_film_out': _L3_xattn_in['W_film_out'], 'L3_xattn_b_film_out': _L3_xattn_in['b_film_out'], 'L3_xattn_g_norm_in': _L3_xattn_in['g_norm_in'], 'L3_xattn_b_norm_in': _L3_xattn_in['b_norm_in'], 'L3_xattn_g_norm_out': _L3_xattn_in['g_norm_out'], 'L3_xattn_b_norm_out': _L3_xattn_in['b_norm_out'], 'L3_xattn_g_ffn': _L3_xattn_in['g_ffn'], 'L3_xattn_b_ffn': _L3_xattn_in['b_ffn'], 'L3_xattn_W1': _L3_xattn_in['W1'], 'L3_xattn_b1': _L3_xattn_in['b1'], 'L3_xattn_W2': _L3_xattn_in['W2'], 'L3_xattn_b2': _L3_xattn_in['b2'], 'L3_xattn_log_dt': _L3_xattn_in['log_dt'], 'L3_xattn_A_re': _L3_xattn_in['A_re'], 'L3_xattn_A_im': _L3_xattn_in['A_im'], 'L3_xattn_C_re': _L3_xattn_in['C_re'], 'L3_xattn_C_im': _L3_xattn_in['C_im'], 'L3_xattn_D_skip': _L3_xattn_in['D_skip'], 'L3_xattn_mod_gate': _L3_xattn_in['mod_gate'], 'L3_ffn_U1': _L3_ffn_in['U1'], 'L3_ffn_V1': _L3_ffn_in['V1'], 'L3_ffn_b1': _L3_ffn_in['b1'], 'L3_ffn_U2': _L3_ffn_in['U2'], 'L3_ffn_V2': _L3_ffn_in['V2'], 'L3_ffn_b2': _L3_ffn_in['b2']}

def reference(x, ctx_768, mask_BxS_bf1, mask_BxS2_bf1, L0_xattn_Wq, L0_xattn_bq, L0_xattn_Wk, L0_xattn_bk, L0_xattn_Wv, L0_xattn_bv, L0_xattn_Wo, L0_xattn_bo, L0_ffn_w1, L0_ffn_conv_w, L0_ffn_conv_b, L0_ffn_w2, L1_xattn_Wq, L1_xattn_Wk, L1_xattn_Wv, L1_xattn_Wo, L1_ffn_rw1, L1_ffn_rb1, L1_ffn_rw2, L1_ffn_rb2, L1_ffn_ew1, L1_ffn_eb1, L1_ffn_ew2, L1_ffn_eb2, L2_xattn_wq, L2_xattn_bq, L2_xattn_wk, L2_xattn_bk, L2_xattn_wv, L2_xattn_bv, L2_xattn_wo, L2_xattn_bo, L2_ffn_gate_w, L2_ffn_gate_b, L2_ffn_dp_w1, L2_ffn_dp_b1, L2_ffn_dp_w2, L2_ffn_dp_b2, L2_ffn_ew1, L2_ffn_eb1, L2_ffn_ew2, L2_ffn_eb2, L3_xattn_Wq, L3_xattn_Wk, L3_xattn_Wv, L3_xattn_W_film_in, L3_xattn_b_film_in, L3_xattn_W_film_out, L3_xattn_b_film_out, L3_xattn_g_norm_in, L3_xattn_b_norm_in, L3_xattn_g_norm_out, L3_xattn_b_norm_out, L3_xattn_g_ffn, L3_xattn_b_ffn, L3_xattn_W1, L3_xattn_b1, L3_xattn_W2, L3_xattn_b2, L3_xattn_log_dt, L3_xattn_A_re, L3_xattn_A_im, L3_xattn_C_re, L3_xattn_C_im, L3_xattn_D_skip, L3_xattn_mod_gate, L3_ffn_U1, L3_ffn_V1, L3_ffn_b1, L3_ffn_U2, L3_ffn_V2, L3_ffn_b2):
    import jax
    import jax.numpy as jnp

    def _L0_xattn_ref(query, key_value, Wq, bq, Wk, bk, Wv, bv, Wo, bo):
        import jax, jax.numpy as jnp
        import numpy as np
        NUM_HEADS = 16
        CLAMP = 10000.0
        B, Nq, Cq = query.shape
        Nkv = key_value.shape[1]
        H = NUM_HEADS
        D = Cq // H
        scale = D ** (-0.5)
        q = (query @ Wq + bq).reshape(B, Nq, H, D).transpose(0, 2, 1, 3)
        k = (key_value @ Wk + bk).reshape(B, Nkv, H, D).transpose(0, 2, 1, 3)
        v = (key_value @ Wv + bv).reshape(B, Nkv, H, D).transpose(0, 2, 1, 3)
        attn = jnp.einsum('bhqd,bhkd->bhqk', q, k) * scale
        attn = jnp.clip(attn, -CLAMP, CLAMP)
        attn = jax.nn.softmax(attn, axis=-1)
        attn = jnp.where(jnp.any(jnp.isnan(attn)), jnp.asarray(1.0 / Nkv, attn.dtype), attn)
        x = jnp.einsum('bhqk,bhkd->bqhd', attn, v).reshape(B, Nq, Cq)
        return x @ Wo + bo

    def _L0_ffn_ref(x, w1, conv_w, conv_b, w2):
        import jax, jax.numpy as jnp
        import numpy as np
        B, S, D_MODEL, D_HIDDEN = (4, 512, 256, 1024)

        def act_quant(x):
            scale = 127.0 / jnp.clip(jnp.max(jnp.abs(x), axis=-1, keepdims=True), 1e-05)
            return jnp.clip(jnp.round(x * scale), -128, 127) / scale

        def weight_quant(w):
            scale = 1.0 / jnp.clip(jnp.mean(jnp.abs(w)), 1e-05)
            return jnp.clip(jnp.round(w * scale), -1, 1) / scale

        def bit_linear(x, w):
            xq = x + jax.lax.stop_gradient(act_quant(x) - x)
            wq = w + jax.lax.stop_gradient(weight_quant(w) - w)
            return jnp.einsum('bsd,hd->bsh', xq, wq)

        def depthwise_conv1d(x_bcl, w, b):
            y = jax.lax.conv_general_dilated(x_bcl, w, window_strides=(1,), padding=[(1, 1)], dimension_numbers=('NCH', 'OIH', 'NCH'), feature_group_count=x_bcl.shape[1])
            return y + b[None, :, None]
        h = bit_linear(x, w1)
        h = depthwise_conv1d(h.transpose(0, 2, 1), conv_w, conv_b)
        h = h.transpose(0, 2, 1)
        h = jax.nn.silu(h)
        return bit_linear(h, w2)

    def _L1_xattn_ref(q, k, Wq, Wk, Wv, Wo):
        import jax, jax.numpy as jnp
        import numpy as np
        EPS = 1e-05
        query = q @ Wq.T
        key_p = k @ Wk.T
        value = k @ Wv.T
        sim = jnp.einsum('bqd,bkd->bqk', query, key_p)
        mean = jnp.mean(sim, axis=(1, 2), keepdims=True)
        var = jnp.var(sim, axis=(1, 2), keepdims=True)
        sim = (sim - mean) * jax.lax.rsqrt(var + EPS)
        attn = jax.nn.softmax(sim, axis=-1)
        out = jnp.einsum('bqk,bkd->bqd', attn, value)
        return out @ Wo.T

    def _L1_ffn_ref(x, rw1, rb1, rw2, rb2, ew1, eb1, ew2, eb2):
        import jax, jax.numpy as jnp
        import numpy as np
        B, T, C, E, K, CAP, H = (8, 512, 256, 8, 2, 1024, 1024)
        Bx, Tx, Cx = x.shape
        N = Bx * Tx
        logits = jax.nn.relu(x @ rw1 + rb1) @ rw2 + rb2
        vals, ids = jax.lax.top_k(logits, K)
        probs = jax.nn.softmax(vals, axis=-1)
        ids_f = ids.reshape(N * K)
        probs_f = probs.reshape(N * K)
        xr = jnp.repeat(x.reshape(N, Cx), K, axis=0)
        m = jax.nn.one_hot(ids_f, E, dtype=jnp.int32)
        pos = jnp.cumsum(m, axis=0) - 1
        pos_tok = jnp.take_along_axis(pos, ids_f[:, None], axis=1)[:, 0]
        keep = (pos_tok < CAP).astype(x.dtype)
        pos_c = jnp.clip(pos_tok, 0, CAP - 1)
        disp = jnp.zeros((E, CAP, Cx), x.dtype).at[ids_f, pos_c].add(xr * keep[:, None])
        h = jax.nn.relu(jnp.einsum('enc,ech->enh', disp, ew1) + eb1[:, None, :])
        eo = jnp.einsum('enh,ehc->enc', h, ew2) + eb2[:, None, :]
        y = eo[ids_f, pos_c] * (probs_f * keep)[:, None]
        return y.reshape(Bx, Tx, K, Cx).sum(axis=2)

    def _L2_xattn_ref(x, y, wq, bq, wk, bk, wv, bv, wo, bo):
        import jax, jax.numpy as jnp
        import numpy as np
        N_HEADS = 16
        D_EMBED = 256
        D_CROSS = 192
        D_HEAD = D_EMBED // N_HEADS
        B, SQ, _ = x.shape
        SKV = y.shape[1]
        q = (x @ wq + bq).reshape(B, SQ, N_HEADS, D_HEAD)
        k = (y @ wk + bk).reshape(B, SKV, N_HEADS, D_HEAD)
        v = (y @ wv + bv).reshape(B, SKV, N_HEADS, D_HEAD)
        scores = jnp.einsum('bqhd,bkhd->bhqk', q, k) / jnp.sqrt(jnp.asarray(D_HEAD, x.dtype))
        attn = jax.nn.softmax(scores, axis=-1)
        out = jnp.einsum('bhqk,bkhd->bqhd', attn, v).reshape(B, SQ, D_EMBED)
        return out @ wo + bo

    def _L2_ffn_ref(x, gate_w, gate_b, dp_w1, dp_b1, dp_w2, dp_b2, ew1, eb1, ew2, eb2):
        import jax, jax.numpy as jnp
        import numpy as np
        D_MODEL = 256
        E = 4
        MIN_E = 1
        TH_LO = 0.5
        TH_HI = 2.0
        B, N, D = x.shape
        xf = x.reshape(B * N, D)
        T = B * N
        h = jax.nn.relu(xf @ dp_w1 + dp_b1)
        entropy = jax.nn.softplus(h @ dp_w2 + dp_b2)[:, 0]
        norm = jnp.clip((entropy - TH_LO) / (TH_HI - TH_LO), 0.0, 1.0)
        k_tok = jnp.clip(jnp.round(MIN_E + norm * (E - MIN_E)).astype(jnp.int32), MIN_E, E)
        logits = xf @ gate_w + gate_b
        top_logits, top_idx = jax.lax.top_k(logits, E)
        pos = jnp.arange(E)
        sel = pos[None, :] < k_tok[:, None]
        masked = jnp.where(sel, top_logits, -jnp.inf)
        w_top = jax.nn.softmax(masked, axis=-1)
        dense_w = jnp.zeros((T, E), dtype=xf.dtype).at[jnp.arange(T)[:, None], top_idx].set(w_top)
        hid = jax.nn.relu(jnp.einsum('td,edh->teh', xf, ew1) + eb1[None, :, :])
        y = jnp.einsum('teh,ehd->ted', hid, ew2) + eb2[None, :, :]
        out = jnp.einsum('te,ted->td', dense_w, y)
        return out.reshape(B, N, D)

    def _L3_xattn_ref(x_text, x_vision, text_mask, vision_mask, Wq, Wk, Wv, W_film_in, b_film_in, W_film_out, b_film_out, g_norm_in, b_norm_in, g_norm_out, b_norm_out, g_ffn, b_ffn, W1, b1, W2, b2, log_dt, A_re, A_im, C_re, C_im, D_skip, mod_gate):
        import jax, jax.numpy as jnp
        import numpy as np
        B, T, DT, G, DV = (16, 128, 256, 144, 192)
        H, DH = (4, 32)
        INNER = H * DH
        HID = 4 * DT
        N_STATE = 64
        K_TOP = 32

        def layernorm(x, g, b, eps=1e-05):
            m = x.mean(-1, keepdims=True)
            v = x.var(-1, keepdims=True)
            return (x - m) * jax.lax.rsqrt(v + eps) * g + b

        def s4d(x, log_dt, A_re, A_im, C_re, C_im, D_skip):
            Bb, L, D = x.shape
            dt = jnp.exp(log_dt)
            A = A_re + 1j * A_im
            C = C_re + 1j * C_im
            dtA = dt[:, None] * A
            dC = C * (jnp.exp(dtA) - 1.0) / A
            powers = jnp.exp(dtA[:, :, None] * jnp.arange(L))
            K = 2.0 * jnp.einsum('dn,dnl->dl', dC, powers).real
            n = 2 * L
            Kf = jnp.fft.rfft(K, n=n, axis=-1)
            xf = jnp.fft.rfft(x, n=n, axis=1)
            y = jnp.fft.irfft(xf * Kf.T[None], n=n, axis=1)[:, :L]
            return y + x * D_skip
        Bb, Tt, D = x_text.shape
        Gg = x_vision.shape[1]
        Q = (x_text @ Wq).reshape(Bb, Tt, H, DH)
        K = (x_vision @ Wk).reshape(Bb, Gg, H, DH)
        scores = jnp.einsum('bthd,bghd->bhtg', Q, K) / np.sqrt(DH).astype(np.float32)
        scores = jnp.where(vision_mask[:, None, None, :], scores, -jnp.inf)
        topv, topi = jax.lax.top_k(scores, K_TOP)
        probs = jax.nn.softmax(topv, axis=-1)
        bi = jnp.arange(Bb)[:, None, None, None]
        hi = jnp.arange(H)[None, :, None, None]
        ti = jnp.arange(Tt)[None, None, :, None]
        attn = jnp.zeros_like(scores).at[bi, hi, ti, topi].set(probs)
        attn_mean = attn.mean(axis=1)
        V = x_vision @ Wv
        c_t = jnp.einsum('btg,bgd->btd', attn_mean, V)
        c_t = c_t * text_mask[..., None]
        x = layernorm(x_text, g_norm_in, b_norm_in)
        scale_in, shift_in = jnp.split(c_t @ W_film_in + b_film_in, 2, axis=-1)
        x = x * (1.0 + mod_gate * scale_in) + mod_gate * shift_in
        y = s4d(x, log_dt, A_re, A_im, C_re, C_im, D_skip)
        scale_out, shift_out = jnp.split(c_t @ W_film_out + b_film_out, 2, axis=-1)
        y = y * (1.0 + mod_gate * scale_out) + mod_gate * shift_out
        xt = x_text + y
        h = layernorm(xt, g_ffn, b_ffn)
        h = jax.nn.gelu(h @ W1 + b1, approximate=False) @ W2 + b2
        xt = xt + h
        return layernorm(xt, g_norm_out, b_norm_out)

    def _L3_ffn_ref(x, U1, V1, b1, U2, V2, b2):
        import jax, jax.numpy as jnp
        import numpy as np
        D_MODEL, D_FF, RANK = (256, 1024, 64)
        B, S = (4, 1024)
        P = jnp.einsum('bsd,dr->bsr', x, U1)
        H = jax.nn.gelu(jnp.einsum('bsr,rf->bsf', P, V1) + b1)
        Q = jnp.einsum('bsf,fr->bsr', H, U2)
        return jnp.einsum('bsr,rd->bsd', Q, V2) + b2
    x = x + _L0_xattn_ref(_layernorm(x, axis=-1), ctx_768, L0_xattn_Wq, L0_xattn_bq, L0_xattn_Wk, L0_xattn_bk, L0_xattn_Wv, L0_xattn_bv, L0_xattn_Wo, L0_xattn_bo)
    x = x + _L0_ffn_ref(_layernorm(x, axis=-1), L0_ffn_w1, L0_ffn_conv_w, L0_ffn_conv_b, L0_ffn_w2)
    x = x + _L1_xattn_ref(_layernorm(x, axis=-1), ctx_768, L1_xattn_Wq, L1_xattn_Wk, L1_xattn_Wv, L1_xattn_Wo)
    x = x + _L1_ffn_ref(_layernorm(x, axis=-1), L1_ffn_rw1, L1_ffn_rb1, L1_ffn_rw2, L1_ffn_rb2, L1_ffn_ew1, L1_ffn_eb1, L1_ffn_ew2, L1_ffn_eb2)
    x = x + _L2_xattn_ref(_layernorm(x, axis=-1), ctx_768, L2_xattn_wq, L2_xattn_bq, L2_xattn_wk, L2_xattn_bk, L2_xattn_wv, L2_xattn_bv, L2_xattn_wo, L2_xattn_bo)
    x = x + _L2_ffn_ref(_layernorm(x, axis=-1), L2_ffn_gate_w, L2_ffn_gate_b, L2_ffn_dp_w1, L2_ffn_dp_b1, L2_ffn_dp_w2, L2_ffn_dp_b2, L2_ffn_ew1, L2_ffn_eb1, L2_ffn_ew2, L2_ffn_eb2)
    x = x + _L3_xattn_ref(_layernorm(x, axis=-1), ctx_768, mask_BxS_bf1, mask_BxS2_bf1, L3_xattn_Wq, L3_xattn_Wk, L3_xattn_Wv, L3_xattn_W_film_in, L3_xattn_b_film_in, L3_xattn_W_film_out, L3_xattn_b_film_out, L3_xattn_g_norm_in, L3_xattn_b_norm_in, L3_xattn_g_norm_out, L3_xattn_b_norm_out, L3_xattn_g_ffn, L3_xattn_b_ffn, L3_xattn_W1, L3_xattn_b1, L3_xattn_W2, L3_xattn_b2, L3_xattn_log_dt, L3_xattn_A_re, L3_xattn_A_im, L3_xattn_C_re, L3_xattn_C_im, L3_xattn_D_skip, L3_xattn_mod_gate)
    x = x + _L3_ffn_ref(_layernorm(x, axis=-1), L3_ffn_U1, L3_ffn_V1, L3_ffn_b1, L3_ffn_U2, L3_ffn_V2, L3_ffn_b2)
    return x

_drawn_inputs = setup_inputs


def setup_inputs(seed=0):
    import zlib

    import numpy as np

    out = dict(_drawn_inputs(seed))
    spreads = {'L0_xattn_bq': (0.0, 0.386),
     'L0_xattn_bk': (0.0, 2.0),
     'L0_xattn_bv': (0.0, 0.1),
     'L0_xattn_bo': (0.0, 0.1),
     'L1_ffn_rb1': (0.0, 0.1),
     'L1_ffn_rb2': (0.0, 0.1),
     'L1_ffn_eb1': (0.0, 0.589),
     'L1_ffn_eb2': (0.0, 0.276),
     'L2_xattn_bq': (0.0, 0.425),
     'L2_xattn_bk': (0.0, 2.0),
     'L2_xattn_bv': (0.0, 0.1),
     'L2_xattn_bo': (0.0, 0.1),
     'L2_ffn_gate_b': (0.0, 0.1),
     'L2_ffn_dp_b1': (0.0, 2.0),
     'L2_ffn_eb1': (0.0, 0.408),
     'L2_ffn_eb2': (0.0, 0.1),
     'L3_xattn_b_film_in': (0.0, 0.274),
     'L3_xattn_b_film_out': (0.0, 0.393),
     'L3_xattn_g_norm_in': (1.0, 0.2),
     'L3_xattn_b_norm_in': (0.0, 0.1),
     'L3_xattn_g_norm_out': (1.0, 0.2),
     'L3_xattn_b_norm_out': (0.0, 0.1),
     'L3_xattn_g_ffn': (1.0, 0.6),
     'L3_xattn_b_ffn': (0.0, 2.0),
     'L3_xattn_b1': (0.0, 0.8),
     'L3_xattn_b2': (0.0, 0.353),
     'L3_xattn_A_re': (-0.5, 0.2),
     'L3_ffn_b1': (0.0, 0.8),
     'L3_ffn_b2': (0.0, 0.8)}
    factors = {'L2_ffn_dp_w1': 8.0,
     'L2_ffn_dp_w2': 8.0,
     'L3_xattn_Wq': 8.0,
     'L3_xattn_Wk': 8.0,
     'L3_xattn_Wv': 3.322,
     'L3_xattn_W_film_in': 4.295,
     'L3_xattn_W_film_out': 5.482,
     'L3_ffn_U1': 8.0,
     'L3_ffn_V1': 8.0,
     'L3_ffn_U2': 8.0,
     'L3_ffn_V2': 8.0}
    for name, (base, spread) in spreads.items():
        noise = np.random.default_rng([zlib.crc32(name.encode()), seed]).standard_normal(out[name].shape)
        drawn = base * np.exp(spread * noise) if base else spread * noise
        out[name] = jnp.asarray(drawn.astype(out[name].dtype))
    for name, factor in factors.items():
        out[name] = (out[name] * factor).astype(out[name].dtype)
    return out
```

```python
from contextlib import ExitStack

import numpy as np

import concourse.bass as bass
from concourse import mybir

P = 128
B, S, D = 32, 256, 256
TL = S // P
KD = D // P
SK, DC = 120, 192
CP = DC // 2
H1 = 1024
KH = H1 // P
NE, CAP = 8, 1024
EPS = 1e-5
MAGIC = 12582912.0
LOW = -1e30

F32 = mybir.dt.float32
BF16 = mybir.dt.bfloat16
I32 = mybir.dt.int32
U32 = mybir.dt.uint32
U8 = mybir.dt.uint8
ALU = mybir.AluOpType
ACT = mybir.ActivationFunctionType
AX = mybir.AxisListType


class It:

    def __init__(self, i, at, rounds, n, unroll):
        self.i, self.n, self.at = i, n, at % unroll
        self.round = rounds + at // unroll
        self.p, self.h = self.at % 2, (rounds + at // unroll) * (unroll // 2) + self.at // 2

    def reused(self, by=2):
        return not isinstance(self.i, int) or self.i >= by

    def followed(self, by):
        return not isinstance(self.i, int) or self.i + by < self.n


def pipeline(eng, n, depth, steps, unroll=2, history=2):
    def slot(t, rounds, j):
        for lag, step in steps:
            if not isinstance(t, int) or 0 <= t - lag < n:
                step(It(t - lag, j - lag, rounds, n, unroll))

    first = min(-(-(depth + history) // unroll), n // unroll)
    for t in range(first * unroll):
        slot(t, t // unroll, t % unroll)
    if first < n // unroll:
        with eng.Fori(first, n // unroll) as rounds:
            for j in range(unroll):
                slot(rounds * unroll + j, rounds, j)
    for t in range(n, n + depth):
        slot(t, t // unroll, t % unroll)


class Chain:

    def __init__(self, eng, sem, i, per):
        self.eng, self.sem, self.base, self.per, self.n = eng, sem, i * per, per, 0

    def add(self, ins):
        self.n += 1
        assert self.n <= self.per
        ins.then_inc(self.sem, 1)

    def wait(self):
        self.eng.wait_ge(self.sem, self.base + self.n)


class Stage:

    def __init__(self, nc, name, extra=()):
        self.nc, self.name, self.stack, self.sems = nc, name, ExitStack(), list(extra)

    def sb(self, name, shape, dt=F32):
        return self.stack.enter_context(self.nc.sbuf_tensor(f"{self.name}_{name}", shape, dt))

    def ps(self, name, shape, dt=F32):
        return self.stack.enter_context(self.nc.psum_tensor(f"{self.name}_{name}", shape, dt))

    def sem(self, name):
        s = self.stack.enter_context(self.nc.semaphore(f"{self.name}_{name}"))
        self.sems.append(s)
        return s

    def end(self):
        nc = self.nc
        for s in self.sems:
            nc.sync.sem_clear(s)
        nc.all_engine_barrier()
        self.stack.close()


def apart(eng, const):
    eng.sem_inc(const["apart"], 1)


def layer_norm_stats(dve, chain, x, st, mv, const):
    for t in range(TL):
        chain.add(dve.bn_stats(st[:, t, :], x[:, t, :]))
    chain.wait()
    apart(dve, const)
    for t in range(TL):
        chain.add(dve.bn_aggr(mv[:, t, :], st[:, t, :]))


def inverse_root(pool, chain, mv, rs, const):
    apart(pool, const)
    chain.add(pool.tensor_scalar(rs, mv, EPS, None, ALU.add))
    chain.wait()
    w = rs.shape[1]
    chain.add(pool.tensor_tensor(rs, rs, const["mhalf"][:, 0:w], ALU.pow))


def normalise(dve, x, mv, rs, out):
    return [dve.tensor_scalar(out[:, t, :], x[:, t, :], mv[:, t, 0:1], rs[:, t:t + 1], ALU.subtract, ALU.mult)
            for t in range(TL)]


def setup(nc, keep):
    sb = lambda n, s, d=F32: keep.enter_context(nc.sbuf_tensor(n, s, d))
    c = {
        "ident": sb("c_ident", [P, P]), "identb": sb("c_identb", [P, P], BF16), "ones": sb("c_ones", [P, P]),
        "tri": sb("c_tri", [P, P]), "back": sb("c_back", [P, P]), "heads16": sb("c_heads16", [P, 8]), "heads4": sb("c_heads4", [P, 4]),
        "mhalf": sb("c_mhalf", [P, 4]), "iota8": sb("c_iota8", [P, 8]),
        "batch": sb("c_batch", [P, TL], I32),
    }
    c["apart"] = keep.enter_context(nc.semaphore("apart"))
    for name in ("rows_placed", "rows_taken", "rows_back"):
        c[name] = [keep.enter_context(nc.semaphore(f"{name}{p}")) for p in range(2)]
    st = Stage(nc, "c")
    done = st.sem("done")
    with nc.Block() as block:
        @block.gpsimd
        def _(pool):
            n = 0
            for name in ("ident", "identb", "ones", "tri", "back", "heads16", "heads4"):
                pool.memset(c[name][:], 1.0).then_inc(done, 1)
                n += 1
            pool.memset(c["mhalf"][:], -0.5).then_inc(done, 1)
            pool.iota(c["batch"][:], [[0, TL]], base=S, channel_multiplier=0).then_inc(done, 1)
            pool.iota(c["iota8"][:], [[1, 8]], base=0, channel_multiplier=0,
                      allow_small_or_imprecise_dtypes=True).then_inc(done, 1)
            n += 3
            pool.wait_ge(done, n)
            for name in ("ident", "identb"):
                pool.affine_select(out=c[name][:], in_=c[name][:], compare_op=ALU.is_equal, fill=0.0, base=0,
                                   pattern=[[-1, P]], channel_multiplier=1).then_inc(done, 1)
                n += 1
            pool.affine_select(out=c["tri"][:], in_=c["tri"][:], compare_op=ALU.is_gt, fill=0.0, base=0,
                               pattern=[[1, P]], channel_multiplier=-1).then_inc(done, 1)
            n += 1
            pool.affine_select(out=c["back"][:], in_=c["back"][:], compare_op=ALU.is_equal, fill=0.0, base=1 - P,
                               pattern=[[1, P]], channel_multiplier=1).then_inc(done, 1)
            n += 1
            for name, wide, k in (("heads16", 16, 8), ("heads4", 32, 4)):
                pool.affine_select(out=c[name][:], in_=c[name][:], compare_op=ALU.is_ge, fill=0.0, base=0,
                                   pattern=[[-wide, k]], channel_multiplier=1).then_inc(done, 1)
                n += 1
                pool.wait_ge(done, n)
                pool.affine_select(out=c[name][:], in_=c[name][:], compare_op=ALU.is_ge, fill=0.0, base=wide - 1,
                                   pattern=[[wide, k]], channel_multiplier=-1).then_inc(done, 1)
                n += 1
            pool.wait_ge(done, n)
    st.end()
    return c


def heads_attention(nc, const, name, src, dst, ctx, w, clip):
    NH, DH = 16, 16
    HM = P // DH
    UW = HM * SK
    st = Stage(nc, name, [const["apart"]])
    wq, wk, wv, wo = (st.sb(n, s) for n, s in (("wq", [P, KD, D]), ("wk", [CP, 2, D]), ("wv", [CP, 2, D]), ("wo", [P, KD, D])))
    bq, bk, bv, bo = (st.sb(n, s) for n, s in (("bq", [P, KD]), ("bk", [P, KD]), ("bv", [P, KD]), ("bo", [P, D])))
    bvw = st.sb("bvw", [P, KD, P])
    xb = [st.sb(f"xb{p}", [P, TL, D]) for p in range(2)]
    cb = [st.sb(f"cb{p}", [CP, 2, SK]) for p in range(2)]
    xres = [st.sb(f"xres{p}", [P, TL, D]) for p in range(2)]
    xo = [st.sb(f"xo{p}", [P, TL, D]) for p in range(2)]
    stt = [st.sb(f"st{p}", [P, TL, 6]) for p in range(2)]
    mv = [st.sb(f"mv{p}", [P, TL, 2]) for p in range(2)]
    rs = [st.sb(f"rs{p}", [P, TL]) for p in range(2)]
    xn = [st.sb(f"xn{p}", [P, TL, D]) for p in range(2)]
    xnT = [st.sb(f"xnT{p}", [P, KD, S]) for p in range(2)]
    qT = [st.sb(f"qT{p}", [P, KD, S]) for p in range(2)]
    kT = [st.sb(f"kT{p}", [P, KD, SK]) for p in range(2)]
    kd = [st.sb(f"kd{p}", [P, KD, HM, SK]) for p in range(2)]
    v = [st.sb(f"v{p}", [SK, NH, DH + 1]) for p in range(2)]
    pr = [st.sb(f"pr{p}", [P, HM, SK]) for p in range(4)]
    mx = [st.sb(f"mx{p}", [P, HM]) for p in range(2)]
    prT = [st.sb(f"prT{p}", [SK, HM, P]) for p in range(2)]
    rec = [st.sb(f"rec{p}", [P, NH]) for p in range(2)]
    ao = [st.sb(f"ao{p}", [P, NH, DH + 1]) for p in range(2)]
    o = [st.sb(f"o{p}", [P, TL, D]) for p in range(2)]
    oT = [st.sb(f"oT{p}", [P, KD, S]) for p in range(2)]
    front = st.ps("front", [P, 512])
    score = [st.ps(f"score{p}", [P, 2, 512]) for p in range(2)]
    turn = st.ps("turn", [P, 2, 512])
    av = st.ps("av", [P, 512])

    weights = st.sem("weights")
    x_in = [st.sem(f"x_in{p}") for p in range(2)]
    c_in = [st.sem(f"c_in{p}") for p in range(2)]
    r_in = [st.sem(f"r_in{p}") for p in range(2)]
    stored = [st.sem(f"stored{p}") for p in range(2)]
    stats, roots, xn_ready, xT_ps, xT_ready, q_ps, q_ready, kv_ps, k_ready, v_ready, kd_ready = (
        st.sem(n) for n in ("stats", "roots", "xn_ready", "xT_ps", "xT_ready", "q_ps", "q_ready", "kv_ps", "k_ready", "v_ready", "kd_ready"))
    shifted = st.sem("shifted")
    s_ps, soft, exp_ready, turned, turn_ready, av_ps, av_ready, rec_ready, o_ready, oT_ps, oT_ready, y_ps, y_ready, res_ready, bias_in, bias_ps, bias_ready = (
        st.sem(n) for n in ("s_ps", "soft", "exp_ready", "turned", "turn_ready", "av_ps", "av_ready", "rec_ready", "o_ready", "oT_ps",
                            "oT_ready", "y_ps", "y_ready", "res_ready", "bias_in", "bias_ps", "bias_ready"))
    NW = 8
    LINKS, READ = (2, 1) if clip else (2, 2)
    DEPTH = 6
    src_v = src.rearrange("b (t p) d -> b p t d", p=P)
    dst_v = dst.rearrange("b (t p) d -> b p t d", p=P)

    with nc.Block() as block:
        @block.sync
        def _(sp):
            for a, n in ((wq, "Wq"), (wk, "Wk"), (wv, "Wv"), (wo, "Wo"), (bq, "bq"), (bk, "bk"), (bv, "bv")):
                sp.dma_start(a[:], w[n]).then_inc(weights, 16)
            sp.dma_start(bo[:], w["bo"].partition_broadcast(P)).then_inc(weights, 16)

            def load(it):
                if it.reused():
                    sp.wait_ge(xn_ready, it.i - 1)
                    sp.wait_ge(kv_ps, it.i - 1)
                sp.dma_start(xb[it.p][:], src_v[it.i]).then_inc(x_in[it.p], 16)
                sp.dma_start(cb[it.p][:], ctx[it.i]).then_inc(c_in[it.p], 16)

            def load_residual(it):
                if it.reused():
                    sp.wait_ge(y_ready, it.i - 1)
                sp.dma_start(xres[it.p][:], src_v[it.i]).then_inc(r_in[it.p], 16)

            def store(it):
                sp.wait_ge(y_ready, it.i + 1)
                sp.dma_start(dst_v[it.i], xo[it.p][:]).then_inc(stored[it.p], 16)

            pipeline(sp, B, DEPTH, [(4, load_residual), (6, store), (0, load)])
            for p in range(2):
                sp.wait_ge(stored[p], 16 * (B // 2))

        @block.gpsimd
        def _(pool):
            for p in range(2):
                pool.memset(v[p][:, :, DH:DH + 1], 1.0).then_inc(v_ready, 1)

            def roots_of(it):
                pool.wait_ge(stats, 4 * it.i + 4)
                c = Chain(pool, roots, it.i, 2)
                inverse_root(pool, c, mv[it.p][:, :, 1], rs[it.p][:], const)

            def spread_k(it):
                pool.wait_ge(k_ready, 2 * it.i + 2)
                if it.reused():
                    pool.wait_ge(s_ps, 4 * it.i - 4)
                pool.tensor_tensor(kd[it.p][:], kT[it.p][:].unsqueeze(2).to_broadcast([P, KD, HM, SK]),
                                   const["heads16"][:].unsqueeze(1).unsqueeze(3).to_broadcast([P, KD, HM, SK]),
                                   ALU.mult).then_inc(kd_ready, 1)

            def add_bias(it):
                pool.wait_ge(r_in[it.p], 16 * (it.h + 1))
                pool.tensor_tensor(xres[it.p][:], xres[it.p][:], bo[:].unsqueeze(1).to_broadcast([P, TL, D]),
                                   ALU.add).then_inc(res_ready, 1)

            def take_off(u):
                def step(it):
                    pool.wait_ge(soft, LINKS * (4 * it.i + u + 1))
                    pool.tensor_tensor(pr[u][:], pr[u][:], mx[u % 2][:].unsqueeze(2).to_broadcast([P, HM, SK]), ALU.subtract).then_inc(shifted, 1)
                return step

            pool.wait_ge(bias_ready, 1)
            if clip:
                pipeline(pool, B, DEPTH, [
                    (3, take_off(0)), (1, roots_of), (4, add_bias), (3, take_off(1)), (3, take_off(2)), (2, spread_k),
                    (3, take_off(3))], history=4)
            else:
                pipeline(pool, B, DEPTH, [(1, roots_of), (2, spread_k), (4, add_bias)])

        @block.vector
        def _(dve):
            dve.wait_ge(weights, 16 * NW)
            dve.tensor_copy(bvw[:], bv[:].unsqueeze(2).to_broadcast([P, KD, P])).then_inc(bias_in, 1)
            dve.wait_ge(bias_ps, 1)
            dve.tensor_tensor(bo[:], front[:, 0:D], bo[:], ALU.add).then_inc(bias_ready, 1)
            dve.tensor_scalar(bq[:], bq[:], DH ** -0.5, None, ALU.mult).then_inc(bias_ready, 1)

            def norm_stats(it):
                dve.wait_ge(x_in[it.p], 16 * (it.h + 1))
                layer_norm_stats(dve, Chain(dve, stats, it.i, 4), xb[it.p], stt[it.p], mv[it.p], const)

            def norm(it):
                dve.wait_ge(roots, 2 * it.i + 2)
                if it.reused():
                    dve.wait_ge(xT_ps, it.i - 1)
                normalise(dve, xb[it.p], mv[it.p], rs[it.p], xn[it.p])[-1].then_inc(xn_ready, 1)

            def softmax_in(u):
                def step(it):
                    a, p = score[u % 2], pr[u]
                    s_in = a[:, :, 0:UW // 2].rearrange("p b (h k) -> p b h k", k=SK)
                    p4 = p[:].rearrange("p (b h) k -> p b h k", b=2)
                    c = Chain(dve, soft, it.i * 4 + u, LINKS)
                    dve.wait_ge(s_ps, 4 * it.i + u + 1)
                    if it.reused(1):
                        dve.wait_ge(turned, 4 * it.i + u - 3)
                    if clip:
                        c.add(dve.tensor_scalar(p4, s_in, clip, -clip, ALU.min, ALU.max))
                        c.wait()
                        if it.reused(1) or u >= 2:
                            dve.wait_ge(shifted, 4 * it.i + u - 1)
                        c.add(dve.tensor_reduce(mx[u % 2][:], p4, AX.X, ALU.max))
                        return
                    c.add(dve.tensor_reduce(mx[u % 2][:], s_in, AX.X, ALU.max))
                    c.wait()
                    m4 = mx[u % 2][:].rearrange("p (b h) -> p b h", b=2).unsqueeze(3).to_broadcast([P, 2, HM // 2, SK])
                    c.add(dve.tensor_tensor(p4, s_in, m4, ALU.subtract))
                return step

            def attend_out(t):
                def step(it):
                    dve.wait_ge(av_ready, 2 * it.i + t + 1)
                    if it.reused():
                        dve.wait_ge(oT_ps, it.i - 1)
                    dve.reciprocal(rec[t][:], ao[t][:, :, DH]).then_inc(rec_ready, 1)
                    dve.wait_ge(rec_ready, 2 * it.i + t + 1)
                    dve.tensor_tensor(o[it.p][:, t, :].rearrange("p (h d) -> p h d", d=DH), ao[t][:, :, 0:DH],
                                      rec[t][:].unsqueeze(2).to_broadcast([P, NH, DH]), ALU.mult).then_inc(o_ready, 1)
                return step

            def y_out(it):
                dve.wait_ge(y_ps, it.i + 1)
                dve.wait_ge(res_ready, it.i + 1)
                if it.reused():
                    dve.wait_ge(stored[it.p], 16 * it.h)
                dve.tensor_tensor(xo[it.p][:], front[:].rearrange("p (t d) -> p t d", t=TL), xres[it.p][:],
                                  ALU.add).then_inc(y_ready, 1)

            if clip:
                pipeline(dve, B, DEPTH, [
                    (1, norm_stats), (3, softmax_in(0)), (3, softmax_in(1)), (1, norm), (4, attend_out(0)), (3, softmax_in(2)),
                    (3, softmax_in(3)), (4, attend_out(1)), (5, y_out)], history=4)
            else:
                pipeline(dve, B, DEPTH, [
                    (3, softmax_in(0)), (1, norm_stats), (1, norm), (3, softmax_in(1)), (3, softmax_in(2)), (4, attend_out(0)),
                    (4, attend_out(1)), (3, softmax_in(3)), (5, y_out)], history=4)

        @block.scalar
        def _(act):
            act.wait_ge(bias_ready, 2)

            def xT_out(it):
                act.wait_ge(xT_ps, it.i + 1)
                if it.reused():
                    act.wait_ge(q_ps, it.i - 1)
                act.copy(xnT[it.p][:], front[:].rearrange("p (k s) -> p k s", k=KD)).then_inc(xT_ready, 1)

            def q_out(it):
                act.wait_ge(q_ps, it.i + 1)
                if it.reused():
                    act.wait_ge(s_ps, 4 * it.i - 4)
                for m in range(KD):
                    last = act.activation(qT[it.p][:, m, :], front[:, m * S:(m + 1) * S], ACT.Identity, bias=bq[:, m:m + 1],
                                          scale=DH ** -0.5)
                last.then_inc(q_ready, 1)

            def kv_out(it):
                act.wait_ge(kv_ps, it.i + 1)
                if it.reused():
                    act.wait_ge(kd_ready, it.i - 1)
                for m in range(KD):
                    act.activation(kT[it.p][:, m, :], front[:, m * SK:(m + 1) * SK], ACT.Identity,
                                   bias=bk[:, m:m + 1]).then_inc(k_ready, 1)
                if it.reused():
                    act.wait_ge(av_ps, 4 * it.i - 4)
                act.copy(v[it.p][:, :, 0:DH], front[0:SK, 256:512].rearrange("p (h d) -> p h d", d=DH)).then_inc(v_ready, 1)

            def attend_copy(t):
                def step(it):
                    act.wait_ge(av_ps, 4 * it.i + 2 * t + 2)
                    if it.reused(1):
                        act.wait_ge(o_ready, 2 * it.i + t - 1)
                    act.copy(ao[t][:], av[:, 0:NH * (DH + 1)].rearrange("p (h d) -> p h d", d=DH + 1)).then_inc(av_ready, 1)
                return step

            def exps(u):
                def step(it):
                    if clip:
                        act.wait_ge(shifted, 4 * it.i + u + 1)
                    else:
                        act.wait_ge(soft, LINKS * (4 * it.i + u + 1))
                    act.activation(pr[u][:], pr[u][:], ACT.Exp).then_inc(exp_ready, 1)
                return step

            def turn_out(u):
                def step(it):
                    act.wait_ge(turned, 4 * it.i + u + 1)
                    if it.reused(1) or u >= 2:
                        act.wait_ge(av_ps, 4 * it.i + u - 1)
                    act.copy(prT[u % 2][:], turn[0:SK, :, :].rearrange("p b (h q) -> p (b h) q", q=P)).then_inc(turn_ready, 1)
                return step

            def oT_out(it):
                act.wait_ge(oT_ps, it.i + 1)
                if it.reused():
                    act.wait_ge(y_ps, it.i - 1)
                act.copy(oT[it.p][:], turn[:, 0, :].rearrange("p (k s) -> p k s", k=KD)).then_inc(oT_ready, 1)

            if clip:
                pipeline(act, B, DEPTH, [
                    (4, turn_out(2)), (2, xT_out), (3, exps(0)), (4, attend_copy(0)), (3, exps(1)), (4, turn_out(3)), (2, q_out),
                    (2, kv_out), (3, turn_out(0)), (3, exps(2)), (4, attend_copy(1)), (3, turn_out(1)), (3, exps(3)),
                    (4, oT_out)], history=4)
            else:
                pipeline(act, B, DEPTH, [
                    (3, exps(0)), (4, turn_out(2)), (2, xT_out), (4, attend_copy(0)), (3, exps(1)), (4, turn_out(3)), (2, q_out),
                    (3, turn_out(0)), (4, attend_copy(1)), (3, exps(2)), (2, kv_out), (3, turn_out(1)), (3, exps(3)),
                    (4, oT_out)], history=4)

        @block.tensor
        def _(pe):
            pe.wait_ge(weights, 16 * NW)
            pe.wait_ge(bias_in, 1)
            for k in range(KD):
                last = pe.matmul(front[:, 0:D], bvw[:, k, :], wo[:, k, :], start=k == 0, stop=k == KD - 1)
            last.then_inc(bias_ps, 1)
            pe.wait_ge(bias_ready, 1)
            pe.wait_ge(v_ready, 2)

            def turn_x(it):
                pe.wait_ge(xn_ready, it.i + 1)
                if it.reused(4):
                    pe.wait_ge(y_ready, it.i - 3)
                elif it.reused(1):
                    pe.wait_ge(k_ready, 2 * it.i)
                    pe.wait_ge(v_ready, it.i + 2)
                for t in range(TL):
                    for k in range(KD):
                        last = pe.transpose(front[:, k * S + t * P:k * S + (t + 1) * P], xn[it.p][:, t, k * P:(k + 1) * P],
                                            const["ident"][:])
                last.then_inc(xT_ps, 1)

            def project_q(it):
                pe.wait_ge(xT_ready, it.i + 1)
                for m in range(KD):
                    for k in range(KD):
                        last = pe.matmul(front[:, m * S:(m + 1) * S], wq[:, k, m * P:(m + 1) * P], xnT[it.p][:, k, :],
                                         start=k == 0, stop=k == KD - 1)
                last.then_inc(q_ps, 1)

            def project_kv(it):
                pe.wait_ge(c_in[it.p], 16 * (it.h + 1))
                pe.wait_ge(q_ready, it.i + 1)
                for m in range(KD):
                    for k in range(2):
                        pe.matmul(front[:, m * SK:(m + 1) * SK], wk[:, k, m * P:(m + 1) * P], cb[it.p][:, k, :],
                                  start=k == 0, stop=k == 1)
                for k in range(2):
                    last = pe.matmul(front[0:SK, 256:512], cb[it.p][:, k, :], wv[:, k, :], start=k == 0, stop=k == 1)
                last.then_inc(kv_ps, 1)

            def scores(u):
                t, m = u // 2, u % 2

                def step(it):
                    if u == 0:
                        pe.wait_ge(kd_ready, it.i + 1)
                    if it.reused(1) or u >= 2:
                        pe.wait_ge(soft, LINKS * (4 * it.i + u - 2) + READ)
                    for b in range(2):
                        last = pe.matmul(score[u % 2][:, b, 0:UW // 2], qT[it.p][:, m, t * P:(t + 1) * P],
                                         kd[it.p][:, m, b * HM // 2:(b + 1) * HM // 2, :].rearrange("p h k -> p (h k)"),
                                         start=True, stop=True)
                    last.then_inc(s_ps, 1)
                return step

            def turn_p(u):
                def step(it):
                    pe.wait_ge(exp_ready, 4 * it.i + u + 1)
                    if it.reused(1) or u >= 1:
                        pe.wait_ge(turn_ready, 4 * it.i + u)
                    if u == 2 and it.reused(1):
                        pe.wait_ge(oT_ready, it.i)
                    for h in range(HM):
                        last = pe.transpose(turn[0:SK, h // 4, (h % 4) * P:(h % 4 + 1) * P], pr[u][:, h, :],
                                            const["ident"][:])
                    last.then_inc(turned, 1)
                return step

            def attend(u):
                t, m = u // 2, u % 2

                def step(it):
                    pe.wait_ge(turn_ready, 4 * it.i + u + 1)
                    if u == 0:
                        pe.wait_ge(v_ready, it.i + 3)
                    if m == 0 and (it.reused(1) or t == 1):
                        pe.wait_ge(av_ready, 2 * it.i + t)
                    for h in range(HM):
                        at = (m * HM + h) * (DH + 1)
                        last = pe.matmul(av[:, at:at + DH + 1], prT[u % 2][:, h, :], v[it.p][:, m * HM + h, :],
                                         start=True, stop=True)
                    last.then_inc(av_ps, 1)
                return step

            def turn_o(it):
                pe.wait_ge(o_ready, 2 * it.i + 2)
                if it.followed(1):
                    pe.wait_ge(turn_ready, 4 * it.i + 6)
                else:
                    pe.wait_ge(turn_ready, 4 * it.i + 4)
                for t in range(TL):
                    for k in range(KD):
                        last = pe.transpose(turn[:, 0, k * S + t * P:k * S + (t + 1) * P], o[it.p][:, t, k * P:(k + 1) * P],
                                            const["ident"][:])
                last.then_inc(oT_ps, 1)

            def project_o(it):
                pe.wait_ge(oT_ready, it.i + 1)
                if it.followed(3):
                    pe.wait_ge(k_ready, 2 * it.i + 8)
                    pe.wait_ge(v_ready, it.i + 6)
                elif it.reused(1):
                    pe.wait_ge(y_ready, it.i)
                for t in range(TL):
                    for k in range(KD):
                        last = pe.matmul(front[:, t * D:(t + 1) * D], oT[it.p][:, k, t * P:(t + 1) * P], wo[:, k, :],
                                         start=k == 0, stop=k == KD - 1)
                last.then_inc(y_ps, 1)

            if clip:
                pipeline(pe, B, DEPTH, [
                    (3, scores(0)), (4, attend(1)), (4, turn_p(2)), (2, turn_x), (3, scores(1)), (4, turn_p(3)), (4, attend(2)),
                    (2, project_q), (3, scores(2)), (3, turn_p(0)), (2, project_kv), (4, attend(3)), (3, scores(3)),
                    (5, project_o), (3, turn_p(1)), (3, attend(0)), (4, turn_o)], history=4)
            else:
                pipeline(pe, B, DEPTH, [
                    (3, scores(0)), (4, turn_p(2)), (4, attend(1)), (2, turn_x), (3, scores(1)), (4, turn_p(3)), (4, attend(2)),
                    (2, project_q), (3, scores(2)), (3, turn_p(0)), (4, attend(3)), (2, project_kv), (3, scores(3)),
                    (5, project_o), (3, turn_p(1)), (3, attend(0)), (4, turn_o)], history=4)
    st.end()


def ternary_feed_forward(nc, const, src, dst, w):
    st = Stage(nc, "f0", [const["apart"]])
    wf = st.sb("wf", [P, KD * H1])
    w1q, w2q = st.sb("w1q", [P, KD, H1], BF16), st.sb("w2q", [P, KH, D], BF16)
    taps, cbias = st.sb("taps", [P, KH, 3]), st.sb("cbias", [P, KH])
    diag = st.sb("diag", [P, KH, 3, P])
    wsum, wmean, wscale = (st.sb(n, [P, 2]) for n in ("wsum", "wmean", "wscale"))
    two = range(2)
    xb, xres, xo, xn = ([st.sb(f"{n}{p}", [P, TL, D]) for p in two] for n in ("xb", "xres", "xo", "xn"))
    stt, mv, rs = ([st.sb(f"{n}{p}", [P, TL, k]) for p in two] for n, k in (("st", 6), ("mv", 2), ("rs", 1)))
    amax, ascale, ainv, hmax, hscale, hinv = ([st.sb(f"{n}{p}", [P, TL]) for p in two]
                                              for n in ("amax", "ascale", "ainv", "hmax", "hscale", "hinv"))
    qx = [st.sb(f"qx{p}", [P, TL, D], BF16) for p in two]
    qxT = [st.sb(f"qxT{p}", [P, KD, S], BF16) for p in two]
    dg, dg2 = ([st.sb(f"{n}{p}", [P, TL, P]) for p in two] for n in ("dg", "dg2"))
    row, row2 = ([st.sb(f"{n}{p}", [P, S]) for p in two] for n in ("row", "row2"))
    hs = [st.sb(f"hs{p}", [P, KH, S + 2]) for p in two]
    y = [st.sb(f"y{p}", [P, KH, S]) for p in range(4)]
    pmax = [st.sb(f"pmax{p}", [P, S]) for p in two]
    qh = [st.sb(f"qh{p}", [P, KH, S], BF16) for p in two]
    qt_ps, aux, y_ps = st.ps("qt_ps", [P, KD * S], BF16), st.ps("aux", [P, 512]), st.ps("y_ps", [P, TL, D])
    h_ps, c_ps = ([st.ps(f"{n}{p}", [P, 2, S]) for p in two] for n in ("h_ps", "c_ps"))

    weights, w_one, w_all, sums, consts = (st.sem(n) for n in ("weights", "w_one", "w_all", "sums", "consts"))
    x_in, r_in, stored = ([st.sem(f"{n}{p}") for p in two] for n in ("x_in", "r_in", "stored"))
    stats, roots, quant, dg_ready, turned, turn_ready, row_done, row_ready = (
        st.sem(n) for n in ("stats", "roots", "quant", "dg_ready", "turned", "turn_ready", "row_done", "row_ready"))
    h_done, h_ready, c_done, silu_ready, pmax_ready, pmax_turned, hq, dg2_ready, row2_done, row2_ready = (
        st.sem(n) for n in ("h_done", "h_ready", "c_done", "silu_ready", "pmax_ready", "pmax_turned", "hq", "dg2_ready", "row2_done", "row2_ready"))
    multiplied = st.sem("multiplied")
    scaled, qh_ready, y_done, y_ready = (st.sem(n) for n in ("scaled", "qh_ready", "y_done", "y_ready"))
    QN = 10
    HQ = 4
    DEPTH = 8
    src_v = src.rearrange("b (t p) d -> b p t d", p=P)
    dst_v = dst.rearrange("b (t p) d -> b p t d", p=P)

    with nc.Block() as block:
        @block.sync
        def _(sp):
            sp.dma_start(wf[:], w["w1"].rearrange("p k n -> p (k n)")).then_inc(w_one, 16)
            sp.dma_start(taps[:], w["conv_w"]).then_inc(weights, 16)
            sp.dma_start(cbias[:], w["conv_b"]).then_inc(weights, 16)
            sp.wait_ge(w_all, 4)
            sp.dma_start(wf[:], w["w2"].rearrange("p k n -> p (k n)")).then_inc(w_one, 16)

            def load(it):
                if it.reused():
                    sp.wait_ge(quant, QN * (it.i - 2) + 2)
                sp.dma_start(xb[it.p][:], src_v[it.i]).then_inc(x_in[it.p], 16)

            def load_residual(it):
                if it.reused():
                    sp.wait_ge(y_ready, it.i - 1)
                sp.dma_start(xres[it.p][:], src_v[it.i]).then_inc(r_in[it.p], 16)

            def store(it):
                sp.wait_ge(y_ready, it.i + 1)
                sp.dma_start(dst_v[it.i], xo[it.p][:]).then_inc(stored[it.p], 16)

            pipeline(sp, B, DEPTH, [(5, load_residual), (0, load), (8, store)], unroll=4, history=4)
            for p in two:
                sp.wait_ge(stored[p], 16 * (B // 2))

        @block.gpsimd
        def _(pool):
            for p in two:
                pool.memset(hs[p][:, :, 0:1], 0.0).then_inc(consts, 1)
                pool.memset(hs[p][:, :, S + 1:S + 2], 0.0).then_inc(consts, 1)
            pool.wait_ge(weights, 32)
            for c in range(KH):
                for j in range(3):
                    pool.tensor_tensor(diag[:, c, j, :], const["ident"][:], taps[:, c, j:j + 1].to_broadcast([P, P]),
                                       ALU.mult).then_inc(consts, 1)

            def roots_of(it):
                pool.wait_ge(stats, 4 * it.i + 4)
                inverse_root(pool, Chain(pool, roots, it.i, 2), mv[it.p][:, :, 1], rs[it.p][:, :, 0], const)

            def spread(out, scale, ready, links, done, used):
                def step(it):
                    pool.wait_ge(ready, links * (it.i + 1))
                    if it.reused():
                        pool.wait_ge(used, it.i - 1)
                    pool.tensor_tensor(out[it.p][:], const["ident"][:].unsqueeze(1).to_broadcast([P, TL, P]),
                                       scale[it.p][:].unsqueeze(2).to_broadcast([P, TL, P]), ALU.mult).then_inc(done, 1)
                return step

            def scale_hidden(it):
                pool.wait_ge(row2_ready, it.i + 1)
                pool.tensor_tensor(y[it.at][:], y[it.at][:], row2[it.p][:].unsqueeze(1).to_broadcast([P, KH, S]), ALU.mult).then_inc(multiplied, 1)

            pipeline(pool, B, DEPTH, [
                (6, scale_hidden), (5, spread(dg2, hscale, hq, HQ, dg2_ready, row2_done)), (1, roots_of),
                (2, spread(dg, ainv, quant, QN, dg_ready, row_done))], unroll=4, history=4)

        @block.vector
        def _(dve):
            n = 0
            for m, wq in enumerate((w1q, w2q)):
                dve.wait_ge(w_one, 16 * (m + 1))
                dve.tensor_reduce(wsum[:, m:m + 1], wf[:], AX.X, ALU.add, apply_absolute_value=True).then_inc(sums, 1)
                dve.wait_ge(w_all, 4 * m + 1)
                dve.tensor_scalar(wmean[:, m:m + 1], aux[:, 0:1], 1.0 / (D * H1), 1e-5, ALU.mult, ALU.max).then_inc(consts, 1)
                n += 1
                dve.wait_ge(consts, 4 + KH * 3 + n)
                dve.reciprocal(wscale[:, m:m + 1], wmean[:, m:m + 1]).then_inc(consts, 1)
                n += 1
                dve.wait_ge(consts, 4 + KH * 3 + n)
                dve.tensor_scalar(wf[:], wf[:], wscale[:, m:m + 1], MAGIC, ALU.mult, ALU.add).then_inc(w_all, 1)
                dve.wait_ge(w_all, 4 * m + 2)
                dve.tensor_scalar(wf[:], wf[:], MAGIC, 1.0, ALU.subtract, ALU.min).then_inc(w_all, 1)
                dve.wait_ge(w_all, 4 * m + 3)
                dve.tensor_scalar(wq[:].rearrange("p k n -> p (k n)"), wf[:], -1.0, None, ALU.max).then_inc(w_all, 1)
            dve.tensor_scalar(wsum[:], wmean[:], 1.0 / 127.0, None, ALU.mult).then_inc(consts, 1)
            n += 1
            dve.wait_ge(consts, 4 + KH * 3 + n)
            back = wsum

            def norm_stats(it):
                dve.wait_ge(x_in[it.p], 16 * (it.h + 1))
                layer_norm_stats(dve, Chain(dve, stats, it.i, 4), xb[it.p], stt[it.p], mv[it.p], const)

            def quantise(it):
                p = it.p
                dve.wait_ge(roots, 2 * it.i + 2)
                c = Chain(dve, quant, it.i, QN)
                for ins in normalise(dve, xb[p], mv[p], rs[p][:, :, 0], xn[p]):
                    c.add(ins)
                c.wait()
                c.add(dve.tensor_reduce(amax[p][:], xn[p][:], AX.X, ALU.max, apply_absolute_value=True))
                c.wait()
                c.add(dve.tensor_scalar(amax[p][:], amax[p][:], 1e-5, None, ALU.max))
                c.wait()
                c.add(dve.reciprocal(ascale[p][:], amax[p][:]))
                c.wait()
                c.add(dve.tensor_scalar(ascale[p][:], ascale[p][:], 127.0, None, ALU.mult))
                c.wait()
                if it.reused():
                    dve.wait_ge(dg_ready, it.i - 1)
                    dve.wait_ge(turned, it.i - 1)
                for t in range(TL):
                    c.add(dve.tensor_scalar(xn[p][:, t, :], xn[p][:, t, :], ascale[p][:, t:t + 1], MAGIC, ALU.mult, ALU.add))
                c.wait()
                c.add(dve.tensor_scalar(qx[p][:], xn[p][:], MAGIC, 127.0, ALU.subtract, ALU.min))
                c.add(dve.tensor_scalar(ainv[p][:], amax[p][:], back[:, 0:1], None, ALU.mult))

            def h_out(m):
                def step(it):
                    if m == 0:
                        dve.wait_ge(row_ready, it.i + 1)
                        if it.reused():
                            dve.wait_ge(c_done, 4 * it.i - 4)
                    dve.wait_ge(h_done, 4 * it.i + m + 1)
                    dve.tensor_tensor(hs[it.p][:, 2 * m:2 * m + 2, 1:S + 1], h_ps[m % 2][:],
                                      row[it.p][:].unsqueeze(1).to_broadcast([P, 2, S]), ALU.mult).then_inc(h_ready, 1)
                return step

            def hidden_max(it):
                dve.wait_ge(silu_ready, KH * (it.i + 1))
                if it.reused():
                    dve.wait_ge(pmax_turned, it.i - 1)
                dve.tensor_reduce(pmax[it.p][:], y[it.at][:].rearrange("p c s -> p s c"), AX.X, ALU.max,
                                  apply_absolute_value=True).then_inc(pmax_ready, 1)

            def hidden_scale(it):
                p = it.p
                dve.wait_ge(pmax_turned, it.i + 1)
                c = Chain(dve, hq, it.i, HQ)
                if it.reused():
                    dve.wait_ge(dg2_ready, it.i - 1)
                c.add(dve.tensor_reduce(hmax[p][:], aux[:, 0:S].rearrange("p (t q) -> p t q", t=TL), AX.X, ALU.max))
                c.wait()
                c.add(dve.tensor_scalar(hmax[p][:], hmax[p][:], 1e-5, None, ALU.max))
                c.wait()
                c.add(dve.reciprocal(hscale[p][:], hmax[p][:]))
                dve.tensor_scalar(hinv[p][:], hmax[p][:], back[:, 1:2], None, ALU.mult)
                c.wait()
                c.add(dve.tensor_scalar(hscale[p][:], hscale[p][:], 127.0, None, ALU.mult))

            def round_hidden(it):
                dve.wait_ge(multiplied, it.i + 1)
                dve.tensor_scalar(y[it.at][:], y[it.at][:], MAGIC, MAGIC + 127.0, ALU.add, ALU.min).then_inc(scaled, 1)

            def y_out(it):
                dve.wait_ge(y_done, it.i + 1)
                dve.wait_ge(r_in[it.p], 16 * (it.h + 1))
                if it.reused():
                    dve.wait_ge(stored[it.p], 16 * it.h)
                for t in range(TL):
                    last = dve.scalar_tensor_tensor(xo[it.p][:, t, :], y_ps[:, t, :], hinv[it.p][:, t:t + 1],
                                                    xres[it.p][:, t, :], ALU.mult, ALU.add)
                last.then_inc(y_ready, 1)

            pipeline(dve, B, DEPTH, [
                (4, h_out(0)), (5, hidden_max), (4, h_out(1)), (6, round_hidden), (7, y_out), (5, hidden_scale), (1, norm_stats),
                (4, h_out(2)), (4, h_out(3)), (2, quantise)], unroll=4, history=4)

        @block.scalar
        def _(act):
            act.wait_ge(weights, 32)

            def turn_out(it):
                act.wait_ge(turned, it.i + 1)
                if it.reused():
                    act.wait_ge(h_done, 4 * it.i - 4)
                act.copy(qxT[it.p][:], qt_ps[:].rearrange("p (k s) -> p k s", k=KD)).then_inc(turn_ready, 1)

            def row_out(out, done, ready, used, per):
                def step(it):
                    act.wait_ge(done, it.i + 1)
                    if it.reused():
                        act.wait_ge(used, per * (it.i - 1))
                    act.copy(out[it.p][:], aux[:, 0:S]).then_inc(ready, 1)
                return step

            def silu(m):
                def step(it):
                    act.wait_ge(c_done, 4 * it.i + m + 1)
                    if m == 0 and it.reused(4):
                        act.wait_ge(qh_ready, it.i - 3)
                    for c in range(2 * m, 2 * m + 2):
                        act.activation(y[it.at][:, c, :], c_ps[m % 2][:, c % 2, :], ACT.Silu, bias=cbias[:, c:c + 1]).then_inc(silu_ready, 1)
                return step

            def quantised(it):
                act.wait_ge(scaled, it.i + 1)
                if it.reused():
                    act.wait_ge(y_done, it.i - 1)
                act.activation(qh[it.p][:], y[it.at][:], ACT.Copy, bias=-MAGIC).then_inc(qh_ready, 1)

            pipeline(act, B, DEPTH, [
                (4, silu(0)), (5, row_out(row2, row2_done, row2_ready, multiplied, 1)), (4, silu(1)), (3, turn_out),
                (4, silu(2)), (6, quantised), (3, row_out(row, row_done, row_ready, h_ready, 4)), (4, silu(3))], unroll=4, history=4)

        @block.tensor
        def _(pe):
            for m in two:
                pe.wait_ge(sums, m + 1)
                pe.matmul(aux[:, 0:1], const["ones"][:], wsum[:, m:m + 1], start=True, stop=True).then_inc(w_all, 1)
            pe.wait_ge(w_all, 8)
            pe.wait_ge(consts, 4 + KH * 3 + 4)

            def turn(it):
                pe.wait_ge(quant, QN * (it.i + 1))
                if it.reused(1):
                    pe.wait_ge(turn_ready, it.i)
                for t in range(TL):
                    for k in range(KD):
                        last = pe.transpose(qt_ps[:, k * S + t * P:k * S + (t + 1) * P], qx[it.p][:, t, k * P:(k + 1) * P],
                                            const["identb"][:])
                last.then_inc(turned, 1)

            def make_row(diagonal, ready, done):
                def step(it):
                    pe.wait_ge(ready, it.i + 1)
                    if done is row_done:
                        if it.followed(-2) and it.reused(2):
                            pe.wait_ge(row2_ready, it.i - 1)
                        elif it.reused(1):
                            pe.wait_ge(row_ready, it.i)
                    for t in range(TL):
                        last = pe.matmul(aux[:, t * P:(t + 1) * P], const["ones"][:], diagonal[it.p][:, t, :], start=True, stop=True)
                    last.then_inc(done, 1)
                return step

            def up(m):
                def step(it):
                    if m == 0:
                        pe.wait_ge(turn_ready, it.i + 1)
                    if it.reused(1) or m >= 2:
                        pe.wait_ge(h_ready, 4 * it.i + m - 1)
                    for c in range(2):
                        for k in range(KD):
                            f = (2 * m + c) * P
                            last = pe.matmul(h_ps[m % 2][:, c, :], w1q[:, k, f:f + P], qxT[it.p][:, k, :], start=k == 0, stop=k == KD - 1)
                    last.then_inc(h_done, 1)
                return step

            def conv(m):
                def step(it):
                    pe.wait_ge(h_ready, 4 * it.i + m + 1)
                    if it.reused(1) or m >= 2:
                        pe.wait_ge(silu_ready, 2 * (4 * it.i + m - 1))
                    for c in range(2):
                        for j in range(3):
                            last = pe.matmul(c_ps[m % 2][:, c, :], diag[:, 2 * m + c, j, :], hs[it.p][:, 2 * m + c, j:j + S],
                                             start=j == 0, stop=j == 2)
                    last.then_inc(c_done, 1)
                return step

            def turn_max(it):
                pe.wait_ge(pmax_ready, it.i + 1)
                if it.followed(2):
                    pe.wait_ge(row_ready, it.i + 2)
                else:
                    pe.wait_ge(row2_ready, it.i)
                    pe.wait_ge(row_ready, B)
                for t in range(TL):
                    last = pe.transpose(aux[:, t * P:(t + 1) * P], pmax[it.p][:, t * P:(t + 1) * P], const["ident"][:])
                last.then_inc(pmax_turned, 1)

            def down(it):
                pe.wait_ge(qh_ready, it.i + 1)
                if it.reused(1):
                    pe.wait_ge(y_ready, it.i)
                for t in range(TL):
                    for k in range(KH):
                        last = pe.matmul(y_ps[:, t, :], qh[it.p][:, k, t * P:(t + 1) * P], w2q[:, k, :], start=k == 0, stop=k == KH - 1)
                last.then_inc(y_done, 1)

            pipeline(pe, B, DEPTH, [
                (4, up(0)), (7, down), (4, up(1)), (4, conv(0)), (5, turn_max), (4, conv(1)), (4, up(2)), (3, turn), (4, up(3)),
                (5, make_row(dg2, dg2_ready, row2_done)), (4, conv(2)), (4, conv(3)), (3, make_row(dg, dg_ready, row_done))], unroll=4, history=4)
    st.end()


def normed_attention(nc, const, src, dst, ctx, w):
    st = Stage(nc, "a1", [const["apart"]])
    two = range(2)
    wq, wk, wv, wo = (st.sb(n, s) for n, s in (("wq", [P, KD, D]), ("wk", [CP, 2, D]), ("wv", [CP, 2, D]), ("wo", [P, KD, D])))
    xb, xres, xo, xn = ([st.sb(f"{n}{p}", [P, TL, D]) for p in two] for n in ("xb", "xres", "xo", "xn"))
    cb = [st.sb(f"cb{p}", [CP, 2, SK]) for p in two]
    stt, mv = ([st.sb(f"{n}{p}", [P, TL, k]) for p in two] for n, k in (("st", 6), ("mv", 2)))
    rs = [st.sb(f"rs{p}", [P, TL]) for p in two]
    xnT, qT, oT = ([st.sb(f"{n}{p}", [P, KD, S]) for p in two] for n in ("xnT", "qT", "oT"))
    kT = [st.sb(f"kT{p}", [P, KD, SK]) for p in two]
    v = [st.sb(f"v{p}", [SK, D]) for p in two]
    sst = [st.sb(f"sst{p}", [P, 6]) for p in two]
    mom, tot = ([st.sb(f"{n}{p}", [P, 2]) for p in two] for n in ("mom", "tot"))
    root, var = ([st.sb(f"{n}{p}", [P, 1]) for p in two] for n in ("root", "var"))
    mx, shift, sums, rec = ([st.sb(f"{n}{p}", [P, TL]) for p in two] for n in ("mx", "shift", "sums", "rec"))
    pr = [st.sb(f"pr{p}", [P, TL, SK]) for p in two]
    prT = [st.sb(f"prT{p}", [SK, TL, P]) for p in two]
    t_ps, q_ps, kv_ps, s_ps, m_ps, p_ps, o_ps, y_ps = (st.ps(n, [P, 512]) for n in ("t", "q", "kv", "s", "m", "p", "o", "y"))

    weights = st.sem("weights")
    x_in, c_in, r_in, stored = ([st.sem(f"{n}{p}") for p in two] for n in ("x_in", "c_in", "r_in", "stored"))
    (stats, roots, xn_ready, x_turned, xT_ready, q_done, q_ready, kv_done, k_ready, v_ready, s_done, moments, m_done, spread,
     root_ready, exp_ready, rec_ready, p_turned, pT_ready, o_done, oT_ready, y_done, y_ready) = (st.sem(n) for n in (
         "stats", "roots", "xn_ready", "x_turned", "xT_ready", "q_done", "q_ready", "kv_done", "k_ready", "v_ready", "s_done", "moments",
         "m_done", "spread", "root_ready", "exp_ready", "rec_ready", "p_turned", "pT_ready", "o_done", "oT_ready", "y_done", "y_ready"))
    MOM, SPR = 4, 5
    DEPTH = 9
    src_v = src.rearrange("b (t p) d -> b p t d", p=P)
    dst_v = dst.rearrange("b (t p) d -> b p t d", p=P)

    with nc.Block() as block:
        @block.sync
        def _(sp):
            for a, n in ((wq, "Wq"), (wk, "Wk"), (wv, "Wv"), (wo, "Wo")):
                sp.dma_start(a[:], w[n]).then_inc(weights, 16)

            def load(it):
                if it.reused():
                    sp.wait_ge(xn_ready, it.i - 1)
                sp.dma_start(xb[it.p][:], src_v[it.i]).then_inc(x_in[it.p], 16)

            def load_context(it):
                if it.reused():
                    sp.wait_ge(kv_done, it.i - 1)
                sp.dma_start(cb[it.p][:], ctx[it.i]).then_inc(c_in[it.p], 16)

            def load_residual(it):
                if it.reused():
                    sp.wait_ge(y_ready, it.i - 1)
                sp.dma_start(xres[it.p][:], src_v[it.i]).then_inc(r_in[it.p], 16)

            def store(it):
                sp.wait_ge(y_ready, it.i + 1)
                sp.dma_start(dst_v[it.i], xo[it.p][:]).then_inc(stored[it.p], 16)

            pipeline(sp, B, DEPTH, [(9, store), (2, load_context), (6, load_residual), (0, load)])
            for p in two:
                sp.wait_ge(stored[p], 16 * (B // 2))

        @block.gpsimd
        def _(pool):
            def roots_of(it):
                pool.wait_ge(stats, 4 * it.i + 4)
                inverse_root(pool, Chain(pool, roots, it.i, 2), mv[it.p][:, :, 1], rs[it.p][:], const)

            def score_root(it):
                pool.wait_ge(spread, SPR * it.i + 3)
                inverse_root(pool, Chain(pool, root_ready, it.i, 2), var[it.p][:], root[it.p][:], const)

            pipeline(pool, B, DEPTH, [(5, score_root), (1, roots_of)])

        @block.vector
        def _(dve):
            def norm_stats(it):
                dve.wait_ge(x_in[it.p], 16 * (it.h + 1))
                layer_norm_stats(dve, Chain(dve, stats, it.i, 4), xb[it.p], stt[it.p], mv[it.p], const)

            def norm(it):
                dve.wait_ge(roots, 2 * it.i + 2)
                if it.reused():
                    dve.wait_ge(x_turned, it.i - 1)
                normalise(dve, xb[it.p], mv[it.p], rs[it.p], xn[it.p])[-1].then_inc(xn_ready, 1)

            def score_moments(it):
                p = it.p
                dve.wait_ge(s_done, it.i + 1)
                c = Chain(dve, moments, it.i, MOM)
                if it.reused():
                    dve.wait_ge(m_done, it.i - 1)
                c.add(dve.bn_stats(sst[p][:], s_ps[:, 0:TL * SK]))
                c.wait()
                apart(dve, const)
                c.add(dve.bn_aggr(mom[p][:], sst[p][:]))
                dve.tensor_reduce(mx[p][:], s_ps[:, 0:TL * SK].rearrange("p (t k) -> p t k", k=SK), AX.X, ALU.max)
                c.wait()
                c.add(dve.tensor_tensor(tot[p][:, 0:1], mom[p][:, 0:1], mom[p][:, 0:1], ALU.mult))
                c.wait()
                c.add(dve.tensor_tensor(mom[p][:, 1:2], mom[p][:, 1:2], tot[p][:, 0:1], ALU.add))

            def score_spread(it):
                p = it.p
                dve.wait_ge(m_done, it.i + 1)
                c = Chain(dve, spread, it.i, SPR)
                c.add(dve.tensor_scalar(tot[p][:], m_ps[:, 0:2], 1.0 / P, None, ALU.mult))
                c.wait()
                c.add(dve.tensor_tensor(var[p][:], tot[p][:, 0:1], tot[p][:, 0:1], ALU.mult))
                c.wait()
                c.add(dve.tensor_tensor(var[p][:], tot[p][:, 1:2], var[p][:], ALU.subtract))
                dve.wait_ge(root_ready, 2 * it.i + 2)
                if it.reused():
                    dve.wait_ge(exp_ready, 2 * it.i - 2)
                c.add(dve.tensor_scalar(shift[p][:], mx[p][:], root[p][:], -1.0, ALU.mult, ALU.mult))
                c.add(dve.tensor_copy(var[p][:], root[p][:]))

            def reciprocal(it):
                dve.wait_ge(exp_ready, 2 * it.i + 2)
                if it.reused():
                    dve.wait_ge(y_ready, it.i - 1)
                dve.reciprocal(rec[it.p][:], sums[it.p][:]).then_inc(rec_ready, 1)

            def y_out(it):
                dve.wait_ge(y_done, it.i + 1)
                dve.wait_ge(r_in[it.p], 16 * (it.h + 1))
                dve.wait_ge(rec_ready, it.i + 1)
                if it.reused():
                    dve.wait_ge(stored[it.p], 16 * it.h)
                for t in range(TL):
                    last = dve.scalar_tensor_tensor(xo[it.p][:, t, :], y_ps[:, t * D:(t + 1) * D], rec[it.p][:, t:t + 1],
                                                    xres[it.p][:, t, :], ALU.mult, ALU.add)
                last.then_inc(y_ready, 1)

            pipeline(dve, B, DEPTH, [(8, y_out), (6, reciprocal), (5, score_moments), (2, norm), (5, score_spread), (1, norm_stats)])

        @block.scalar
        def _(act):
            def leave(out, bank, done, ready, used, per=1):
                def step(it):
                    act.wait_ge(done, it.i + 1)
                    if it.reused():
                        act.wait_ge(used, per * (it.i - 1))
                    act.copy(out[it.p][:], bank).then_inc(ready, 1)
                return step

            def exps(it):
                p = it.p
                act.wait_ge(spread, SPR * (it.i + 1))
                if it.reused():
                    act.wait_ge(p_turned, it.i - 1)
                    act.wait_ge(rec_ready, it.i - 1)
                for t in range(TL):
                    act.activation(pr[p][:, t, :], s_ps[:, t * SK:(t + 1) * SK], ACT.Exp, bias=shift[p][:, t:t + 1],
                                   scale=root[p][:, 0:1], accum_out=sums[p][:, t:t + 1]).then_inc(exp_ready, 1)

            chunks = lambda bank: bank[:].rearrange("p (k s) -> p k s", k=KD)
            pipeline(act, B, DEPTH, [
                (4, leave(kT, kv_ps[:, 0:KD * SK].rearrange("p (k s) -> p k s", k=KD), kv_done, k_ready, s_done)),
                (7, leave(oT, chunks(o_ps), o_done, oT_ready, y_done)),
                (3, leave(xnT, chunks(t_ps), x_turned, xT_ready, q_done)),
                (6, leave(prT, p_ps[0:SK, 0:TL * P].rearrange("p (t q) -> p t q", t=TL), p_turned, pT_ready, o_done)),
                (4, leave(qT, chunks(q_ps), q_done, q_ready, s_done)), (5, exps),
                (4, leave(v, kv_ps[0:SK, 256:512], kv_done, v_ready, o_done))])

        @block.tensor
        def _(pe):
            pe.wait_ge(weights, 64)

            def turn_x(it):
                pe.wait_ge(xn_ready, it.i + 1)
                if it.reused(1):
                    pe.wait_ge(xT_ready, it.i)
                for t in range(TL):
                    for k in range(KD):
                        last = pe.transpose(t_ps[:, k * S + t * P:k * S + (t + 1) * P], xn[it.p][:, t, k * P:(k + 1) * P],
                                            const["ident"][:])
                last.then_inc(x_turned, 1)

            def project_q(it):
                pe.wait_ge(xT_ready, it.i + 1)
                if it.reused(1):
                    pe.wait_ge(q_ready, it.i)
                for m in range(KD):
                    for k in range(KD):
                        last = pe.matmul(q_ps[:, m * S:(m + 1) * S], wq[:, k, m * P:(m + 1) * P], xnT[it.p][:, k, :],
                                         start=k == 0, stop=k == KD - 1)
                last.then_inc(q_done, 1)

            def project_kv(it):
                pe.wait_ge(c_in[it.p], 16 * (it.h + 1))
                if it.reused(1):
                    pe.wait_ge(k_ready, it.i)
                    pe.wait_ge(v_ready, it.i)
                for m in range(KD):
                    for k in range(2):
                        pe.matmul(kv_ps[:, m * SK:(m + 1) * SK], wk[:, k, m * P:(m + 1) * P], cb[it.p][:, k, :],
                                  start=k == 0, stop=k == 1)
                for k in range(2):
                    last = pe.matmul(kv_ps[0:SK, 256:512], cb[it.p][:, k, :], wv[:, k, :], start=k == 0, stop=k == 1)
                last.then_inc(kv_done, 1)

            def scores(it):
                pe.wait_ge(q_ready, it.i + 1)
                pe.wait_ge(k_ready, it.i + 1)
                if it.reused(1):
                    pe.wait_ge(exp_ready, 2 * it.i)
                for t in range(TL):
                    for k in range(KD):
                        last = pe.matmul(s_ps[:, t * SK:(t + 1) * SK], qT[it.p][:, k, t * P:(t + 1) * P], kT[it.p][:, k, :],
                                         start=k == 0, stop=k == KD - 1)
                last.then_inc(s_done, 1)

            def sum_moments(it):
                pe.wait_ge(moments, MOM * (it.i + 1))
                if it.reused(1):
                    pe.wait_ge(spread, SPR * (it.i - 1) + 1)
                pe.matmul(m_ps[:, 0:2], const["ones"][:], mom[it.p][:], start=True, stop=True).then_inc(m_done, 1)

            def turn_p(it):
                pe.wait_ge(exp_ready, 2 * it.i + 2)
                if it.reused(1):
                    pe.wait_ge(pT_ready, it.i)
                for t in range(TL):
                    last = pe.transpose(p_ps[0:SK, t * P:(t + 1) * P], pr[it.p][:, t, :], const["ident"][:])
                last.then_inc(p_turned, 1)

            def attend(it):
                pe.wait_ge(pT_ready, it.i + 1)
                pe.wait_ge(v_ready, it.i + 1)
                if it.reused(1):
                    pe.wait_ge(oT_ready, it.i)
                for m in range(KD):
                    last = pe.matmul(o_ps[:, m * S:(m + 1) * S], v[it.p][:, m * P:(m + 1) * P],
                                     prT[it.p][:].rearrange("p t q -> p (t q)"), start=True, stop=True)
                last.then_inc(o_done, 1)

            def project_o(it):
                pe.wait_ge(oT_ready, it.i + 1)
                if it.reused(1):
                    pe.wait_ge(y_ready, it.i)
                for t in range(TL):
                    for k in range(KD):
                        last = pe.matmul(y_ps[:, t * D:(t + 1) * D], oT[it.p][:, k, t * P:(t + 1) * P], wo[:, k, :],
                                         start=k == 0, stop=k == KD - 1)
                last.then_inc(y_done, 1)

            pipeline(pe, B, DEPTH, [
                (8, project_o), (3, turn_x), (7, attend), (5, scores), (4, project_kv), (5, sum_moments), (6, turn_p),
                (4, project_q)])
    st.end()


def route(nc, const, src, xn_all, table, meta_at, meta_w, w):
    st = Stage(nc, "r", [const["apart"]])
    two = range(2)
    rw1, rb1, rw2, rb2 = (st.sb(n, s) for n, s in (("rw1", [P, KD, H1]), ("rb1", [P, KH]), ("rw2", [P, KH, NE]), ("rb2", [P, NE])))
    xb, xn = ([st.sb(f"{n}{p}", [P, TL, D]) for p in two] for n in ("xb", "xn"))
    stt, mv = ([st.sb(f"{n}{p}", [P, TL, k]) for p in two] for n, k in (("st", 6), ("mv", 2)))
    rs = [st.sb(f"rs{p}", [P, TL]) for p in two]
    xnT = [st.sb(f"xnT{p}", [P, KD, S]) for p in two]
    hT = [st.sb(f"hT{p}", [P, KH, S]) for p in two]
    lg, best = ([st.sb(f"{n}{p}", [P, TL, NE]) for p in two] for n in ("lg", "best"))
    at = [st.sb(f"at{p}", [P, TL, NE], U32) for p in two]
    atf, prob, keep, place, wgt = ([st.sb(f"{n}{p}", [P, TL, 2]) for p in two] for n in ("atf", "prob", "keep", "place", "wgt"))
    gap, ex = ([st.sb(f"{n}{p}", [P, TL]) for p in two] for n in ("gap", "ex"))
    hot = [st.sb(f"hot{p}", [P, TL, 2, NE]) for p in two]
    spot = [st.sb(f"spot{p}", [P, TL, 2, NE]) for p in two]
    sel, count = ([st.sb(f"{n}{p}", s) for p in two] for n, s in (("sel", [P, TL, NE]), ("count", [P, NE])))
    slot = [st.sb(f"slot{p}", [P, TL, 2], U32) for p in two]
    read_at = [st.sb(f"read_at{p}", [P, TL, 2], U32) for p in two]
    tok = [st.sb(f"tok{p}", [P, TL], I32) for p in two]
    zeros, none = st.sb("zeros", [P, D]), st.sb("none", [P, NE * CAP // P], U32)
    t_ps, l_ps, n_ps = (st.ps(n, [P, 512]) for n in ("t", "l", "n"))
    h_ps = [st.ps(f"h{p}", [P, 2, S]) for p in two]

    weights, filled, emptied = (st.sem(n) for n in ("weights", "filled", "emptied"))
    x_in, xn_out, meta_out = ([st.sem(f"{n}{p}") for p in two] for n in ("x_in", "xn_out", "meta_out"))
    scattered = const["rows_placed"]
    (stats, roots, xn_ready, x_turned, xT_ready, h_done, h_ready, l_done, top, exp_ready, chosen, n_done, placed, tok_ready) = (
        st.sem(n) for n in ("stats", "roots", "xn_ready", "x_turned", "xT_ready", "h_done", "h_ready", "l_done", "top", "exp_ready",
                            "chosen", "n_done", "placed", "tok_ready"))
    kept = st.sem("kept")
    TOP, CHO, PLC, TOK = 6, 8, 10, 1
    DEPTH = 8
    src_v = src.rearrange("b (t p) d -> b p t d", p=P)
    xn_v = xn_all[0:B * S].rearrange("(b t p) d -> b p t d", p=P, t=TL)

    with nc.Block() as block:
        @block.sync
        def _(sp):
            for a, n in ((rw1, "rw1"), (rb1, "rb1"), (rw2, "rw2")):
                sp.dma_start(a[:], w[n]).then_inc(weights, 16)
            sp.dma_start(rb2[:], w["rb2"].partition_broadcast(P)).then_inc(weights, 16)
            sp.wait_ge(filled, 2)
            sp.dma_start(xn_all[B * S:B * S + P], zeros[:]).then_inc(emptied, 16)
            sp.dma_start(table.rearrange("(p n) o -> p (n o)", p=P), none[:]).then_inc(emptied, 16)

            def load(it):
                if it.reused():
                    sp.wait_ge(xn_ready, it.i - 1)
                sp.dma_start(xb[it.p][:], src_v[it.i]).then_inc(x_in[it.p], 16)

            def store_xn(it):
                sp.wait_ge(xn_ready, it.i + 1)
                sp.dma_start(xn_v[it.i], xn[it.p][:]).then_inc(xn_out[it.p], 16)

            def store_meta(it):
                sp.wait_ge(placed, PLC * (it.i + 1))
                sp.dma_start(meta_at[it.i], read_at[it.p][:].rearrange("p t r -> p (t r)")).then_inc(meta_out[it.p], 16)
                sp.dma_start(meta_w[it.i], wgt[it.p][:].rearrange("p t r -> p (t r)")).then_inc(meta_out[it.p], 16)

            pipeline(sp, B, DEPTH, [(0, load), (3, store_xn), (8, store_meta)])
            for p in two:
                sp.wait_ge(xn_out[p], 16 * (B // 2))
                sp.wait_ge(meta_out[p], 32 * (B // 2))
                sp.wait_ge(scattered[p], 64 * (B // 2))

        @block.gpsimd
        def _(pool):
            pool.memset(zeros[:], 0.0).then_inc(filled, 1)
            pool.iota(none[:], [[0, NE * CAP // P]], base=B * S, channel_multiplier=0).then_inc(filled, 1)
            pool.iota(tok[1][:], [[P, TL]], base=-S, channel_multiplier=1).then_inc(filled, 1)
            pool.memset(count[0][:], 0.0).then_inc(filled, 1)
            pool.wait_ge(filled, 4)
            pool.wait_ge(emptied, 32)

            def roots_of(it):
                pool.wait_ge(stats, 4 * it.i + 4)
                inverse_root(pool, Chain(pool, roots, it.i, 2), mv[it.p][:, :, 1], rs[it.p][:], const)

            def scatter(it):
                p = it.p
                c = Chain(pool, tok_ready, it.i, TOK)
                if it.reused():
                    pool.wait_ge(scattered[p], 64 * it.h)
                c.add(pool.tensor_tensor(tok[p][:], tok[1 - p][:], const["batch"][:], ALU.add))
                c.wait()
                pool.wait_ge(placed, PLC * it.i + PLC - 1)
                apart(pool, const)
                for t in range(TL):
                    for r in range(2):
                        pool.indirect_dma_start(table[:, :], bass.IndirectOffsetOnAxis(ap=slot[p][:, t, r:r + 1], axis=0),
                                                tok[p][:, t:t + 1].bitcast(U32), None, bounds_check=NE * CAP - 1, oob_is_err=False).then_inc(scattered[p], 16)

            pipeline(pool, B, DEPTH, [(1, roots_of), (7, scatter)])

        @block.vector
        def _(dve):
            dve.wait_ge(weights, 64)
            dve.wait_ge(filled, 4)

            def norm_stats(it):
                dve.wait_ge(x_in[it.p], 16 * (it.h + 1))
                layer_norm_stats(dve, Chain(dve, stats, it.i, 4), xb[it.p], stt[it.p], mv[it.p], const)

            def norm(it):
                dve.wait_ge(roots, 2 * it.i + 2)
                if it.reused():
                    dve.wait_ge(x_turned, it.i - 1)
                    dve.wait_ge(xn_out[it.p], 16 * it.h)
                normalise(dve, xb[it.p], mv[it.p], rs[it.p], xn[it.p])[-1].then_inc(xn_ready, 1)

            def choose(it):
                p = it.p
                dve.wait_ge(l_done, it.i + 1)
                c = Chain(dve, top, it.i, TOP)
                c.add(dve.tensor_tensor(lg[p][:], l_ps[:, 0:TL * NE].rearrange("p (t e) -> p t e", e=NE),
                                        rb2[:].unsqueeze(1).to_broadcast([P, TL, NE]), ALU.add))
                c.wait()
                apart(dve, const)
                for t in range(TL):
                    c.add(dve.max(best[p][:, t, :], lg[p][:, t, :]))
                c.wait()
                apart(dve, const)
                for t in range(TL):
                    c.add(dve.max_index(at[p][:, t, :], best[p][:, t, :], lg[p][:, t, :]))
                c.add(dve.tensor_tensor(gap[p][:], best[p][:, :, 1], best[p][:, :, 0], ALU.subtract))

            def select(it):
                p = it.p
                c = Chain(dve, chosen, it.i, CHO)
                if it.reused():
                    dve.wait_ge(n_done, it.i - 1)
                dve.wait_ge(top, TOP * (it.i + 1))
                c.add(dve.tensor_copy(atf[p][:], at[p][:, :, 0:2]))
                c.wait()
                c.add(dve.tensor_tensor(hot[p][:], const["iota8"][:].unsqueeze(1).unsqueeze(1).to_broadcast([P, TL, 2, NE]),
                                        atf[p][:].unsqueeze(3).to_broadcast([P, TL, 2, NE]), ALU.is_equal))
                c.wait()
                c.add(dve.tensor_tensor(sel[p][:], hot[p][:, :, 0, :], hot[p][:, :, 1, :], ALU.add))
                c.wait()
                c.add(dve.tensor_tensor(count[1 - p][:], count[p][:], sel[p][:, 0, :], ALU.add))
                c.wait()
                c.add(dve.tensor_tensor(count[1 - p][:], count[1 - p][:], sel[p][:, 1, :], ALU.add))
                dve.wait_ge(exp_ready, it.i + 1)
                c.add(dve.tensor_scalar(prob[p][:, :, 0], ex[p][:], 1.0, None, ALU.add))
                c.wait()
                c.add(dve.reciprocal(prob[p][:, :, 0], prob[p][:, :, 0]))
                c.wait()
                c.add(dve.tensor_tensor(prob[p][:, :, 1], prob[p][:, :, 0], ex[p][:], ALU.mult))

            def place_choices(it):
                p = it.p
                dve.wait_ge(n_done, it.i + 1)
                dve.wait_ge(chosen, CHO * (it.i + 1))
                c = Chain(dve, placed, it.i, PLC)
                for t in range(TL):
                    c.add(dve.tensor_tensor(spot[p][:, t], hot[p][:, t], n_ps[:, t * NE:(t + 1) * NE].unsqueeze(1).to_broadcast([P, 2, NE]), ALU.mult))
                c.wait()
                c.add(dve.tensor_reduce(place[p][:], spot[p][:], AX.X, ALU.add))
                c.wait()
                c.add(dve.tensor_scalar(keep[p][:], place[p][:], float(CAP), None, ALU.is_ge))
                c.add(dve.tensor_scalar(place[p][:], place[p][:], float(CAP - 1), None, ALU.min))
                c.wait()
                c.add(dve.scalar_tensor_tensor(place[p][:], atf[p][:], float(CAP), place[p][:], ALU.mult, ALU.add))
                c.wait()
                if it.reused():
                    dve.wait_ge(meta_out[p], 32 * it.h)
                    dve.wait_ge(scattered[p], 64 * it.h)
                c.add(dve.tensor_copy(read_at[p][:], place[p][:]))
                c.add(dve.scalar_tensor_tensor(place[p][:], keep[p][:], float(2 * NE * CAP), place[p][:], ALU.mult, ALU.add))
                c.wait()
                c.add(dve.tensor_copy(slot[p][:], place[p][:]))
                dve.tensor_scalar(keep[p][:], keep[p][:], -1.0, 1.0, ALU.mult, ALU.add).then_inc(kept, 1)
                dve.wait_ge(kept, it.i + 1)
                c.add(dve.tensor_tensor(wgt[p][:], prob[p][:], keep[p][:], ALU.mult))

            pipeline(dve, B, DEPTH, [(7, place_choices), (5, choose), (1, norm_stats), (6, select), (2, norm)])

        @block.scalar
        def _(act):
            act.wait_ge(weights, 64)

            def xT_out(it):
                act.wait_ge(x_turned, it.i + 1)
                if it.reused():
                    act.wait_ge(h_done, 4 * it.i - 4)
                act.copy(xnT[it.p][:], t_ps[:].rearrange("p (k s) -> p k s", k=KD)).then_inc(xT_ready, 1)

            def relu(m):
                def step(it):
                    act.wait_ge(h_done, 4 * it.i + m + 1)
                    if m == 0 and it.reused():
                        act.wait_ge(l_done, it.i - 1)
                    for c in range(2):
                        act.activation(hT[it.p][:, 2 * m + c, :], h_ps[m % 2][:, c, :], ACT.Relu,
                                       bias=rb1[:, 2 * m + c:2 * m + c + 1]).then_inc(h_ready, 1)
                return step

            def exps(it):
                act.wait_ge(top, TOP * (it.i + 1))
                if it.reused():
                    act.wait_ge(chosen, CHO * (it.i - 1))
                act.activation(ex[it.p][:], gap[it.p][:], ACT.Exp).then_inc(exp_ready, 1)

            pipeline(act, B, DEPTH, [(4, relu(0)), (5, exps), (3, xT_out), (4, relu(1)), (4, relu(2)), (4, relu(3))])

        @block.tensor
        def _(pe):
            pe.wait_ge(weights, 64)
            pe.wait_ge(filled, 4)

            def turn_x(it):
                pe.wait_ge(xn_ready, it.i + 1)
                if it.reused(1):
                    pe.wait_ge(xT_ready, it.i)
                for t in range(TL):
                    for k in range(KD):
                        last = pe.transpose(t_ps[:, k * S + t * P:k * S + (t + 1) * P], xn[it.p][:, t, k * P:(k + 1) * P],
                                            const["ident"][:])
                last.then_inc(x_turned, 1)

            def up(m):
                def step(it):
                    if m == 0:
                        pe.wait_ge(xT_ready, it.i + 1)
                    if it.reused(1) or m >= 2:
                        pe.wait_ge(h_ready, 2 * (4 * it.i + m - 1))
                    for c in range(2):
                        for k in range(KD):
                            f = (2 * m + c) * P
                            last = pe.matmul(h_ps[m % 2][:, c, :], rw1[:, k, f:f + P], xnT[it.p][:, k, :], start=k == 0, stop=k == KD - 1)
                    last.then_inc(h_done, 1)
                return step

            def logits(it):
                pe.wait_ge(h_ready, KH * (it.i + 1))
                if it.reused(1):
                    pe.wait_ge(top, TOP * (it.i - 1) + 1)
                for t in range(TL):
                    for k in range(KH):
                        last = pe.matmul(l_ps[:, t * NE:(t + 1) * NE], hT[it.p][:, k, t * P:(t + 1) * P], rw2[:, k, :],
                                         start=k == 0, stop=k == KH - 1)
                last.then_inc(l_done, 1)

            def count_before(it):
                pe.wait_ge(chosen, CHO * it.i + 3)
                if it.reused(1):
                    pe.wait_ge(placed, PLC * (it.i - 1) + 2)
                p = it.p
                pe.matmul(n_ps[:, 0:NE], const["ones"][:], count[p][:], start=True, stop=False)
                pe.matmul(n_ps[:, 0:NE], const["tri"][:], sel[p][:, 0, :], start=False, stop=True)
                pe.matmul(n_ps[:, NE:2 * NE], const["ones"][:], count[p][:], start=True, stop=False)
                pe.matmul(n_ps[:, NE:2 * NE], const["ones"][:], sel[p][:, 0, :], start=False, stop=False)
                pe.matmul(n_ps[:, NE:2 * NE], const["tri"][:], sel[p][:, 1, :], start=False, stop=True).then_inc(n_done, 1)

            pipeline(pe, B, DEPTH, [(4, up(0)), (5, logits), (4, up(1)), (3, turn_x), (6, count_before), (4, up(2)), (4, up(3))])
    st.end()


def experts(nc, const, xn_all, table, eo, w):
    st = Stage(nc, "e", [const["apart"]])
    two = range(2)
    PER = CAP // S
    N = NE * PER
    w1 = [st.sb(f"w1{p}", [P, KD, H1]) for p in two]
    w2 = [st.sb(f"w2{p}", [P, KH, D]) for p in two]
    b1, b2 = st.sb("b1", [P, NE, KH]), st.sb("b2", [P, NE, D])
    idx = [st.sb(f"idx{p}", [P, TL], U32) for p in two]
    xg, yo = ([st.sb(f"{n}{p}", [P, TL, D]) for p in two] for n in ("xg", "yo"))
    xT = [st.sb(f"xT{p}", [P, KD, S]) for p in two]
    hT = [st.sb(f"hT{p}", [P, KH, S]) for p in two]
    t_ps, y_ps = st.ps("t", [P, 512]), [st.ps(f"y{p}", [P, 512]) for p in two]
    h_ps = [st.ps(f"h{p}", [P, 2, S]) for p in range(4)]
    biases = st.sem("biases")
    w1_in, w2_in, i_in, stored = ([st.sem(f"{n}{p}") for p in two] for n in ("w1_in", "w2_in", "i_in", "stored"))
    g_in = const["rows_taken"]
    x_turned, xT_ready, h_done, h_ready, y_done, y_ready = (st.sem(n) for n in ("x_turned", "xT_ready", "h_done", "h_ready", "y_done", "y_ready"))
    DEPTH, UNROLL = 6, 2 * PER
    table_v = table.rearrange("(n p t) o -> n p (t o)", p=P, t=TL)
    eo_v = eo.rearrange("(n p t) d -> n p t d", p=P, t=TL)
    sched = dict(unroll=UNROLL)

    def expert_of(it):
        return it.round * 2 + it.at // PER

    with nc.Block() as block:
        @block.sync
        def _(sp):
            sp.dma_start(b1[:], w["eb1"]).then_inc(biases, 16)
            sp.dma_start(b2[:].rearrange("p e d -> p (e d)"), w["eb2"].partition_broadcast(P)).then_inc(biases, 16)

            def load_index(it):
                if it.reused():
                    sp.wait_ge(g_in[it.p], 32 * it.h)
                sp.dma_start(idx[it.p][:], table_v[it.i]).then_inc(i_in[it.p], 16)

            def load_weights(it):
                if it.at % PER:
                    return
                e = it.at // PER
                expert = expert_of(it)
                if it.reused(2 * PER):
                    sp.wait_ge(h_done, 4 * (it.i - PER))
                    sp.wait_ge(y_done, it.i - PER)
                    apart(sp, const)
                sp.dma_start(w1[e][:], w["ew1"][expert]).then_inc(w1_in[e], 16)
                sp.dma_start(w2[e][:], w["ew2"][expert]).then_inc(w2_in[e], 16)

            def store(it):
                sp.wait_ge(y_ready, it.i + 1)
                sp.dma_start(eo_v[it.i], yo[it.p][:]).then_inc(stored[it.p], 16)

            pipeline(sp, N, DEPTH, [(0, load_index), (0, load_weights), (6, store)], **sched)
            for p in two:
                sp.wait_ge(stored[p], 16 * (N // 2))

        @block.gpsimd
        def _(pool):
            def gather(it):
                p = it.p
                pool.wait_ge(i_in[p], 16 * (it.h + 1))
                if it.reused():
                    pool.wait_ge(x_turned, it.i - 1)
                apart(pool, const)
                for t in range(TL):
                    pool.indirect_dma_start(xg[p][:, t, :], None, xn_all[:, :],
                                            bass.IndirectOffsetOnAxis(ap=idx[p][:, t:t + 1], axis=0),
                                            bounds_check=B * S + P - 1, oob_is_err=False).then_inc(g_in[p], 16)

            pipeline(pool, N, DEPTH, [(1, gather)], **sched)

        @block.vector
        def _(dve):
            dve.wait_ge(biases, 32)

            def xT_out(it):
                dve.wait_ge(x_turned, it.i + 1)
                if it.reused():
                    dve.wait_ge(h_done, 4 * it.i - 4)
                dve.tensor_copy(xT[it.p][:], t_ps[:].rearrange("p (k s) -> p k s", k=KD)).then_inc(xT_ready, 1)

            def y_out(it):
                dve.wait_ge(y_done, it.i + 1)
                if it.reused():
                    dve.wait_ge(stored[it.p], 16 * it.h)
                dve.tensor_tensor(yo[it.p][:], y_ps[it.p][:].rearrange("p (t d) -> p t d", t=TL),
                                  b2_of(it).to_broadcast([P, TL, D]), ALU.add).then_inc(y_ready, 1)

            def b2_of(it):
                return b2[:, expert_of(it):expert_of(it) + 1, :] if isinstance(it.i, int) else b2[:, bass.ds(expert_of(it), 1), :]

            pipeline(dve, N, DEPTH, [(5, y_out), (3, xT_out)], **sched)

        @block.scalar
        def _(act):
            act.wait_ge(biases, 32)

            def relu(m):
                def step(it):
                    act.wait_ge(h_done, 4 * it.i + m + 1)
                    if m == 0 and it.reused():
                        act.wait_ge(y_done, it.i - 1)
                    apart(act, const)
                    e = expert_of(it)
                    for c in range(2 * m, 2 * m + 2):
                        bias = b1[:, e, c:c + 1] if isinstance(it.i, int) else b1[:, bass.ds(e, 1), c:c + 1].rearrange("p a b -> p (a b)")
                        act.activation(hT[it.p][:, c, :], h_ps[m][:, c % 2, :], ACT.Relu, bias=bias).then_inc(h_ready, 1)
                return step

            pipeline(act, N, DEPTH, [(4, relu(0)), (4, relu(1)), (4, relu(2)), (4, relu(3))], **sched)

        @block.tensor
        def _(pe):
            def turn_x(it):
                pe.wait_ge(g_in[it.p], 32 * (it.h + 1))
                if it.reused(1):
                    pe.wait_ge(xT_ready, it.i)
                for t in range(TL):
                    for k in range(KD):
                        last = pe.transpose(t_ps[:, k * S + t * P:k * S + (t + 1) * P], xg[it.p][:, t, k * P:(k + 1) * P],
                                            const["ident"][:])
                last.then_inc(x_turned, 1)

            def up(m):
                def step(it):
                    e = it.at // PER
                    if m == 0:
                        pe.wait_ge(xT_ready, it.i + 1)
                        pe.wait_ge(w1_in[e], 16 * (it.round + 1))
                    if it.reused(1):
                        pe.wait_ge(h_ready, 2 * (4 * it.i + m - 3))
                    for c in range(2):
                        for k in range(KD):
                            f = (2 * m + c) * P
                            last = pe.matmul(h_ps[m][:, c, :], w1[e][:, k, f:f + P], xT[it.p][:, k, :], start=k == 0, stop=k == KD - 1)
                    last.then_inc(h_done, 1)
                return step

            def down(it):
                e = it.at // PER
                pe.wait_ge(h_ready, KH * (it.i + 1))
                pe.wait_ge(w2_in[e], 16 * (it.round + 1))
                if it.reused():
                    pe.wait_ge(y_ready, it.i - 1)
                for t in range(TL):
                    for k in range(KH):
                        last = pe.matmul(y_ps[it.p][:, t * D:(t + 1) * D], hT[it.p][:, k, t * P:(t + 1) * P], w2[e][:, k, :],
                                         start=k == 0, stop=k == KH - 1)
                last.then_inc(y_done, 1)

            pipeline(pe, N, DEPTH, [(4, up(0)), (4, up(1)), (3, turn_x), (4, up(2)), (4, up(3)), (5, down)], **sched)
    st.end()


def combine(nc, const, src, dst, eo, meta_at, meta_w):
    st = Stage(nc, "m", [const["apart"]])
    two = range(2)
    xb, xo, xs = ([st.sb(f"{n}{p}", [P, TL, D]) for p in two] for n in ("xb", "xo", "xs"))
    at = [st.sb(f"at{p}", [P, TL * 2], U32) for p in two]
    wgt = [st.sb(f"wgt{p}", [P, TL * 2]) for p in two]
    g = [st.sb(f"g{p}", [P, TL * 2, D]) for p in two]
    x_in, m_in, w_in, stored = ([st.sem(f"{n}{p}") for p in two] for n in ("x_in", "m_in", "w_in", "stored"))
    g_in = const["rows_back"]
    first, summed = st.sem("first"), st.sem("summed")
    DEPTH = 4
    src_v = src.rearrange("b (t p) d -> b p t d", p=P)
    dst_v = dst.rearrange("b (t p) d -> b p t d", p=P)

    with nc.Block() as block:
        @block.sync
        def _(sp):
            def load(it):
                if it.reused():
                    sp.wait_ge(summed, it.i - 1)
                sp.dma_start(at[it.p][:], meta_at[it.i]).then_inc(m_in[it.p], 16)
                sp.dma_start(wgt[it.p][:], meta_w[it.i]).then_inc(w_in[it.p], 16)
                sp.dma_start(xb[it.p][:], src_v[it.i]).then_inc(x_in[it.p], 16)

            def store(it):
                sp.wait_ge(summed, it.i + 1)
                sp.dma_start(dst_v[it.i], xo[it.p][:]).then_inc(stored[it.p], 16)

            pipeline(sp, B, DEPTH, [(3, store), (0, load)])
            for p in two:
                sp.wait_ge(stored[p], 16 * (B // 2))

        @block.gpsimd
        def _(pool):
            def gather(it):
                p = it.p
                pool.wait_ge(m_in[p], 16 * (it.h + 1))
                if it.reused():
                    pool.wait_ge(summed, it.i - 1)
                apart(pool, const)
                for j in range(2 * TL):
                    pool.indirect_dma_start(g[p][:, j, :], None, eo[:, :], bass.IndirectOffsetOnAxis(ap=at[p][:, j:j + 1], axis=0),
                                            bounds_check=NE * CAP - 1, oob_is_err=False).then_inc(g_in[p], 16)

            pipeline(pool, B, DEPTH, [(1, gather)])

        @block.vector
        def _(dve):
            def add(it):
                p = it.p
                dve.wait_ge(x_in[p], 16 * (it.h + 1))
                dve.wait_ge(w_in[p], 16 * (it.h + 1))
                dve.wait_ge(g_in[p], 64 * (it.h + 1))
                if it.reused():
                    dve.wait_ge(stored[p], 16 * it.h)
                for t in range(TL):
                    last = dve.scalar_tensor_tensor(xs[p][:, t, :], g[p][:, 2 * t, :], wgt[p][:, 2 * t:2 * t + 1], xb[p][:, t, :],
                                                    ALU.mult, ALU.add)
                last.then_inc(first, 1)
                dve.wait_ge(first, it.i + 1)
                for t in range(TL):
                    last = dve.scalar_tensor_tensor(xo[p][:, t, :], g[p][:, 2 * t + 1, :], wgt[p][:, 2 * t + 1:2 * t + 2], xs[p][:, t, :],
                                                    ALU.mult, ALU.add)
                last.then_inc(summed, 1)

            pipeline(dve, B, DEPTH, [(2, add)])
    st.end()


def routed_feed_forward(nc, const, src, dst, w):
    dram = lambda n, s, d: nc.dram_tensor(n, s, d, kind="Internal").ap()
    xn_all, eo = dram("moe_rows", (B * S + P, D), F32), dram("moe_out", (NE * CAP, D), F32)
    table = dram("moe_table", (NE * CAP, 1), U32)
    meta_at, meta_w = dram("moe_at", (B, P, TL * 2), U32), dram("moe_weight", (B, P, TL * 2), F32)
    route(nc, const, src, xn_all, table, meta_at, meta_w, w)
    experts(nc, const, xn_all, table, eo, w)
    combine(nc, const, src, dst, eo, meta_at, meta_w)


def adaptive_feed_forward(nc, const, src, dst, w):
    st = Stage(nc, "f2", [const["apart"]])
    two = range(2)
    NG = 4
    HE = 512
    KE = HE // P
    w1, w2, b1 = st.sb("w1", [P, NG, KD, HE]), st.sb("w2", [P, NG, KE, D]), st.sb("b1", [P, NG * KE])
    b2 = st.sb("b2", [NG, D])
    gw, gb = st.sb("gw", [P, KD, NG]), st.sb("gb", [P, NG])
    dw1, db1, dw2, db2 = st.sb("dw1", [P, KD, P]), st.sb("db1", [P, 1]), st.sb("dw2", [P, 1]), st.sb("db2", [P, 1])
    xb, xres, xo, xn = ([st.sb(f"{n}{p}", [P, TL, D]) for p in two] for n in ("xb", "xres", "xo", "xn"))
    stt, mv = ([st.sb(f"{n}{p}", [P, TL, k]) for p in two] for n, k in (("st", 6), ("mv", 2)))
    rs = [st.sb(f"rs{p}", [P, TL]) for p in two]
    xnT = [st.sb(f"xnT{p}", [P, KD, S]) for p in two]
    dT = [st.sb(f"dT{p}", [P, S]) for p in two]
    hT = [st.sb(f"hT{p}", [P, KE, S]) for p in two]
    wT = [st.sb(f"wT{p}", [NG, S]) for p in two]
    lg, best = ([st.sb(f"{n}{p}", [P, TL, 8]) for p in two] for n in ("lg", "best"))
    at = [st.sb(f"at{p}", [P, TL, 8], U32) for p in two]
    z, soft, ln = ([st.sb(f"{n}{p}", [P, TL]) for p in two] for n in ("z", "soft", "ln"))
    arg = [st.sb(f"arg{p}", [P, TL, NG + 1]) for p in two]
    ex = [st.sb(f"ex{p}", [P, TL, NG + 1]) for p in two]
    atf, first, wgt = ([st.sb(f"{n}{p}", [P, TL, NG]) for p in two] for n in ("atf", "first", "wgt"))
    hot = [st.sb(f"hot{p}", [P, TL, NG, NG]) for p in two]
    t_ps, d_ps, g_ps, b_ps = (st.ps(n, [P, 512]) for n in ("t", "d", "g", "b"))
    h_ps = [st.ps(f"h{p}", [P, 2, S]) for p in two]
    y_ps = [st.ps(f"y{p}", [P, 512]) for p in two]
    WT = 256

    weights, padded = st.sem("weights"), st.sem("padded")
    x_in, r_in, stored = ([st.sem(f"{n}{p}") for p in two] for n in ("x_in", "r_in", "stored"))
    (stats, roots, xn_ready, x_turned, xT_ready, d_done, d_ready, g_done, gate, exp_ready, ln_ready, w_turned, wT_ready, b_done,
     h_done, h_ready, y_done, summed) = (st.sem(n) for n in (
         "stats", "roots", "xn_ready", "x_turned", "xT_ready", "d_done", "d_ready", "g_done", "gate", "exp_ready", "ln_ready",
         "w_turned", "wT_ready", "b_done", "h_done", "h_ready", "y_done", "summed"))
    PRE = 8
    GATE = PRE + 14
    SUM = NG + 1
    PAIRS = NG * KE // 2
    DEPTH = 7
    src_v = src.rearrange("b (t p) d -> b p t d", p=P)
    dst_v = dst.rearrange("b (t p) d -> b p t d", p=P)

    with nc.Block() as block:
        @block.sync
        def _(sp):
            for a, n in ((w1, "ew1"), (w2, "ew2"), (b1, "eb1"), (b2, "eb2"), (gw, "gate_w"), (dw1, "dp_w1"), (db1, "dp_b1"), (dw2, "dp_w2")):
                sp.dma_start(a[:], w[n]).then_inc(weights, 16)
            sp.dma_start(gb[:], w["gate_b"].partition_broadcast(P)).then_inc(weights, 16)
            sp.dma_start(db2[:], w["dp_b2"].partition_broadcast(P)).then_inc(weights, 16)

            def load(it):
                if it.reused():
                    sp.wait_ge(xn_ready, it.i - 1)
                sp.dma_start(xb[it.p][:], src_v[it.i]).then_inc(x_in[it.p], 16)

            def load_residual(it):
                if it.reused():
                    sp.wait_ge(summed, SUM * (it.i - 2) + 1)
                sp.dma_start(xres[it.p][:], src_v[it.i]).then_inc(r_in[it.p], 16)

            def store(it):
                sp.wait_ge(summed, SUM * (it.i + 1))
                sp.dma_start(dst_v[it.i], xo[it.p][:]).then_inc(stored[it.p], 16)

            pipeline(sp, B, DEPTH, [(4, load_residual), (6, store), (0, load)])
            for p in two:
                sp.wait_ge(stored[p], 16 * (B // 2))

        @block.gpsimd
        def _(pool):
            for p in two:
                pool.memset(lg[p][:], -3e38).then_inc(padded, 1)

            def roots_of(it):
                pool.wait_ge(stats, 4 * it.i + 4)
                inverse_root(pool, Chain(pool, roots, it.i, 2), mv[it.p][:, :, 1], rs[it.p][:], const)

            pipeline(pool, B, DEPTH, [(1, roots_of)])

        @block.vector
        def _(dve):
            dve.wait_ge(weights, 160)
            dve.wait_ge(padded, 2)

            def norm_stats(it):
                dve.wait_ge(x_in[it.p], 16 * (it.h + 1))
                layer_norm_stats(dve, Chain(dve, stats, it.i, 4), xb[it.p], stt[it.p], mv[it.p], const)

            def norm(it):
                dve.wait_ge(roots, 2 * it.i + 2)
                if it.reused():
                    dve.wait_ge(x_turned, it.i - 1)
                normalise(dve, xb[it.p], mv[it.p], rs[it.p], xn[it.p])[-1].then_inc(xn_ready, 1)

            def gating(it):
                p = it.p
                four = lambda a: a.unsqueeze(2).to_broadcast([P, TL, NG])
                c = Chain(dve, gate, it.i, GATE)
                dve.wait_ge(g_done, it.i + 1)
                if it.reused():
                    dve.wait_ge(w_turned, it.i - 1)
                    dve.wait_ge(summed, SUM * (it.i - 1))
                g = g_ps[:, 0:TL * (NG + 1)].rearrange("p (t e) -> p t e", t=TL)
                c.add(dve.tensor_tensor(lg[p][:, :, 0:NG], g[:, :, 0:NG], gb[:].unsqueeze(1).to_broadcast([P, TL, NG]), ALU.add))
                c.add(dve.tensor_scalar(z[p][:], g[:, :, NG], db2[:, 0:1], None, ALU.add))
                c.wait()
                apart(dve, const)
                for t in range(TL):
                    c.add(dve.max(best[p][:, t, :], lg[p][:, t, :]))
                c.wait()
                apart(dve, const)
                for t in range(TL):
                    c.add(dve.max_index(at[p][:, t, :], best[p][:, t, :], lg[p][:, t, :]))
                c.add(dve.scalar_tensor_tensor(arg[p][:, :, NG], z[p][:], -1.0, z[p][:], ALU.mult, ALU.min))
                c.add(dve.tensor_tensor(arg[p][:, :, 0:NG], best[p][:, :, 0:NG], four(best[p][:, :, 0]), ALU.subtract))
                c.wait()
                c.add(dve.tensor_copy(atf[p][:], at[p][:, :, 0:NG]))
                c.wait()
                c.add(dve.tensor_tensor(hot[p][:], const["iota8"][:, 0:NG].unsqueeze(1).unsqueeze(3).to_broadcast([P, TL, NG, NG]),
                                        atf[p][:].unsqueeze(2).to_broadcast([P, TL, NG, NG]), ALU.is_equal))
                dve.wait_ge(ln_ready, it.i + 1)
                c.add(dve.scalar_tensor_tensor(soft[p][:], z[p][:], 0.0, ln[p][:], ALU.max, ALU.add))
                c.wait()
                c.add(dve.tensor_scalar(soft[p][:], soft[p][:], -0.5, 1.0 / 1.5, ALU.add, ALU.mult))
                c.wait()
                c.add(dve.tensor_scalar(soft[p][:], soft[p][:], 0.0, 1.0, ALU.max, ALU.min))
                c.wait()
                c.add(dve.tensor_scalar(soft[p][:], soft[p][:], 3.0, 1.0, ALU.mult, ALU.add))
                c.wait()
                c.add(dve.tensor_scalar(soft[p][:], soft[p][:], MAGIC, MAGIC, ALU.add, ALU.subtract))
                c.wait()
                c.add(dve.tensor_tensor(first[p][:], const["iota8"][:, 0:NG].unsqueeze(1).to_broadcast([P, TL, NG]),
                                        four(soft[p][:]), ALU.is_lt))
                c.wait()
                c.add(dve.tensor_tensor(first[p][:], first[p][:], ex[p][:, :, 0:NG], ALU.mult))
                c.wait()
                c.add(dve.tensor_reduce(soft[p][:], first[p][:], AX.X, ALU.add))
                c.wait()
                c.add(dve.reciprocal(soft[p][:], soft[p][:]))
                c.wait()
                c.add(dve.tensor_tensor(first[p][:], first[p][:], four(soft[p][:]), ALU.mult))
                c.wait()
                c.add(dve.tensor_tensor(hot[p][:], hot[p][:], first[p][:].unsqueeze(2).to_broadcast([P, TL, NG, NG]), ALU.mult))
                c.wait()
                c.add(dve.tensor_reduce(wgt[p][:], hot[p][:], AX.X, ALU.add))

            def wT_out(it):
                dve.wait_ge(w_turned, it.i + 1)
                if it.reused():
                    dve.wait_ge(b_done, it.i - 1)
                dve.tensor_copy(wT[it.p][:], g_ps[0:NG, WT:WT + S]).then_inc(wT_ready, 1)

            def begin_sum(it):
                p = it.p
                dve.wait_ge(b_done, it.i + 1)
                dve.wait_ge(r_in[p], 16 * (it.h + 1))
                if it.reused():
                    dve.wait_ge(stored[p], 16 * it.h)
                dve.tensor_tensor(xo[p][:], b_ps[:].rearrange("p (t d) -> p t d", t=TL), xres[p][:], ALU.add).then_inc(summed, 1)

            def add_expert(e):
                def step(it):
                    p = it.p
                    dve.wait_ge(summed, SUM * it.i + e + 1)
                    dve.wait_ge(y_done, NG * it.i + e + 1)
                    for t in range(TL):
                        last = dve.scalar_tensor_tensor(xo[p][:, t, :], y_ps[e % 2][:, t * D:(t + 1) * D], wgt[p][:, t, e:e + 1],
                                                        xo[p][:, t, :], ALU.mult, ALU.add)
                    last.then_inc(summed, 1)
                return step

            pipeline(dve, B, DEPTH, [
                (4, gating), (2, norm), (5, begin_sum), (5, add_expert(0)), (1, norm_stats), (5, add_expert(1)),
                (5, add_expert(2)), (4, wT_out), (5, add_expert(3))])

        @block.scalar
        def _(act):
            act.wait_ge(weights, 160)

            def xT_out(it):
                act.wait_ge(x_turned, it.i + 1)
                if it.reused():
                    act.wait_ge(h_done, PAIRS * (it.i - 1))
                act.copy(xnT[it.p][:], t_ps[:].rearrange("p (k s) -> p k s", k=KD)).then_inc(xT_ready, 1)

            def d_out(it):
                act.wait_ge(d_done, it.i + 1)
                if it.reused():
                    act.wait_ge(g_done, it.i - 1)
                act.activation(dT[it.p][:], d_ps[:, 0:S], ACT.Relu, bias=db1[:, 0:1]).then_inc(d_ready, 1)

            def exps(it):
                act.wait_ge(gate, GATE * it.i + PRE)
                if it.reused():
                    act.wait_ge(gate, GATE * (it.i - 1))
                act.activation(ex[it.p][:], arg[it.p][:], ACT.Exp).then_inc(exp_ready, 1)
                act.wait_ge(exp_ready, it.i + 1)
                act.activation(ln[it.p][:], ex[it.p][:, :, NG], ACT.Ln, bias=1.0).then_inc(ln_ready, 1)

            def relu(j):
                e, m = j // 2, j % 2

                def step(it):
                    act.wait_ge(h_done, PAIRS * it.i + j + 1)
                    if m == 0 and (e >= 2 or it.reused(1)):
                        act.wait_ge(y_done, NG * it.i + e - 1)
                    for c in range(2):
                        f = e * KE + 2 * m + c
                        act.activation(hT[e % 2][:, 2 * m + c, :], h_ps[j % 2][:, c, :], ACT.Relu, bias=b1[:, f:f + 1]).then_inc(h_ready, 1)
                return step

            pipeline(act, B, DEPTH, [
                (4, d_out), (5, relu(0)), (5, relu(1)), (5, relu(2)), (4, exps), (5, relu(3)), (5, relu(4)), (5, relu(5)),
                (5, relu(6)), (5, relu(7)), (3, xT_out)])

        @block.tensor
        def _(pe):
            pe.wait_ge(weights, 160)

            def turn_x(it):
                pe.wait_ge(xn_ready, it.i + 1)
                if it.reused(1):
                    pe.wait_ge(xT_ready, it.i)
                for t in range(TL):
                    for k in range(KD):
                        last = pe.transpose(t_ps[:, k * S + t * P:k * S + (t + 1) * P], xn[it.p][:, t, k * P:(k + 1) * P],
                                            const["ident"][:])
                last.then_inc(x_turned, 1)

            def difficulty(it):
                pe.wait_ge(xT_ready, it.i + 1)
                if it.reused(1):
                    pe.wait_ge(d_ready, it.i)
                for k in range(KD):
                    last = pe.matmul(d_ps[:, 0:S], dw1[:, k, :], xnT[it.p][:, k, :], start=k == 0, stop=k == KD - 1)
                last.then_inc(d_done, 1)

            def gates(it):
                pe.wait_ge(d_ready, it.i + 1)
                if it.reused(1):
                    pe.wait_ge(wT_ready, it.i)
                for t in range(TL):
                    at_e = t * (NG + 1)
                    for k in range(KD):
                        pe.matmul(g_ps[:, at_e:at_e + NG], xnT[it.p][:, k, t * P:(t + 1) * P], gw[:, k, :], start=k == 0, stop=k == KD - 1)
                    last = pe.matmul(g_ps[:, at_e + NG:at_e + NG + 1], dT[it.p][:, t * P:(t + 1) * P], dw2[:, 0:1], start=True, stop=True)
                last.then_inc(g_done, 1)

            def turn_weights(it):
                pe.wait_ge(gate, GATE * (it.i + 1))
                for t in range(TL):
                    last = pe.transpose(g_ps[0:NG, WT + t * P:WT + (t + 1) * P], wgt[it.p][:, t, :], const["ident"][:])
                last.then_inc(w_turned, 1)

            def bias(it):
                pe.wait_ge(wT_ready, it.i + 1)
                if it.reused(1):
                    pe.wait_ge(summed, SUM * (it.i - 1) + 1)
                for t in range(TL):
                    last = pe.matmul(b_ps[:, t * D:(t + 1) * D], wT[it.p][:, t * P:(t + 1) * P], b2[:], start=True, stop=True)
                last.then_inc(b_done, 1)

            def up(j):
                e, m = j // 2, j % 2

                def step(it):
                    if it.reused(1) or j >= 2:
                        pe.wait_ge(h_ready, 2 * (PAIRS * it.i + j - 1))
                    for c in range(2):
                        for k in range(KD):
                            f = (2 * m + c) * P
                            last = pe.matmul(h_ps[j % 2][:, c, :], w1[:, e, k, f:f + P], xnT[it.p][:, k, :], start=k == 0, stop=k == KD - 1)
                    last.then_inc(h_done, 1)
                return step

            def down(e):
                def step(it):
                    pe.wait_ge(h_ready, KE * (NG * it.i + e + 1))
                    if e >= 2:
                        pe.wait_ge(summed, SUM * it.i + e)
                    elif it.reused(1):
                        pe.wait_ge(summed, SUM * (it.i - 1) + NG + e)
                    for t in range(TL):
                        for k in range(KE):
                            last = pe.matmul(y_ps[e % 2][:, t * D:(t + 1) * D], hT[e % 2][:, k, t * P:(t + 1) * P], w2[:, e, k, :],
                                             start=k == 0, stop=k == KE - 1)
                    last.then_inc(y_done, 1)
                return step

            pipeline(pe, B, DEPTH, [
                (4, difficulty), (5, up(0)), (4, gates), (5, up(1)), (5, up(2)), (5, bias), (5, up(3)), (5, up(4)), (5, down(0)),
                (5, down(1)), (5, up(5)), (4, turn_weights), (5, up(6)), (5, up(7)), (3, turn_x), (5, down(2)), (5, down(3))])
    st.end()


DX = 256
NS = 64
LP = P
STEP = 16


def convolution_kernel(nc, const, kpad, w):
    st = Stage(nc, "k")
    NT = STEP
    are, aim, cre, cim, dt, a, r, skip = (st.sb(n, [P, DX]) for n in ("are", "aim", "cre", "cim", "dt", "a", "r", "skip"))
    t0, t1, t2, t3, t4, t5, x1, x2 = (st.sb(n, [P, DX]) for n in ("t0", "t1", "t2", "t3", "t4", "t5", "x1", "x2"))
    cols = st.sb("cols", [P, NT])
    ph = st.sb("ph", [P, 3])
    sgn = st.sb("sgn", [P, 1])
    f, g, e, u, v = (st.sb(n, [P, DX, NT]) for n in ("f", "g", "e", "u", "v"))
    kout = st.sb("kout", [NT, DX, NT])
    zero = st.sb("zero", [P, DX // P, LP])
    k_ps = [st.ps(f"k{p}", [P, 512]) for p in range(2)]
    loaded, made, chain, acts, done, left, stored = (st.sem(n) for n in ("loaded", "made", "chain", "acts", "done", "left", "stored"))
    TWO_PI = 6.283185
    PB = 512 // NT
    HALF = P // 2

    with nc.Block() as block:
        @block.sync
        def _(sp):
            for t, n in ((are, "A_re"), (aim, "A_im"), (cre, "C_re"), (cim, "C_im")):
                for half in range(2):
                    sp.dma_start(t[half * HALF:(half + 1) * HALF, :], w[n]).then_inc(loaded, 16)
            sp.dma_start(dt[:], w["log_dt"].partition_broadcast(P)).then_inc(loaded, 16)
            sp.dma_start(skip[0:1, :], w["D_skip"]).then_inc(loaded, 16)
            sp.wait_ge(made, 2)
            sp.dma_start(kpad[:, 0:LP].rearrange("(p c) l -> p c l", p=P), zero[:]).then_inc(stored, 16)
            sp.wait_ge(left, DX // PB + 1)
            sp.dma_start(kpad[:, LP:LP + S].rearrange("d (i j) -> i d j", j=NT), kout[:]).then_inc(stored, 16)
            sp.wait_ge(stored, 32)

        @block.gpsimd
        def _(pool):
            low, high = slice(0, HALF), slice(HALF, P)
            pool.iota(cols[:], [[1, NT]], base=0, channel_multiplier=0, allow_small_or_imprecise_dtypes=True).then_inc(made, 1)
            pool.wait_ge(made, 1)
            for n, (part, value) in enumerate(((zero[:], 0.0), (ph[:], 0.0), (sgn[low], -1.0), (sgn[high], 1.0), (ph[low, 0:1], 0.25),
                                               (ph[high, 1:2], 0.25), (ph[low, 2:3], 0.25), (ph[high, 2:3], 0.5))):
                pool.memset(part, value).then_inc(made, 1)
                pool.wait_ge(made, n + 2)

        @block.vector
        def _(dve):
            n = [0]

            def do(ins):
                ins.then_inc(chain, 1)
                n[0] += 1
                dve.wait_ge(chain, n[0])

            tt = lambda o, x, y, op: do(dve.tensor_tensor(o, x, y, op))
            dve.wait_ge(loaded, 160)
            dve.wait_ge(made, 9)
            dve.wait_ge(acts, 1)
            tt(a[:], are[:], dt[:], ALU.mult)
            tt(t0[:], aim[:], dt[:], ALU.mult)
            do(dve.tensor_scalar(t0[:], t0[:], 0.15915494309189535, None, ALU.mult))
            do(dve.tensor_scalar(t1[:], t0[:], MAGIC, MAGIC, ALU.add, ALU.subtract))
            tt(r[:], t0[:], t1[:], ALU.subtract)
            dve.wait_ge(acts, 4)
            do(dve.tensor_scalar(t0[:], t2[:], -1.0, 1.0, ALU.mult, ALU.add))
            do(dve.reciprocal(t0[:], t0[:]))
            do(dve.scalar_tensor_tensor(t0[:], t0[:], 2.0, t2[:], ALU.mult, ALU.mult))
            do(dve.scalar_tensor_tensor(t3[:], t3[:], 2.0, t3[:], ALU.mult, ALU.mult))
            do(dve.tensor_scalar(t1[:], t3[:], -1.0, 1.0, ALU.mult, ALU.add))
            tt(t1[:], t1[:], t0[:], ALU.mult)
            tt(t1[:], t1[:], t3[:], ALU.subtract)
            do(dve.scalar_tensor_tensor(t2[:], t0[:], 1.0, t4[:], ALU.add, ALU.mult))
            tt(t3[:], t1[:], are[:], ALU.mult)
            tt(t4[:], t2[:], aim[:], ALU.mult)
            tt(t3[:], t3[:], t4[:], ALU.add)
            tt(t4[:], t2[:], are[:], ALU.mult)
            tt(t5[:], t1[:], aim[:], ALU.mult)
            tt(t4[:], t4[:], t5[:], ALU.subtract)
            tt(t1[:], are[:], are[:], ALU.mult)
            tt(t2[:], aim[:], aim[:], ALU.mult)
            tt(t1[:], t1[:], t2[:], ALU.add)
            do(dve.reciprocal(t1[:], t1[:]))
            do(dve.scalar_tensor_tensor(t3[:], t3[:], 2.0, t1[:], ALU.mult, ALU.mult))
            do(dve.scalar_tensor_tensor(t4[:], t4[:], 2.0, t1[:], ALU.mult, ALU.mult))
            tt(x1[:], cre[:], t3[:], ALU.mult)
            tt(t5[:], cim[:], t4[:], ALU.mult)
            tt(x1[:], x1[:], t5[:], ALU.subtract)
            tt(x2[:], cre[:], t4[:], ALU.mult)
            tt(t5[:], cim[:], t3[:], ALU.mult)
            tt(x2[:], x2[:], t5[:], ALU.add)
            do(dve.tensor_scalar(x2[:], x2[:], sgn[:, 0:1], None, ALU.mult))
            wide = lambda q: q[:].unsqueeze(2).to_broadcast([P, DX, NT])
            row = cols[:].unsqueeze(1).to_broadcast([P, DX, NT])

            def angles(turns, phase):
                tt(f[:], wide(turns), row, ALU.mult)
                do(dve.tensor_scalar(f[:], f[:], ph[:, phase:phase + 1], None, ALU.add))
                do(dve.tensor_scalar(g[:], f[:], MAGIC, MAGIC, ALU.add, ALU.subtract))
                tt(f[:], f[:], g[:], ALU.subtract)

            angles(r, 2)
            marks = [n[0]]
            tt(g[:], wide(a), row, ALU.mult)
            marks.append(n[0])
            dve.wait_ge(acts, 6)
            tt(v[:], f[:], e[:], ALU.mult)
            do(dve.tensor_scalar(t0[:], r[:], float(STEP), None, ALU.mult))
            do(dve.tensor_scalar(t1[:], t0[:], MAGIC, MAGIC, ALU.add, ALU.subtract))
            tt(t0[:], t0[:], t1[:], ALU.subtract)
            angles(t0, 0)
            marks.append(n[0])
            dve.wait_ge(acts, 7)
            tt(u[:], f[:], wide(x1), ALU.mult)
            angles(t0, 1)
            marks.append(n[0])
            do(dve.tensor_scalar(t1[:], a[:], float(STEP), None, ALU.mult))
            tt(g[:], wide(t1), row, ALU.mult)
            marks.append(n[0])
            dve.wait_ge(acts, 9)
            tt(f[:], f[:], wide(x2), ALU.mult)
            tt(u[:], u[:], f[:], ALU.add)
            tt(u[:], u[:], e[:], ALU.mult)
            marks.append(n[0])
            assert marks == KERNEL_MARKS, marks

            for b in range(DX // PB):
                dve.wait_ge(done, b + 1)
                dve.tensor_copy(kout[:, b * PB:(b + 1) * PB, :], k_ps[b % 2][0:NT, :].rearrange("p (d j) -> p d j", j=NT)).then_inc(left, 1)
            dve.wait_ge(left, DX // PB)
            dve.tensor_tensor(kout[0:1, :, 0], kout[0:1, :, 0], skip[0:1, :], ALU.add).then_inc(left, 1)

        @block.scalar
        def _(act):
            act.wait_ge(loaded, 160)
            act.activation(dt[:], dt[:], ACT.Exp).then_inc(acts, 1)
            act.wait_ge(chain, 5)
            act.activation(t2[:], a[:], ACT.Tanh, scale=0.5).then_inc(acts, 1)
            act.activation(t3[:], r[:], ACT.Sin, scale=TWO_PI / 2).then_inc(acts, 1)
            act.activation(t4[:], r[:], ACT.Sin, scale=TWO_PI).then_inc(acts, 1)
            m = KERNEL_MARKS
            for mark, out, inp, func, scale in ((m[0], f, f, ACT.Sin, TWO_PI), (m[1], e, g, ACT.Exp, 1.0), (m[2], f, f, ACT.Sin, TWO_PI),
                                                (m[3], f, f, ACT.Sin, TWO_PI), (m[4], e, g, ACT.Exp, 1.0)):
                act.wait_ge(chain, mark)
                act.activation(out[:], inp[:], func, scale=scale).then_inc(acts, 1)

        @block.tensor
        def _(pe):
            pe.wait_ge(chain, KERNEL_MARKS[5])
            for b in range(DX // PB):
                if b >= 2:
                    pe.wait_ge(left, b - 1)
                for c in range(PB):
                    d = b * PB + c
                    last = pe.matmul(k_ps[b % 2][0:NT, c * NT:(c + 1) * NT], u[:, d, :], v[:, d, :], start=True, stop=True)
                last.then_inc(done, 1)
    st.end()


KERNEL_MARKS = [36, 37, 45, 50, 52, 55]


def sparse_attention(nc, const, src, xin, rows_text, c_all, ctx, w, masks):
    st = Stage(nc, "a3", [const["apart"]])
    two = range(2)
    NH, ROUNDS = 4, 4
    wq, wk, wv, wf = (st.sb(n, s) for n, s in (("wq", [P, KD, P]), ("wk", [CP, 2, P]), ("wv", [CP, 2, D]), ("wf", [P, KD, 2 * D])))
    bf, gate, gin, bin_ = st.sb("bf", [P, 2 * D]), st.sb("gate", [P, 1]), st.sb("gin", [P, D]), st.sb("bin", [P, D])
    xb, xn, xl = ([st.sb(f"{n}{p}", [P, TL, D]) for p in two] for n in ("xb", "xn", "xl"))
    xr = [st.sb(f"xr{p}", [P, TL, D]) for p in two]
    cb, cv = ([st.sb(f"{n}{p}", [CP, 2, SK]) for p in two] for n in ("cb", "cv"))
    stt, mv, st2, mv2 = ([st.sb(f"{n}{p}", [P, TL, k]) for p in two] for n, k in (("st", 6), ("mv", 2), ("st2", 6), ("mv2", 2)))
    rs, rs2 = ([st.sb(f"{n}{p}", [P, TL]) for p in two] for n in ("rs", "rs2"))
    xnT, cT = ([st.sb(f"{n}{p}", [P, KD, S]) for p in two] for n in ("xnT", "cT"))
    qT = [st.sb(f"qT{p}", [P, S]) for p in two]
    kT = [st.sb(f"kT{p}", [P, SK]) for p in two]
    kd = [st.sb(f"kd{p}", [P, NH, SK]) for p in two]
    v = [st.sb(f"v{p}", [SK, D]) for p in two]
    sc, left, ex, kept = ([st.sb(f"{n}{t}", [P, NH, SK]) for t in two] for n in ("sc", "left", "ex", "kept"))
    best = [st.sb(f"best{t}", [P, ROUNDS, NH, 8]) for t in two]
    wsum, wgt, nmax = ([st.sb(f"{n}{t}", [P, NH]) for t in two] for n in ("wsum", "wgt", "nmax"))
    dg = [st.sb(f"dg{t}", [P, NH, P]) for t in two]
    aT = [st.sb(f"aT{p}", [SK, S]) for p in two]
    film = [st.sb(f"film{t}", [P, 2 * D]) for t in two]
    km = [st.sb(f"km{p}", [P, SK], U8) for p in two]
    tm = [st.sb(f"tm{p}", [P, TL], U8) for p in two]
    kmf = [st.sb(f"kmf{p}", [P, SK]) for p in two]
    tmf = [st.sb(f"tmf{p}", [P, TL]) for p in two]
    t_ps, q_ps, k_ps, a_ps, c_ps, f_ps = (st.ps(n, [P, 512]) for n in ("t", "q", "k", "a", "c", "f"))
    s_ps = [st.ps(f"s{t}", [P, 512]) for t in two]

    weights, wready = st.sem("weights"), st.sem("wready")
    x_in, c_in, cv_in, m_in, t_in, r_in, xl_out, cT_out = ([st.sem(f"{n}{p}") for p in two] for n in ("x_in", "c_in", "cv_in", "m_in", "t_in", "r_in", "xl_out", "cT_out"))
    (stats, roots, stats2, roots2, xn_ready, xl_part, xl_ready, x_turned, xT_ready, q_done, q_ready, v_done, v_ready, k_done, k_ready, kd_ready,
     km_ready) = (st.sem(n) for n in (
         "stats", "roots", "stats2", "roots2", "xn_ready", "xl_part", "xl_ready", "x_turned", "xT_ready", "q_done", "q_ready", "v_done", "v_ready", "k_done",
         "k_ready", "kd_ready", "km_ready"))
    (s_done, pick, nmax_ready, exp_ready, weigh, dg_ready, a_done, aT_ready, c_done, cT_ready, f_done, film_ready, mixed, xin_ready) = (st.sem(n) for n in (
        "s_done", "pick", "nmax_ready", "exp_ready", "weigh", "dg_ready", "a_done", "aT_ready", "c_done", "cT_ready", "f_done", "film_ready",
        "mixed", "xin_ready"))
    summed = st.sem("summed")
    PICK = TL * (1 + ROUNDS * 2 * NH + 1)
    WEIGH = 3
    TAKEN = -3e38
    DEPTH = 10
    src_v = src.rearrange("b (t p) d -> b p t d", p=P)

    with nc.Block() as block:
        @block.sync
        def _(sp):
            for a, n in ((wq, "Wq"), (wk, "Wk"), (wv, "Wv"), (wf, "W_film_in")):
                sp.dma_start(a[:], w[n]).then_inc(weights, 16)
            for a, n in ((bf, "b_film_in"), (gate, "mod_gate"), (gin, "g_norm_in"), (bin_, "b_norm_in")):
                sp.dma_start(a[:], w[n].partition_broadcast(P)).then_inc(weights, 16)

            def load(it):
                if it.reused():
                    sp.wait_ge(xn_ready, it.i - 1)
                apart(sp, const)
                sp.dma_start(xb[it.p][:], src_v[it.i]).then_inc(x_in[it.p], 16)

            def load_context(it):
                if it.reused():
                    sp.wait_ge(q_done, it.i - 1)
                apart(sp, const)
                sp.dma_start(cb[it.p][:], ctx[it.i]).then_inc(c_in[it.p], 16)

            def load_context_again(it):
                if it.reused():
                    sp.wait_ge(v_done, it.i - 1)
                    apart(sp, const)
                sp.dma_start(cv[it.p][:], ctx[it.i]).then_inc(cv_in[it.p], 16)

            def load_masks(it):
                if it.reused():
                    sp.wait_ge(km_ready, it.i - 1)
                apart(sp, const)
                sp.dma_start(km[it.p][:], masks[1][it.i].partition_broadcast(P)).then_inc(m_in[it.p], 16)

            def load_text_mask(it):
                if it.reused():
                    sp.wait_ge(weigh, 2 * WEIGH * (it.i - 1))
                apart(sp, const)
                sp.dma_start(tm[it.p][:], masks[0][it.i]).then_inc(t_in[it.p], 16)

            def keep_rows(it):
                sp.wait_ge(xl_ready, it.i + 1)
                apart(sp, const)
                sp.dma_start(rows_text[it.i], xl[it.p][:]).then_inc(xl_out[it.p], 16)

            def load_rows(it):
                if it.reused():
                    sp.wait_ge(xin_ready, 2 * (it.i - 1))
                    apart(sp, const)
                sp.wait_ge(xl_out[it.p], 16 * (it.h + 1))
                apart(sp, const)
                sp.dma_start(xr[it.p][:], rows_text[it.i]).then_inc(r_in[it.p], 16)

            def store_c(it):
                sp.wait_ge(cT_ready, it.i + 1)
                apart(sp, const)
                sp.dma_start(c_all[it.i], cT[it.p][:]).then_inc(cT_out[it.p], 16)

            pipeline(sp, B, DEPTH, [(0, load), (2, load_context), (6, load_context_again), (3, load_masks), (6, load_text_mask), (4, keep_rows), (8, load_rows), (9, store_c)])
            for p in two:
                sp.wait_ge(cT_out[p], 16 * (B // 2))
                sp.wait_ge(xl_out[p], 16 * (B // 2))

        @block.gpsimd
        def _(pool):
            pool.wait_ge(wready, 2)

            def roots_of(it):
                pool.wait_ge(stats, 4 * it.i + 4)
                inverse_root(pool, Chain(pool, roots, it.i, 2), mv[it.p][:, :, 1], rs[it.p][:], const)

            def roots_again(it):
                pool.wait_ge(stats2, 4 * it.i + 4)
                inverse_root(pool, Chain(pool, roots2, it.i, 2), mv2[it.p][:, :, 1], rs2[it.p][:], const)

            def affine(it):
                pool.wait_ge(xl_part, 2 * it.i + 1)
                pool.tensor_tensor(xl[it.p][:], xl[it.p][:], gin[:].unsqueeze(1).to_broadcast([P, TL, D]), ALU.mult).then_inc(xl_part, 1)
                pool.wait_ge(xl_part, 2 * it.i + 2)
                pool.tensor_tensor(xl[it.p][:], xl[it.p][:], bin_[:].unsqueeze(1).to_broadcast([P, TL, D]), ALU.add).then_inc(xl_ready, 1)

            def spread_k(it):
                pool.wait_ge(k_ready, it.i + 1)
                if it.reused():
                    pool.wait_ge(s_done, 2 * it.i - 2)
                pool.tensor_tensor(kd[it.p][:], kT[it.p][:].unsqueeze(1).to_broadcast([P, NH, SK]),
                                   const["heads4"][:].unsqueeze(2).to_broadcast([P, NH, SK]), ALU.mult).then_inc(kd_ready, 1)

            def key_mask(it):
                pool.wait_ge(m_in[it.p], 16 * (it.h + 1))
                if it.reused():
                    pool.wait_ge(pick, PICK * (it.i - 2) + TL)
                apart(pool, const)
                pool.tensor_scalar(kmf[it.p][:], km[it.p][:], -LOW, LOW, ALU.mult, ALU.add).then_inc(km_ready, 1)

            def negate_max(t):
                def step(it):
                    pool.wait_ge(pick, PICK * it.i + TL + (t + 1) * NH)
                    apart(pool, const)
                    pool.tensor_scalar(nmax[t][:], best[t][:, 0, :, 0], -1.0, None, ALU.mult).then_inc(nmax_ready, 1)
                return step

            def diagonals(t):
                def step(it):
                    pool.wait_ge(weigh, WEIGH * (2 * it.i + t + 1))
                    if it.reused(1):
                        pool.wait_ge(a_done, 2 * it.i + t - 1)
                    pool.tensor_tensor(dg[t][:], const["ident"][:].unsqueeze(1).to_broadcast([P, NH, P]),
                                       wgt[t][:].unsqueeze(2).to_broadcast([P, NH, P]), ALU.mult).then_inc(dg_ready, 1)
                return step

            def mix(t):
                def step(it):
                    p = it.p
                    if t == 0:
                        pool.wait_ge(r_in[p], 16 * (it.h + 1))
                    pool.wait_ge(film_ready, 2 * it.i + t + 1)
                    pool.tensor_tensor(xr[p][:, t, :], xr[p][:, t, :], film[t][:, 0:D], ALU.mult).then_inc(mixed, 1)
                    pool.wait_ge(mixed, 2 * it.i + t + 1)
                    apart(pool, const)
                    pool.tensor_tensor(xin[:, it.i, t, :], xr[p][:, t, :], film[t][:, D:2 * D], ALU.add).then_inc(xin_ready, 1)
                return step

            pipeline(pool, B, DEPTH, [(3, roots_again), (7, diagonals(0)), (7, diagonals(1)), (9, mix(0)), (9, mix(1)), (3, affine), (4, key_mask),
                                      (4, spread_k), (6, negate_max(0)), (6, negate_max(1)), (1, roots_of)])

        @block.vector
        def _(dve):
            dve.wait_ge(weights, 128)
            dve.tensor_scalar(bf[:], bf[:], gate[:, 0:1], None, ALU.mult).then_inc(wready, 1)
            dve.wait_ge(wready, 1)
            dve.tensor_scalar(bf[:, 0:D], bf[:, 0:D], 1.0, None, ALU.add).then_inc(wready, 1)
            dve.wait_ge(wready, 2)

            def norm_stats(it):
                dve.wait_ge(x_in[it.p], 16 * (it.h + 1))
                layer_norm_stats(dve, Chain(dve, stats, it.i, 4), xb[it.p], stt[it.p], mv[it.p], const)

            def norm(it):
                dve.wait_ge(roots, 2 * it.i + 2)
                if it.reused():
                    dve.wait_ge(x_turned, it.i - 1)
                    dve.wait_ge(xl_part, 2 * it.i - 3)
                normalise(dve, xb[it.p], mv[it.p], rs[it.p], xn[it.p])[-1].then_inc(xn_ready, 1)
                dve.wait_ge(xn_ready, it.i + 1)
                apart(dve, const)
                layer_norm_stats(dve, Chain(dve, stats2, it.i, 4), xn[it.p], st2[it.p], mv2[it.p], const)

            def norm_again(it):
                dve.wait_ge(roots2, 2 * it.i + 2)
                if it.reused():
                    dve.wait_ge(xl_out[it.p], 16 * it.h)
                normalise(dve, xn[it.p], mv2[it.p], rs2[it.p], xl[it.p])[-1].then_inc(xl_part, 1)

            def pick_best(it):
                base = PICK * it.i
                dve.wait_ge(km_ready, it.i + 1)
                c = Chain(dve, pick, it.i, PICK)
                for t in range(TL):
                    dve.wait_ge(s_done, 2 * it.i + t + 1)
                    c.add(dve.scalar_tensor_tensor(sc[t][:], s_ps[t][:, 0:NH * SK].rearrange("p (h k) -> p h k", k=SK), (P // NH) ** -0.5,
                                                   kmf[it.p][:].unsqueeze(1).to_broadcast([P, NH, SK]), ALU.mult, ALU.add))
                for rnd in range(ROUNDS):
                    for t in range(TL):
                        dve.wait_ge(pick, base + TL + (2 * rnd - 1) * TL * NH + (t + 1) * NH if rnd else base + t + 1)
                        apart(dve, const)
                        rows = sc[t] if rnd == 0 else left[t]
                        for h in range(NH):
                            c.add(dve.max(best[t][:, rnd, h, :], rows[:, h, :]))
                    for t in range(TL):
                        dve.wait_ge(pick, base + TL + 2 * rnd * TL * NH + (t + 1) * NH)
                        apart(dve, const)
                        rows = sc[t] if rnd == 0 else left[t]
                        for h in range(NH):
                            c.add(dve.match_replace(left[t][:, h, :], best[t][:, rnd, h, :], rows[:, h, :], TAKEN))
                for t in range(TL):
                    dve.wait_ge(pick, base + PICK - 2 * TL - NH * (TL - 1) + t * NH + TL)
                    dve.wait_ge(exp_ready, 2 * it.i + t + 1)
                    if it.reused(1):
                        dve.wait_ge(a_done, 2 * it.i + t - 1)
                    c.add(dve.scalar_tensor_tensor(kept[t][:], left[t][:], TAKEN / 2, ex[t][:], ALU.is_lt, ALU.mult))

            def weigh_heads(t):
                def step(it):
                    dve.wait_ge(pick, PICK * (it.i + 1) - TL + t + 1)
                    if t == 0:
                        dve.wait_ge(t_in[it.p], 16 * (it.h + 1))
                    if it.reused(1):
                        dve.wait_ge(dg_ready, 2 * it.i + t - 1)
                    c = Chain(dve, weigh, 2 * it.i + t, WEIGH)
                    c.add(dve.tensor_reduce(wsum[t][:], kept[t][:], AX.X, ALU.add))
                    c.add(dve.tensor_scalar(tmf[t][:, 0:1], tm[it.p][:, t:t + 1], 1.0 / NH, None, ALU.mult))
                    c.wait()
                    dve.reciprocal(wsum[t][:], wsum[t][:]).then_inc(summed, 1)
                    dve.wait_ge(summed, 2 * it.i + t + 1)
                    c.add(dve.tensor_scalar(wgt[t][:], wsum[t][:], tmf[t][:, 0:1], None, ALU.mult))
                return step

            def film_out(t):
                def step(it):
                    dve.wait_ge(f_done, 2 * it.i + t + 1)
                    if it.reused(1):
                        dve.wait_ge(xin_ready, 2 * it.i + t - 1)
                    dve.scalar_tensor_tensor(film[t][:], f_ps[:], gate[:, 0:1], bf[:], ALU.mult, ALU.add).then_inc(film_ready, 1)
                return step

            pipeline(dve, B, DEPTH, [(9, film_out(0)), (7, weigh_heads(0)), (7, weigh_heads(1)), (9, film_out(1)), (2, norm), (3, norm_again),
                                     (1, norm_stats), (6, pick_best)])

        @block.scalar
        def _(act):
            def leave(out, bank, done, ready, used, per=1, extra=None):
                def step(it):
                    act.wait_ge(done, it.i + 1)
                    if it.reused():
                        act.wait_ge(used, per * (it.i - 1))
                        if extra is not None:
                            act.wait_ge(extra[it.p], 16 * it.h)
                    act.copy(out[it.p][:], bank).then_inc(ready, 1)
                return step

            def exps(t):
                def step(it):
                    act.wait_ge(nmax_ready, 2 * it.i + t + 1)
                    for h in range(NH):
                        last = act.activation(ex[t][:, h, :], sc[t][:, h, :], ACT.Exp, bias=nmax[t][:, h:h + 1])
                    last.then_inc(exp_ready, 1)
                return step

            def aT_out(it):
                act.wait_ge(a_done, 2 * it.i + 2)
                if it.reused():
                    act.wait_ge(c_done, it.i - 1)
                act.wait_ge(v_done, it.i + 1)
                act.copy(aT[it.p][:], a_ps[0:SK, 0:S]).then_inc(aT_ready, 1)
                act.copy(v[it.p][:], a_ps[0:SK, S:2 * S]).then_inc(v_ready, 1)

            chunks = lambda bank: bank[:].rearrange("p (k s) -> p k s", k=KD)
            pipeline(act, B, DEPTH, [
                (3, leave(xnT, chunks(t_ps), x_turned, xT_ready, q_done)),
                (4, leave(kT, k_ps[:, 0:SK], k_done, k_ready, kd_ready)),
                (4, leave(qT, q_ps[:, 0:S], q_done, q_ready, s_done, 2)),
                (8, leave(cT, chunks(c_ps), c_done, cT_ready, f_done, 2, cT_out)),
                (7, aT_out), (6, exps(0)), (6, exps(1))])

        @block.tensor
        def _(pe):
            pe.wait_ge(weights, 128)

            def turn_x(it):
                pe.wait_ge(xn_ready, it.i + 1)
                if it.reused(1):
                    pe.wait_ge(xT_ready, it.i)
                for t in range(TL):
                    for k in range(KD):
                        last = pe.transpose(t_ps[:, k * S + t * P:k * S + (t + 1) * P], xn[it.p][:, t, k * P:(k + 1) * P],
                                            const["ident"][:])
                last.then_inc(x_turned, 1)

            def project(it):
                pe.wait_ge(xT_ready, it.i + 1)
                pe.wait_ge(c_in[it.p], 16 * (it.h + 1))
                if it.reused(1):
                    pe.wait_ge(k_ready, it.i)
                    pe.wait_ge(q_ready, it.i)
                for k in range(2):
                    last = pe.matmul(k_ps[:, 0:SK], wk[:, k, :], cb[it.p][:, k, :], start=k == 0, stop=k == 1)
                last.then_inc(k_done, 1)
                for k in range(KD):
                    last = pe.matmul(q_ps[:, 0:S], wq[:, k, :], xnT[it.p][:, k, :], start=k == 0, stop=k == KD - 1)
                last.then_inc(q_done, 1)

            def scores(t):
                def step(it):
                    if t == 0:
                        pe.wait_ge(q_ready, it.i + 1)
                        pe.wait_ge(kd_ready, it.i + 1)
                    if it.reused(1):
                        pe.wait_ge(pick, PICK * (it.i - 1) + t + 1)
                    pe.matmul(s_ps[t][:, 0:NH * SK], qT[it.p][:, t * P:(t + 1) * P], kd[it.p][:].rearrange("p h k -> p (h k)"),
                              start=True, stop=True).then_inc(s_done, 1)
                return step

            def mean_heads(t):
                def step(it):
                    pe.wait_ge(pick, PICK * (it.i + 1) - TL + t + 1)
                    pe.wait_ge(dg_ready, 2 * it.i + t + 1)
                    if t == 0 and it.reused(1):
                        pe.wait_ge(v_ready, it.i)
                    for h in range(NH):
                        last = pe.matmul(a_ps[0:SK, t * P:(t + 1) * P], kept[t][:, h, :], dg[t][:, h, :], start=h == 0, stop=h == NH - 1)
                    last.then_inc(a_done, 1)
                    if t == 1:
                        pe.wait_ge(cv_in[it.p], 16 * (it.h + 1))
                        if it.reused(1):
                            pe.wait_ge(v_ready, it.i)
                        for k in range(2):
                            last = pe.matmul(a_ps[0:SK, S:2 * S], cv[it.p][:, k, :], wv[:, k, :], start=k == 0, stop=k == 1)
                        last.then_inc(v_done, 1)
                return step

            def attend(it):
                pe.wait_ge(aT_ready, it.i + 1)
                pe.wait_ge(v_ready, it.i + 1)
                if it.reused(1):
                    pe.wait_ge(cT_ready, it.i)
                for m in range(KD):
                    last = pe.matmul(c_ps[:, m * S:(m + 1) * S], v[it.p][:, m * P:(m + 1) * P], aT[it.p][:], start=True, stop=True)
                last.then_inc(c_done, 1)

            def film_in(t):
                def step(it):
                    if t == 0:
                        pe.wait_ge(cT_ready, it.i + 1)
                    if t == 1 or it.reused(1):
                        pe.wait_ge(film_ready, 2 * it.i + t)
                    for k in range(KD):
                        last = pe.matmul(f_ps[:], cT[it.p][:, k, t * P:(t + 1) * P], wf[:, k, :], start=k == 0, stop=k == KD - 1)
                    last.then_inc(f_done, 1)
                return step

            pipeline(pe, B, DEPTH, [
                (9, film_in(0)), (3, turn_x), (9, film_in(1)), (4, project), (8, attend), (7, mean_heads(0)), (7, mean_heads(1)), (5, scores(0)),
                (5, scores(1))])
    st.end()


def convolve_channels(nc, const, xin, kpad):
    st = Stage(nc, "cv", [const["apart"]])
    two = range(2)
    CG = 16
    HG = CG // 2
    toep = [st.sb(f"toep{p}", [P, CG, S]) for p in two]
    xg, xg_back = ([st.sb(f"{n}{p}", [P, CG, TL, B]) for p in two] for n in ("xg", "xg_back"))
    y_ps = [[st.ps(f"y{p}{half}", [P, HG, TL, B]) for half in two] for p in two]
    r_ps = [st.ps(f"r{half}", [P, HG, TL, B]) for half in two]
    t_in = [st.sem(f"t_in{p}") for p in two]
    gathered, r_done, reversed_, y_done, y_out = (st.sem(n) for n in ("gathered", "r_done", "reversed", "y_done", "y_out"))

    with nc.Block() as block:
        @block.sync
        def _(sp):
            def load(it):
                if it.reused():
                    sp.wait_ge(y_done, 2 * (it.i - 1))
                    apart(sp, const)
                rows = bass.AP(kpad.tensor, it.i * (CG * (LP + S)) + 1, [[1, P], [LP + S, CG], [1, S]])
                sp.dma_start(toep[it.p][:], rows).then_inc(t_in[it.p], 16)

            pipeline(sp, D // CG, 3, [(0, load)])

        @block.vector
        def _(dve):
            def gather(it):
                if it.reused():
                    dve.wait_ge(r_done, 2 * (it.i - 1))
                apart(dve, const)
                rows = xin[:, :, :, bass.ds(it.i * CG, CG)]
                dve.tensor_copy(xg[it.p][:], rows.rearrange("p b t c -> p c t b")).then_inc(gathered, 1)

            def reversed_out(half):
                def step(it):
                    dve.wait_ge(r_done, 2 * it.i + half + 1)
                    if it.reused():
                        dve.wait_ge(y_done, 2 * (it.i - 1))
                    dve.tensor_copy(xg_back[it.p][:, half * HG:(half + 1) * HG], r_ps[half][:]).then_inc(reversed_, 1)
                return step

            pipeline(dve, D // CG, 4, [(0, gather), (1, reversed_out(0)), (1, reversed_out(1))])

        @block.scalar
        def _(act):
            def scatter(half):
                def step(it):
                    act.wait_ge(y_done, 2 * it.i + half + 1)
                    apart(act, const)
                    act.copy(xin[:, :, :, bass.ds(it.i * CG + half * HG, HG)].rearrange("p b t c -> p c t b"), y_ps[it.p][half][:]).then_inc(y_out, 1)
                return step

            pipeline(act, D // CG, 4, [(3, scatter(0)), (3, scatter(1))])
            act.wait_ge(y_out, 2 * D // CG)

        @block.tensor
        def _(pe):
            def reverse(it):
                pe.wait_ge(gathered, it.i + 1)
                if it.reused(1):
                    pe.wait_ge(reversed_, 2 * it.i)
                for half in two:
                    pe.matmul(r_ps[half][:], const["back"][:], xg[it.p][:, half * HG:(half + 1) * HG], start=True, stop=True).then_inc(r_done, 1)

            def convolve(half):
                def step(it):
                    if half == 0:
                        pe.wait_ge(t_in[it.p], 16 * (it.h + 1))
                    pe.wait_ge(reversed_, 2 * it.i + half + 1)
                    if it.reused():
                        pe.wait_ge(y_out, 2 * (it.i - 2) + half + 1)
                    for c in range(HG):
                        d = half * HG + c
                        pe.matmul(y_ps[it.p][half][:, c], toep[it.p][:, d, 0:P], xg_back[it.p][:, d], start=True, stop=False)
                        last = pe.matmul(y_ps[it.p][half][:, c, 1], toep[it.p][:, d, P:2 * P], xg_back[it.p][:, d, 0], start=False, stop=True)
                    last.then_inc(y_done, 1)
                return step

            pipeline(pe, D // CG, 4, [(1, reverse), (2, convolve(0)), (2, convolve(1))])
    st.end()


def modulated_feed_forward(nc, const, src, dst, xin, rows_text, c_all, w):
    st = Stage(nc, "m3", [const["apart"]])
    two = range(2)
    wf, w1, w2, b1 = st.sb("wf", [P, KD, 2 * D]), st.sb("w1", [P, KD, H1]), st.sb("w2", [P, KH, D]), st.sb("b1", [P, KH])
    gf, bff = st.sb("gf", [P, KD]), st.sb("bff", [P, KD])
    bf, gate, gout, bout, b2 = st.sb("bf", [P, 2 * D]), st.sb("gate", [P, 1]), st.sb("gout", [P, D]), st.sb("bout", [P, D]), st.sb("b2", [P, D])
    xb, xn, xt, xn2, xs, xres, xo = ([st.sb(f"{n}{p}", [P, TL, D]) for p in two] for n in ("xb", "xn", "xt", "xn2", "xs", "xres", "xo"))
    stt, mv, st2, mv2, st3, mv3 = ([st.sb(f"{n}{p}", [P, TL, k]) for p in two] for n, k in (
        ("st", 6), ("mv", 2), ("st2", 6), ("mv2", 2), ("st3", 6), ("mv3", 2)))
    rs, rs2, rs3 = ([st.sb(f"{n}{p}", [P, TL]) for p in two] for n in ("rs", "rs2", "rs3"))
    cT, hnT = ([st.sb(f"{n}{p}", [P, KD, S]) for p in two] for n in ("cT", "hnT"))
    film = [st.sb(f"film{p}", [P, TL, 2 * D]) for p in two]
    hT = [st.sb(f"hT{p}", [P, KH, S]) for p in two]
    t_ps, y_ps = st.ps("t", [P, 512]), st.ps("y", [P, TL, D])
    f_ps = [st.ps(f"f{t}", [P, 512]) for t in range(TL)]
    h_ps = [st.ps(f"h{p}", [P, 2, S]) for p in two]
    weights, wready = st.sem("weights"), st.sem("wready")
    x_in, c_in, xt_out, xt_in, r_in, stored = ([st.sem(f"{n}{p}") for p in two] for n in ("x_in", "c_in", "xt_out", "xt_in", "r_in", "stored"))
    (stats, roots, stats2, roots2, stats3, roots3, xn_ready, xn2_ready, xn3_ready, f_done, film_ready, mixed, x_turned, hn_ready, h_done,
     h_ready, y_done, summed, ended) = (st.sem(n) for n in (
         "stats", "roots", "stats2", "roots2", "stats3", "roots3", "xn_ready", "xn2_ready", "xn3_ready", "f_done", "film_ready", "mixed",
         "x_turned", "hn_ready", "h_done", "h_ready", "y_done", "summed", "ended"))
    MIX, SUM, END = 3, 2, 3
    DEPTH = 9
    src_v = src.rearrange("b (t p) d -> b p t d", p=P)
    dst_v = dst.rearrange("b (t p) d -> b p t d", p=P)
    over = lambda a: a[:].unsqueeze(1).to_broadcast([P, TL, D])

    with nc.Block() as block:
        @block.sync
        def _(sp):
            for a, n in ((wf, "W_film_out"), (w1, "W1"), (w2, "W2"), (b1, "b1"), (gf, "g_ffn"), (bff, "b_ffn")):
                sp.dma_start(a[:], w[n]).then_inc(weights, 16)
            for a, n in ((bf, "b_film_out"), (gate, "mod_gate"), (gout, "g_norm_out"), (bout, "b_norm_out"), (b2, "b2")):
                sp.dma_start(a[:], w[n].partition_broadcast(P)).then_inc(weights, 16)

            def load(it):
                if it.reused():
                    sp.wait_ge(xn_ready, it.i - 1)
                apart(sp, const)
                sp.dma_start(xb[it.p][:], src_v[it.i]).then_inc(x_in[it.p], 16)

            def load_c(it):
                if it.reused():
                    sp.wait_ge(f_done, it.i - 1)
                apart(sp, const)
                sp.dma_start(cT[it.p][:], c_all[it.i]).then_inc(c_in[it.p], 16)

            def keep_xt(it):
                sp.wait_ge(mixed, MIX * (it.i + 1))
                apart(sp, const)
                sp.dma_start(rows_text[it.i], xt[it.p][:]).then_inc(xt_out[it.p], 16)

            def load_xt(it):
                if it.reused():
                    sp.wait_ge(ended, END * (it.i - 2) + 1)
                    apart(sp, const)
                sp.wait_ge(xt_out[it.p], 16 * (it.h + 1))
                apart(sp, const)
                sp.dma_start(xs[it.p][:], rows_text[it.i]).then_inc(xt_in[it.p], 16)

            def load_residual(it):
                if it.reused():
                    sp.wait_ge(ended, END * (it.i - 1))
                apart(sp, const)
                sp.dma_start(xres[it.p][:], src_v[it.i]).then_inc(r_in[it.p], 16)

            def store(it):
                sp.wait_ge(ended, END * (it.i + 1))
                apart(sp, const)
                sp.dma_start(dst_v[it.i], xo[it.p][:]).then_inc(stored[it.p], 16)

            pipeline(sp, B, DEPTH, [(0, load), (1, load_c), (4, keep_xt), (6, load_xt), (7, load_residual), (9, store)])
            for p in two:
                sp.wait_ge(stored[p], 16 * (B // 2))
                sp.wait_ge(xt_out[p], 16 * (B // 2))

        @block.gpsimd
        def _(pool):
            pool.wait_ge(weights, 176)

            def roots_of(ready, mvs, out, done):
                def step(it):
                    pool.wait_ge(ready, 4 * it.i + 4)
                    inverse_root(pool, Chain(pool, done, it.i, 2), mvs[it.p][:, :, 1], out[it.p][:], const)
                return step

            def mix(it):
                p = it.p
                c = Chain(pool, mixed, it.i, MIX)
                pool.wait_ge(film_ready, 2 * it.i + 2)
                if it.reused():
                    pool.wait_ge(xn2_ready, it.i - 1)
                    pool.wait_ge(xt_out[p], 16 * it.h)
                apart(pool, const)
                c.add(pool.tensor_tensor(xt[p][:], xin[:, it.i], film[p][:, :, 0:D], ALU.mult))
                c.wait()
                c.add(pool.tensor_tensor(xt[p][:], xt[p][:], film[p][:, :, D:2 * D], ALU.add))
                c.wait()
                pool.wait_ge(xn_ready, it.i + 1)
                c.add(pool.tensor_tensor(xt[p][:], xt[p][:], xn[p][:], ALU.add))

            def end(it):
                p = it.p
                c = Chain(pool, ended, it.i, END)
                pool.wait_ge(xn3_ready, it.i + 1)
                if it.reused():
                    pool.wait_ge(stored[p], 16 * it.h)
                c.add(pool.tensor_tensor(xo[p][:], xs[p][:], over(gout), ALU.mult))
                c.wait()
                c.add(pool.tensor_tensor(xo[p][:], xo[p][:], over(bout), ALU.add))
                c.wait()
                pool.wait_ge(r_in[p], 16 * (it.h + 1))
                c.add(pool.tensor_tensor(xo[p][:], xo[p][:], xres[p][:], ALU.add))

            pipeline(pool, B, DEPTH, [(1, roots_of(stats, mv, rs, roots)), (8, roots_of(stats3, mv3, rs3, roots3)),
                                      (3, mix), (4, roots_of(stats2, mv2, rs2, roots2)), (8, end)])

        @block.vector
        def _(dve):
            dve.wait_ge(weights, 176)
            dve.tensor_scalar(bf[:], bf[:], gate[:, 0:1], None, ALU.mult).then_inc(wready, 1)
            dve.wait_ge(wready, 1)
            dve.tensor_scalar(bf[:, 0:D], bf[:, 0:D], 1.0, None, ALU.add).then_inc(wready, 1)
            dve.wait_ge(wready, 2)

            def norm_stats(it):
                dve.wait_ge(x_in[it.p], 16 * (it.h + 1))
                layer_norm_stats(dve, Chain(dve, stats, it.i, 4), xb[it.p], stt[it.p], mv[it.p], const)

            def norm(it):
                dve.wait_ge(roots, 2 * it.i + 2)
                if it.reused():
                    dve.wait_ge(mixed, MIX * (it.i - 1))
                normalise(dve, xb[it.p], mv[it.p], rs[it.p], xn[it.p])[-1].then_inc(xn_ready, 1)

            def film_out(it):
                dve.wait_ge(f_done, it.i + 1)
                if it.reused():
                    dve.wait_ge(mixed, MIX * (it.i - 1))
                for t in range(TL):
                    dve.scalar_tensor_tensor(film[it.p][:, t, :], f_ps[t][:], gate[:, 0:1], bf[:], ALU.mult, ALU.add).then_inc(film_ready, 1)

            def xt_stats(it):
                dve.wait_ge(mixed, MIX * (it.i + 1))
                layer_norm_stats(dve, Chain(dve, stats2, it.i, 4), xt[it.p], st2[it.p], mv2[it.p], const)

            def xt_norm(it):
                dve.wait_ge(roots2, 2 * it.i + 2)
                if it.reused():
                    dve.wait_ge(x_turned, it.i - 1)
                normalise(dve, xt[it.p], mv2[it.p], rs2[it.p], xn2[it.p])[-1].then_inc(xn2_ready, 1)

            def add_all(it):
                p = it.p
                c = Chain(dve, summed, it.i, SUM)
                dve.wait_ge(xt_in[p], 16 * (it.h + 1))
                c.add(dve.tensor_tensor(xs[p][:], xs[p][:], over(b2), ALU.add))
                dve.wait_ge(y_done, it.i + 1)
                c.wait()
                c.add(dve.tensor_tensor(xs[p][:], xs[p][:], y_ps[:], ALU.add))
                c.wait()
                apart(dve, const)
                layer_norm_stats(dve, Chain(dve, stats3, it.i, 4), xs[p], st3[p], mv3[p], const)

            def last_norm(it):
                dve.wait_ge(roots3, 2 * it.i + 2)
                normalise(dve, xs[it.p], mv3[it.p], rs3[it.p], xs[it.p])[-1].then_inc(xn3_ready, 1)

            pipeline(dve, B, DEPTH, [(1, norm_stats), (5, xt_norm), (4, xt_stats), (2, norm), (2, film_out), (8, last_norm), (7, add_all)])

        @block.scalar
        def _(act):
            act.wait_ge(weights, 176)

            def hn_out(it):
                act.wait_ge(x_turned, it.i + 1)
                if it.reused():
                    act.wait_ge(h_done, KH // 2 * (it.i - 1))
                for k in range(KD):
                    last = act.activation(hnT[it.p][:, k, :], t_ps[:, k * S:(k + 1) * S], ACT.Identity, bias=bff[:, k:k + 1], scale=gf[:, k:k + 1])
                last.then_inc(hn_ready, 1)

            def gelu(m):
                def step(it):
                    act.wait_ge(h_done, KH // 2 * it.i + m + 1)
                    if m == 0 and it.reused():
                        act.wait_ge(y_done, it.i - 1)
                    for c in range(2):
                        f = 2 * m + c
                        act.activation(hT[it.p][:, f, :], h_ps[m % 2][:, c, :], ACT.Gelu, bias=b1[:, f:f + 1]).then_inc(h_ready, 1)
                return step

            pipeline(act, B, DEPTH, [(6, gelu(m)) for m in range(KH // 2)] + [(5, hn_out)])

        @block.tensor
        def _(pe):
            pe.wait_ge(weights, 176)

            def film_product(it):
                pe.wait_ge(c_in[it.p], 16 * (it.h + 1))
                if it.reused(1):
                    pe.wait_ge(film_ready, 2 * it.i)
                for t in range(TL):
                    for k in range(KD):
                        last = pe.matmul(f_ps[t][:], cT[it.p][:, k, t * P:(t + 1) * P], wf[:, k, :], start=k == 0, stop=k == KD - 1)
                last.then_inc(f_done, 1)

            def turn_x(it):
                pe.wait_ge(xn2_ready, it.i + 1)
                if it.reused(1):
                    pe.wait_ge(hn_ready, it.i)
                for t in range(TL):
                    for k in range(KD):
                        last = pe.transpose(t_ps[:, k * S + t * P:k * S + (t + 1) * P], xn2[it.p][:, t, k * P:(k + 1) * P],
                                            const["ident"][:])
                last.then_inc(x_turned, 1)

            def up(m):
                def step(it):
                    if m == 0:
                        pe.wait_ge(hn_ready, it.i + 1)
                    if it.reused(1) or m >= 2:
                        pe.wait_ge(h_ready, KH * it.i + 2 * m - 2)
                    for c in range(2):
                        f = (2 * m + c) * P
                        for k in range(KD):
                            last = pe.matmul(h_ps[m % 2][:, c, :], w1[:, k, f:f + P], hnT[it.p][:, k, :], start=k == 0, stop=k == KD - 1)
                    last.then_inc(h_done, 1)
                return step

            def down(it):
                pe.wait_ge(h_ready, KH * (it.i + 1))
                if it.reused(1):
                    pe.wait_ge(summed, SUM * it.i)
                for t in range(TL):
                    for k in range(KH):
                        last = pe.matmul(y_ps[:, t, :], hT[it.p][:, k, t * P:(t + 1) * P], w2[:, k, :], start=k == 0, stop=k == KH - 1)
                last.then_inc(y_done, 1)

            pipeline(pe, B, DEPTH, [(6, up(0)), (6, up(1)), (2, film_product), (6, up(2)), (6, up(3)), (5, turn_x), (7, down)])
    st.end()


def low_rank_feed_forward(nc, const, src, dst, w):
    st = Stage(nc, "f3", [const["apart"]])
    two = range(2)
    RK = 64
    u1, v1, u2, v2 = st.sb("u1", [P, KD, RK]), st.sb("v1", [RK, H1]), st.sb("u2", [P, KH, RK]), st.sb("v2", [RK, D])
    b1, b2 = st.sb("b1", [P, KH]), st.sb("b2", [P, D])
    xb, xn, xo, xres = ([st.sb(f"{n}{p}", [P, TL, D]) for p in two] for n in ("xb", "xn", "xo", "xres"))
    stt, mv = ([st.sb(f"{n}{p}", [P, TL, k]) for p in two] for n, k in (("st", 6), ("mv", 2)))
    rs = [st.sb(f"rs{p}", [P, TL]) for p in two]
    xnT = [st.sb(f"xnT{p}", [P, KD, S]) for p in two]
    pT, qT = ([st.sb(f"{n}{p}", [RK, S]) for p in two] for n in ("pT", "qT"))
    hT = [st.sb(f"hT{p}", [P, KH, S]) for p in two]
    t_ps, p_ps, q_ps, y_ps = st.ps("t", [P, 512]), st.ps("p", [RK, S]), st.ps("q", [RK, S]), st.ps("y", [P, TL, D])
    h_ps = [st.ps(f"h{p}", [P, 2, S]) for p in two]
    weights = st.sem("weights")
    x_in, r_in, stored = ([st.sem(f"{n}{p}") for p in two] for n in ("x_in", "r_in", "stored"))
    (stats, roots, xn_ready, x_turned, xT_ready, p_done, p_ready, h_done, h_ready, q_done, q_ready, y_done, begun, summed) = (st.sem(n) for n in (
        "stats", "roots", "xn_ready", "x_turned", "xT_ready", "p_done", "p_ready", "h_done", "h_ready", "q_done", "q_ready", "y_done", "begun", "summed"))
    DEPTH = 8
    src_v = src.rearrange("b (t p) d -> b p t d", p=P)
    dst_v = dst.rearrange("b (t p) d -> b p t d", p=P)

    with nc.Block() as block:
        @block.sync
        def _(sp):
            for a, n in ((u1, "U1"), (v1, "V1"), (u2, "U2"), (v2, "V2"), (b1, "b1")):
                sp.dma_start(a[:], w[n]).then_inc(weights, 16)
            sp.dma_start(b2[:], w["b2"].partition_broadcast(P)).then_inc(weights, 16)

            def load(it):
                if it.reused():
                    sp.wait_ge(xn_ready, it.i - 1)
                apart(sp, const)
                sp.dma_start(xb[it.p][:], src_v[it.i]).then_inc(x_in[it.p], 16)

            def load_residual(it):
                if it.reused():
                    sp.wait_ge(begun, it.i - 1)
                apart(sp, const)
                sp.dma_start(xres[it.p][:], src_v[it.i]).then_inc(r_in[it.p], 16)

            def store(it):
                sp.wait_ge(summed, it.i + 1)
                apart(sp, const)
                sp.dma_start(dst_v[it.i], xo[it.p][:]).then_inc(stored[it.p], 16)

            pipeline(sp, B, DEPTH, [(0, load), (5, load_residual), (7, store)])
            for p in two:
                sp.wait_ge(stored[p], 16 * (B // 2))

        @block.gpsimd
        def _(pool):
            pool.wait_ge(weights, 96)

            def roots_of(it):
                pool.wait_ge(stats, 4 * it.i + 4)
                inverse_root(pool, Chain(pool, roots, it.i, 2), mv[it.p][:, :, 1], rs[it.p][:], const)

            def residual(it):
                pool.wait_ge(r_in[it.p], 16 * (it.h + 1))
                if it.reused():
                    pool.wait_ge(stored[it.p], 16 * it.h)
                pool.tensor_tensor(xo[it.p][:], xres[it.p][:], b2[:].unsqueeze(1).to_broadcast([P, TL, D]), ALU.add).then_inc(begun, 1)

            pipeline(pool, B, DEPTH, [(1, roots_of), (6, residual)])

        @block.vector
        def _(dve):
            def norm_stats(it):
                dve.wait_ge(x_in[it.p], 16 * (it.h + 1))
                layer_norm_stats(dve, Chain(dve, stats, it.i, 4), xb[it.p], stt[it.p], mv[it.p], const)

            def norm(it):
                dve.wait_ge(roots, 2 * it.i + 2)
                if it.reused():
                    dve.wait_ge(x_turned, it.i - 1)
                normalise(dve, xb[it.p], mv[it.p], rs[it.p], xn[it.p])[-1].then_inc(xn_ready, 1)

            def leave(bank, outs, done, ready, used):
                def step(it):
                    dve.wait_ge(done, it.i + 1)
                    if it.reused():
                        dve.wait_ge(used[0], used[1] * (it.i - 1))
                    dve.tensor_copy(outs[it.p][:], bank).then_inc(ready, 1)
                return step

            def add_all(it):
                dve.wait_ge(begun, it.i + 1)
                dve.wait_ge(y_done, it.i + 1)
                dve.tensor_tensor(xo[it.p][:], xo[it.p][:], y_ps[:], ALU.add).then_inc(summed, 1)

            pipeline(dve, B, DEPTH, [
                (6, leave(q_ps[:], qT, q_done, q_ready, (y_done, 1))), (4, leave(p_ps[:], pT, p_done, p_ready, (h_done, KH // 2))),
                (1, norm_stats), (2, norm),
                (3, leave(t_ps[:].rearrange("p (k s) -> p k s", k=KD), xnT, x_turned, xT_ready, (p_done, 1))), (6, add_all)])

        @block.scalar
        def _(act):
            act.wait_ge(weights, 96)

            def gelu(m):
                def step(it):
                    act.wait_ge(h_done, KH // 2 * it.i + m + 1)
                    if m == 0 and it.reused():
                        act.wait_ge(q_done, it.i - 1)
                    for c in range(2):
                        f = 2 * m + c
                        act.activation(hT[it.p][:, f, :], h_ps[m % 2][:, c, :], ACT.Gelu_apprx_tanh, bias=b1[:, f:f + 1]).then_inc(h_ready, 1)
                return step

            pipeline(act, B, DEPTH, [(5, gelu(m)) for m in range(KH // 2)])

        @block.tensor
        def _(pe):
            pe.wait_ge(weights, 96)

            def turn_x(it):
                pe.wait_ge(xn_ready, it.i + 1)
                if it.reused(1):
                    pe.wait_ge(xT_ready, it.i)
                for t in range(TL):
                    for k in range(KD):
                        last = pe.transpose(t_ps[:, k * S + t * P:k * S + (t + 1) * P], xn[it.p][:, t, k * P:(k + 1) * P],
                                            const["ident"][:])
                last.then_inc(x_turned, 1)

            def narrow(it):
                pe.wait_ge(xT_ready, it.i + 1)
                if it.reused(1):
                    pe.wait_ge(p_ready, it.i)
                for k in range(KD):
                    last = pe.matmul(p_ps[:], u1[:, k, :], xnT[it.p][:, k, :], start=k == 0, stop=k == KD - 1)
                last.then_inc(p_done, 1)

            def up(m):
                def step(it):
                    if m == 0:
                        pe.wait_ge(p_ready, it.i + 1)
                    if it.reused(1) or m >= 2:
                        pe.wait_ge(h_ready, KH * it.i + 2 * m - 2)
                    for c in range(2):
                        f = (2 * m + c) * P
                        last = pe.matmul(h_ps[m % 2][:, c, :], v1[:, f:f + P], pT[it.p][:], start=True, stop=True)
                    last.then_inc(h_done, 1)
                return step

            def down(half):
                def step(it):
                    pe.wait_ge(h_ready, KH * it.i + KH // 2 * (half + 1))
                    if half == 0 and it.reused(1):
                        pe.wait_ge(q_ready, it.i)
                    for k in range(half * KH // 2, (half + 1) * KH // 2):
                        last = pe.matmul(q_ps[:], u2[:, k, :], hT[it.p][:, k, :], start=k == 0, stop=k == KH - 1)
                    if half == 1:
                        last.then_inc(q_done, 1)
                return step

            def widen(it):
                pe.wait_ge(q_ready, it.i + 1)
                if it.reused(1):
                    pe.wait_ge(summed, it.i)
                for t in range(TL):
                    last = pe.matmul(y_ps[:, t, :], qT[it.p][:, t * P:(t + 1) * P], v2[:], start=True, stop=True)
                last.then_inc(y_done, 1)

            pipeline(pe, B, DEPTH, [(5, up(0)), (5, up(1)), (6, widen), (4, narrow), (5, up(2)), (5, down(0)), (5, up(3)), (3, turn_x), (5, down(1))])
    st.end()


def state_space_attention(nc, const, src, dst, i):
    w = {n[len("L3_xattn_"):]: a for n, a in i.items() if n.startswith("L3_xattn_")}
    kpad = nc.dram_tensor("kernels", (D, LP + S), F32, kind="Internal").ap()
    rows_text = nc.dram_tensor("rows_text", (B, P, TL, D), F32, kind="Internal").ap()
    c_all = nc.dram_tensor("c_all", (B, P, KD, S), F32, kind="Internal").ap()
    convolution_kernel(nc, const, kpad, w)
    with nc.sbuf_tensor("xin", [P, B, TL, D], F32) as xin:
        sparse_attention(nc, const, src, xin, rows_text, c_all, i["ctx"], w, (i["text_mask"], i["vision_mask"]))
        convolve_channels(nc, const, xin, kpad)
        modulated_feed_forward(nc, const, src, dst, xin, rows_text, c_all, w)


def cross_attention_stack(nc, i, out):
    keep = ExitStack()
    with keep:
        const = setup(nc, keep)
        scratch = [nc.dram_tensor(f"x_{n}", (B, S, D), F32, kind="Internal").ap() for n in range(2)]
        stages = [
            lambda s, d: heads_attention(nc, const, "a0", s, d, i["ctx"], {n: i["L0_xattn_" + n] for n in
                                         ("Wq", "bq", "Wk", "bk", "Wv", "bv", "Wo", "bo")}, 10000.0),
            lambda s, d: ternary_feed_forward(nc, const, s, d, {n: i["L0_ffn_" + n] for n in ("w1", "conv_w", "conv_b", "w2")}),
            lambda s, d: normed_attention(nc, const, s, d, i["ctx"], {n: i["L1_xattn_" + n] for n in ("Wq", "Wk", "Wv", "Wo")}),
            lambda s, d: routed_feed_forward(nc, const, s, d, {n: i["L1_ffn_" + n] for n in
                                             ("rw1", "rb1", "rw2", "rb2", "ew1", "eb1", "ew2", "eb2")}),
            lambda s, d: heads_attention(nc, const, "a2", s, d, i["ctx"], {n: i["L2_xattn_" + n] for n in
                                         ("Wq", "Wk", "Wv", "Wo", "bq", "bk", "bv", "bo")}, None),
            lambda s, d: adaptive_feed_forward(nc, const, s, d, {n: i["L2_ffn_" + n] for n in
                                               ("gate_w", "gate_b", "dp_w1", "dp_b1", "dp_w2", "dp_b2", "ew1", "eb1", "ew2", "eb2")}),
            lambda s, d: state_space_attention(nc, const, s, d, i),
            lambda s, d: low_rank_feed_forward(nc, const, s, d, {n: i["L3_ffn_" + n] for n in ("U1", "V1", "b1", "U2", "V2", "b2")}),
        ]
        src = i["x"]
        for n, stage in enumerate(stages):
            dst = out if n == len(stages) - 1 else scratch[n % 2]
            stage(src, dst)
            src = dst


def _rows(a, p=P):
    return a.reshape(a.shape[0] // p, p, -1).transpose(1, 0, 2)


def _cols(a):
    return a.reshape(-1, P).T


def _layout(x):
    a = {"x": x["x"]}
    ctx = x["ctx_768"].transpose(0, 2, 1).reshape(B, 2, CP, SK)
    a["ctx"] = ctx.transpose(0, 2, 1, 3)
    row = lambda v: v.reshape(-1)
    for n in ("Wq", "Wo"):
        a["L0_xattn_" + n] = _rows(x["L0_xattn_" + n])
        a["L2_xattn_" + n] = _rows(x["L2_xattn_" + n.lower()])
        a["L1_xattn_" + n] = _rows(x["L1_xattn_" + n].T)
    for n in ("Wk", "Wv"):
        a["L0_xattn_" + n] = _rows(x["L0_xattn_" + n], CP)
        a["L2_xattn_" + n] = _rows(x["L2_xattn_" + n.lower()], CP)
        a["L1_xattn_" + n] = _rows(x["L1_xattn_" + n].T, CP)
        a["L3_xattn_" + n] = _rows(x["L3_xattn_" + n], CP)
    for layer in ("L0", "L2"):
        for n in ("bq", "bk", "bv"):
            a[f"{layer}_xattn_{n}"] = _cols(x[f"{layer}_xattn_{n}"])
        a[f"{layer}_xattn_bo"] = x[f"{layer}_xattn_bo"]
    a["L0_ffn_w1"], a["L0_ffn_w2"] = _rows(x["L0_ffn_w1"].T), _rows(x["L0_ffn_w2"].T)
    a["L0_ffn_conv_w"] = _rows(x["L0_ffn_conv_w"].reshape(H1, 3))
    a["L0_ffn_conv_b"] = _cols(x["L0_ffn_conv_b"])
    a["L1_ffn_rw1"], a["L1_ffn_rb1"] = _rows(x["L1_ffn_rw1"]), _cols(x["L1_ffn_rb1"])
    a["L1_ffn_rw2"], a["L1_ffn_rb2"] = _rows(x["L1_ffn_rw2"]), x["L1_ffn_rb2"]
    a["L1_ffn_ew1"] = np.stack([_rows(e) for e in x["L1_ffn_ew1"]])
    a["L1_ffn_ew2"] = np.stack([_rows(e) for e in x["L1_ffn_ew2"]])
    a["L1_ffn_eb1"] = x["L1_ffn_eb1"].reshape(NE, KH, P).transpose(2, 0, 1)
    a["L1_ffn_eb2"] = row(x["L1_ffn_eb2"])
    a["L2_ffn_gate_w"], a["L2_ffn_gate_b"] = _rows(x["L2_ffn_gate_w"]), x["L2_ffn_gate_b"]
    a["L2_ffn_dp_w1"], a["L2_ffn_dp_b1"] = _rows(x["L2_ffn_dp_w1"]), _cols(x["L2_ffn_dp_b1"])
    a["L2_ffn_dp_w2"], a["L2_ffn_dp_b2"] = x["L2_ffn_dp_w2"], x["L2_ffn_dp_b2"]
    a["L2_ffn_ew1"] = np.stack([_rows(e) for e in x["L2_ffn_ew1"]], 1)
    a["L2_ffn_ew2"] = np.stack([_rows(e) for e in x["L2_ffn_ew2"]], 1)
    a["L2_ffn_eb1"] = x["L2_ffn_eb1"].reshape(-1, P).T
    a["L2_ffn_eb2"] = x["L2_ffn_eb2"]
    l3 = "L3_xattn_"
    for n in ("Wq", "W_film_in", "W_film_out", "W1", "W2"):
        a[l3 + n] = _rows(x[l3 + n])
    for n in ("b1", "g_ffn", "b_ffn"):
        a[l3 + n] = _cols(x[l3 + n])
    for n in ("b_film_in", "b_film_out", "g_norm_in", "b_norm_in", "g_norm_out", "b_norm_out", "b2", "log_dt"):
        a[l3 + n] = x[l3 + n]
    a[l3 + "mod_gate"], a[l3 + "D_skip"] = row(x[l3 + "mod_gate"]), x[l3 + "D_skip"].reshape(1, D)
    for n in ("A_re", "A_im", "C_re", "C_im"):
        a[l3 + n] = x[l3 + n].T
    a["text_mask"] = x["mask_BxS_bf1"].view(np.uint8).reshape(B, TL, P).transpose(0, 2, 1)
    a["vision_mask"] = x["mask_BxS2_bf1"].view(np.uint8)
    for n in ("U1", "U2"):
        a["L3_ffn_" + n] = _rows(x["L3_ffn_" + n])
    a["L3_ffn_V1"], a["L3_ffn_V2"] = x["L3_ffn_V1"], x["L3_ffn_V2"]
    a["L3_ffn_b1"], a["L3_ffn_b2"] = _cols(x["L3_ffn_b1"]), x["L3_ffn_b2"]
    return a


def kernel(**inputs):
    import concourse.bacc as bacc
    from concourse.bass_utils import run_bass_kernel_spmd

    arrays = {n: np.ascontiguousarray(a) for n, a in _layout({n: np.asarray(a) for n, a in inputs.items()}).items()}
    nc = bacc.Bacc("TRN2", target_bir_lowering=False, num_devices=1)
    aps = {n: nc.dram_tensor(f"in_{n}", a.shape, mybir.dt.from_np(a.dtype), kind="ExternalInput").ap() for n, a in arrays.items()}
    out = nc.dram_tensor("out", (B, S, D), F32, kind="ExternalOutput").ap()
    cross_attention_stack(nc, aps, out)
    r = run_bass_kernel_spmd(nc, [{f"in_{n}": a for n, a in arrays.items()}], core_ids=[0])
    return r.results[0]["out"]
```
